# Optimizing a Trainium2 kernel written in Bass

```python
import numpy as np
import jax
import jax.numpy as jnp

def _softmax(x, axis=-1):
    return jax.nn.softmax(x, axis=axis)

def _gelu(x):
    return jax.nn.gelu(x, approximate=True)

def _silu(x):
    return jax.nn.silu(x)

def _sigmoid(x):
    return jax.nn.sigmoid(x)

def _layernorm(x, axis=-1, eps=1e-05):
    m = jnp.mean(x, axis=axis, keepdims=True)
    v = jnp.var(x, axis=axis, keepdims=True)
    return (x - m) / jnp.sqrt(v + eps)

def _scatter_add(tgt, idx, src, axis=0):
    return tgt.at[idx].add(src)

def _segment_sum(src, seg, n):
    return jax.ops.segment_sum(src, seg, n)
kernel_name = 'mk_cond_resid_d4_seqx_r8_055f47'

def setup_inputs(seed: int=0):
    np.random.seed(seed)
    _w = jnp.asarray

    def _rec_inputs():
        import jax
        import jax.numpy as jnp
        _rk = jax.random.key(seed)
        x = 7.22e-05 + 1 * jax.random.normal(jax.random.fold_in(_rk, 1), (8, 128, 512), jnp.float32)
        _lenS = 128 - jax.random.randint(jax.random.fold_in(_rk, 7), (8,), 0, max(1, 128 // 4) + 1, jnp.int32)
        _lenS2 = 128 - jax.random.randint(jax.random.fold_in(_rk, 8), (8,), 0, max(1, 128 // 4) + 1, jnp.int32)
        itok_B_2_6 = jax.random.randint(jax.random.fold_in(_rk, 11), (8,), 2, 7, jnp.int32)
        itok_B_1_7 = jax.random.randint(jax.random.fold_in(_rk, 12), (8,), 1, 8, jnp.int32)
        itok_B_0_23 = jax.random.randint(jax.random.fold_in(_rk, 13), (8,), 0, 24, jnp.int32)
        itok_Bx16_0_63 = jax.random.randint(jax.random.fold_in(_rk, 14), (8, 16), 0, 64, jnp.int32)
        itok_B_207_1644 = jax.random.randint(jax.random.fold_in(_rk, 15), (8,), 207, 1645, jnp.int32)
        return (x, itok_B_2_6, itok_B_1_7, itok_B_0_23, itok_Bx16_0_63, itok_B_207_1644)
    x, itok_B_2_6, itok_B_1_7, itok_B_0_23, itok_Bx16_0_63, itok_B_207_1644 = _rec_inputs()

    def _L0_cond_setup():
        import jax, jax.numpy as jnp
        import numpy as np
        B, N, H, F = (4, 64, 512, 1376)
        L, R, RANK = (1, 16, 16)
        SCALE = 0.5
        key = jax.random.key(seed)
        ks = jax.random.split(key, 12)
        nrm = lambda k, shape, fan: jax.random.normal(k, shape, jnp.float32) * fan ** (-0.5)
        inp = {'x': jax.random.normal(ks[0], (B, N, H), jnp.float32), 'W_gate': nrm(ks[1], (F, H), H), 'W_up': nrm(ks[2], (F, H), H), 'W_down': nrm(ks[3], (H, F), F), 'A_gate': nrm(ks[4], (L, R, RANK, H), H), 'B_gate': nrm(ks[5], (L, R, F, RANK), RANK), 'A_up': nrm(ks[6], (L, R, RANK, H), H), 'B_up': nrm(ks[7], (L, R, F, RANK), RANK), 'A_down': nrm(ks[8], (L, R, RANK, F), F), 'B_down': nrm(ks[9], (L, R, H, RANK), RANK), 'lora_indices': jax.random.randint(ks[10], (B,), 0, R), 'layer_idx': 0}
        return inp
    _L0_cond_all = _L0_cond_setup()
    _L0_cond_in = {k: v for k, v in _L0_cond_all.items() if k in ('W_gate', 'W_up', 'W_down', 'A_gate', 'B_gate', 'A_up', 'B_up', 'A_down', 'B_down')}
    del _L0_cond_all

    def _L1_cond_setup():
        import jax, jax.numpy as jnp
        import numpy as np
        B, S, D_IN, D_OUT = (4, 256, 512, 512)
        N_ADAPTERS, MAX_RANK = (8, 16)
        key = jax.random.key(seed)
        ks = jax.random.split(key, 7)
        x = jax.random.normal(ks[0], (B, S, D_IN), dtype=jnp.float32)
        weight = jax.random.normal(ks[1], (D_OUT, D_IN), dtype=jnp.float32) * (1.0 / np.sqrt(D_IN))
        bias = jax.random.normal(ks[2], (D_OUT,), dtype=jnp.float32) * 0.01
        lora_a_weights = jax.random.normal(ks[3], (N_ADAPTERS, MAX_RANK, D_IN), dtype=jnp.float32) * (1.0 / np.sqrt(D_IN))
        lora_b_weights = jax.random.normal(ks[4], (N_ADAPTERS, D_OUT, MAX_RANK), dtype=jnp.float32) * 0.02
        scaling_factors = jax.random.uniform(ks[5], (N_ADAPTERS,), dtype=jnp.float32, minval=0.5, maxval=2.0)
        adapter_id = jax.random.randint(ks[6], (B,), 0, N_ADAPTERS, dtype=jnp.int64)
        return {'x': x, 'weight': weight, 'bias': bias, 'lora_a_weights': lora_a_weights, 'lora_b_weights': lora_b_weights, 'scaling_factors': scaling_factors, 'adapter_id': adapter_id}
    _L1_cond_all = _L1_cond_setup()
    _L1_cond_in = {k: v for k, v in _L1_cond_all.items() if k in ('weight', 'bias', 'lora_a_weights', 'lora_b_weights', 'scaling_factors')}
    del _L1_cond_all

    def _L2_cond_setup():
        import jax, jax.numpy as jnp
        import numpy as np
        R = 16
        ALPHA = 32
        SCALING = ALPHA / R
        SLOTS = 32
        IN_F = 512
        OUT_F = 512
        B, T = (8, 128)
        key = jax.random.key(seed)
        k1, k2, k3, k4, k5, k6 = jax.random.split(key, 6)
        x = jax.random.normal(k1, (B, T, IN_F), dtype=jnp.float32)
        adapter_mapping = jax.random.randint(k2, (B,), 0, SLOTS, dtype=jnp.int32)
        W = jax.random.normal(k3, (OUT_F, IN_F), dtype=jnp.float32) * 0.02
        b = jax.random.normal(k4, (OUT_F,), dtype=jnp.float32) * 0.02
        lora_As = jax.random.normal(k5, (SLOTS, IN_F, R), dtype=jnp.float32) * 0.02
        lora_Bs = jax.random.normal(k6, (SLOTS, R, OUT_F), dtype=jnp.float32) * 0.02
        return {'x': x, 'adapter_mapping': adapter_mapping, 'W': W, 'b': b, 'lora_As': lora_As, 'lora_Bs': lora_Bs}
    _L2_cond_all = _L2_cond_setup()
    _L2_cond_in = {k: v for k, v in _L2_cond_all.items() if k in ('W', 'b', 'lora_As', 'lora_Bs')}
    del _L2_cond_all

    def _L3_cond_setup():
        import jax, jax.numpy as jnp
        import numpy as np
        B, S, HID = (4, 128, 512)
        D, HQ, HK = (128, 32, 8)
        PAGES, PSIZE, NPP = (64, 32, 16)
        THETA = 10000.0
        EPS = 1e-06
        SCALE = 1.0 / float(np.sqrt(D))

        def _rmsnorm(t, w):
            var = jnp.mean(t * t, axis=-1, keepdims=True)
            return t * jax.lax.rsqrt(var + EPS) * w

        def _rope(t, pos):
            inv_freq = 1.0 / THETA ** (jnp.arange(0, D, 2, dtype=jnp.float32) / D)
            freqs = pos[..., None].astype(jnp.float32) * inv_freq
            cos = jnp.cos(freqs)[:, :, None, :]
            sin = jnp.sin(freqs)[:, :, None, :]
            t1, t2 = (t[..., :D // 2], t[..., D // 2:])
            return jnp.concatenate([t1 * cos - t2 * sin, t2 * cos + t1 * sin], axis=-1)
        key = jax.random.key(seed)
        ks = jax.random.split(key, 10)
        x = jax.random.normal(ks[0], (B, S, HID), jnp.float32)
        Wq = jax.random.normal(ks[1], (HQ * D, HID), jnp.float32) * 0.02
        Wk = jax.random.normal(ks[2], (HK * D, HID), jnp.float32) * 0.02
        Wv = jax.random.normal(ks[3], (HK * D, HID), jnp.float32) * 0.02
        Wo = jax.random.normal(ks[4], (HID, HQ * D), jnp.float32) * 0.02
        q_norm_w = jax.random.uniform(ks[5], (D,), jnp.float32)
        k_norm_w = jax.random.uniform(ks[6], (D,), jnp.float32)
        k_cache = jax.random.normal(ks[7], (PAGES, PSIZE, HK, D), jnp.float32)
        v_cache = jax.random.normal(ks[8], (PAGES, PSIZE, HK, D), jnp.float32)
        block_table = jnp.arange(B * NPP, dtype=jnp.int32).reshape(B, NPP)
        cache_seqlens = jax.random.randint(ks[9], (B,), 0, 475).astype(jnp.int32)
        return dict(x=x, Wq=Wq, Wk=Wk, Wv=Wv, Wo=Wo, q_norm_w=q_norm_w, k_norm_w=k_norm_w, k_cache=k_cache, v_cache=v_cache, block_table=block_table, cache_seqlens=cache_seqlens)
    _L3_cond_all = _L3_cond_setup()
    _L3_cond_in = {k: v for k, v in _L3_cond_all.items() if k in ('Wq', 'Wk', 'Wv', 'Wo', 'q_norm_w', 'k_norm_w', 'k_cache', 'v_cache')}
    del _L3_cond_all
    return {'x': x, 'itok_B_2_6': itok_B_2_6, 'itok_B_1_7': itok_B_1_7, 'itok_B_0_23': itok_B_0_23, 'itok_Bx16_0_63': itok_Bx16_0_63, 'itok_B_207_1644': itok_B_207_1644, 'L0_cond_W_gate': _L0_cond_in['W_gate'], 'L0_cond_W_up': _L0_cond_in['W_up'], 'L0_cond_W_down': _L0_cond_in['W_down'], 'L0_cond_A_gate': _L0_cond_in['A_gate'], 'L0_cond_B_gate': _L0_cond_in['B_gate'], 'L0_cond_A_up': _L0_cond_in['A_up'], 'L0_cond_B_up': _L0_cond_in['B_up'], 'L0_cond_A_down': _L0_cond_in['A_down'], 'L0_cond_B_down': _L0_cond_in['B_down'], 'L1_cond_weight': _L1_cond_in['weight'], 'L1_cond_bias': _L1_cond_in['bias'], 'L1_cond_lora_a_weights': _L1_cond_in['lora_a_weights'], 'L1_cond_lora_b_weights': _L1_cond_in['lora_b_weights'], 'L1_cond_scaling_factors': _L1_cond_in['scaling_factors'], 'L2_cond_W': _L2_cond_in['W'], 'L2_cond_b': _L2_cond_in['b'], 'L2_cond_lora_As': _L2_cond_in['lora_As'], 'L2_cond_lora_Bs': _L2_cond_in['lora_Bs'], 'L3_cond_Wq': _L3_cond_in['Wq'], 'L3_cond_Wk': _L3_cond_in['Wk'], 'L3_cond_Wv': _L3_cond_in['Wv'], 'L3_cond_Wo': _L3_cond_in['Wo'], 'L3_cond_q_norm_w': _L3_cond_in['q_norm_w'], 'L3_cond_k_norm_w': _L3_cond_in['k_norm_w'], 'L3_cond_k_cache': _L3_cond_in['k_cache'], 'L3_cond_v_cache': _L3_cond_in['v_cache']}

def reference(x, itok_B_2_6, itok_B_1_7, itok_B_0_23, itok_Bx16_0_63, itok_B_207_1644, L0_cond_W_gate, L0_cond_W_up, L0_cond_W_down, L0_cond_A_gate, L0_cond_B_gate, L0_cond_A_up, L0_cond_B_up, L0_cond_A_down, L0_cond_B_down, L1_cond_weight, L1_cond_bias, L1_cond_lora_a_weights, L1_cond_lora_b_weights, L1_cond_scaling_factors, L2_cond_W, L2_cond_b, L2_cond_lora_As, L2_cond_lora_Bs, L3_cond_Wq, L3_cond_Wk, L3_cond_Wv, L3_cond_Wo, L3_cond_q_norm_w, L3_cond_k_norm_w, L3_cond_k_cache, L3_cond_v_cache):
    import jax
    import jax.numpy as jnp

    def _L0_cond_ref(x, W_gate, W_up, W_down, A_gate, B_gate, A_up, B_up, A_down, B_down, lora_indices, layer_idx):
        import jax, jax.numpy as jnp
        import numpy as np
        B, N, H, F = (4, 64, 512, 1376)
        L, R, RANK = (1, 16, 16)
        SCALE = 0.5

        def lora_add(base, inp, A, B):
            Ab = A[layer_idx][lora_indices]
            Bb = B[layer_idx][lora_indices]
            t = jnp.einsum('bri,bni->bnr', Ab, inp)
            return base + jnp.einsum('bor,bnr->bno', Bb, t) * SCALE
        gate = lora_add(jnp.einsum('bnh,fh->bnf', x, W_gate), x, A_gate, B_gate)
        up = lora_add(jnp.einsum('bnh,fh->bnf', x, W_up), x, A_up, B_up)
        act = jax.nn.silu(gate) * up
        down = lora_add(jnp.einsum('bnf,hf->bnh', act, W_down), act, A_down, B_down)
        return down

    def _L1_cond_ref(x, weight, bias, lora_a_weights, lora_b_weights, scaling_factors, adapter_id):
        import jax, jax.numpy as jnp
        import numpy as np
        B, S, D_IN, D_OUT = (4, 256, 512, 512)
        N_ADAPTERS, MAX_RANK = (8, 16)
        base = jnp.einsum('bsi,oi->bso', x, weight) + bias
        a_sel = lora_a_weights[adapter_id]
        b_sel = lora_b_weights[adapter_id]
        scale = scaling_factors[adapter_id]
        low = jnp.einsum('bsi,bri->bsr', x, a_sel)
        delta = jnp.einsum('bsr,bor->bso', low, b_sel)
        return base + scale[:, None, None] * delta

    def _L2_cond_ref(x, adapter_mapping, W, b, lora_As, lora_Bs):
        import jax, jax.numpy as jnp
        import numpy as np
        R = 16
        ALPHA = 32
        SCALING = ALPHA / R
        SLOTS = 32
        IN_F = 512
        OUT_F = 512
        B, T = (8, 128)
        base_out = jnp.einsum('bti,oi->bto', x, W) + b
        A = lora_As[adapter_mapping]
        Bm = lora_Bs[adapter_mapping]
        lora_h = jnp.einsum('bti,bir->btr', x, A)
        lora_out = jnp.einsum('btr,bro->bto', lora_h, Bm)
        return base_out + lora_out * SCALING

    def _L3_cond_ref(x, Wq, Wk, Wv, Wo, q_norm_w, k_norm_w, k_cache, v_cache, block_table, cache_seqlens):
        import jax, jax.numpy as jnp
        import numpy as np
        B, S, HID = (4, 128, 512)
        D, HQ, HK = (128, 32, 8)
        PAGES, PSIZE, NPP = (64, 32, 16)
        THETA = 10000.0
        EPS = 1e-06
        SCALE = 1.0 / float(np.sqrt(D))

        def _rmsnorm(t, w):
            var = jnp.mean(t * t, axis=-1, keepdims=True)
            return t * jax.lax.rsqrt(var + EPS) * w

        def _rope(t, pos):
            inv_freq = 1.0 / THETA ** (jnp.arange(0, D, 2, dtype=jnp.float32) / D)
            freqs = pos[..., None].astype(jnp.float32) * inv_freq
            cos = jnp.cos(freqs)[:, :, None, :]
            sin = jnp.sin(freqs)[:, :, None, :]
            t1, t2 = (t[..., :D // 2], t[..., D // 2:])
            return jnp.concatenate([t1 * cos - t2 * sin, t2 * cos + t1 * sin], axis=-1)
        bsz, seqlen, _ = x.shape
        q = jnp.einsum('bsd,ed->bse', x, Wq).reshape(bsz, seqlen, HQ, D)
        k = jnp.einsum('bsd,ed->bse', x, Wk).reshape(bsz, seqlen, HK, D)
        v = jnp.einsum('bsd,ed->bse', x, Wv).reshape(bsz, seqlen, HK, D)
        q = _rmsnorm(q, q_norm_w)
        k = _rmsnorm(k, k_norm_w)
        pos = cache_seqlens[:, None] + jnp.arange(seqlen)[None, :]
        q = _rope(q, pos)
        k = _rope(k, pos)
        L = NPP * PSIZE
        kc = k_cache[block_table].reshape(bsz, L, HK, D)
        vc = v_cache[block_table].reshape(bsz, L, HK, D)
        k_all = jnp.concatenate([kc, k], axis=1)
        v_all = jnp.concatenate([vc, v], axis=1)
        valid_c = jnp.arange(L)[None, :] < cache_seqlens[:, None]
        valid = jnp.concatenate([valid_c, jnp.ones((bsz, seqlen), dtype=bool)], axis=1)
        rep = HQ // HK
        k_all = jnp.repeat(k_all, rep, axis=2)
        v_all = jnp.repeat(v_all, rep, axis=2)
        scores = jnp.einsum('bqhd,bkhd->bhqk', q, k_all) * SCALE
        scores = jnp.where(valid[:, None, None, :], scores, -1e+30)
        probs = jax.nn.softmax(scores, axis=-1)
        o = jnp.einsum('bhqk,bkhd->bqhd', probs, v_all)
        o = o.reshape(bsz, seqlen, HQ * D)
        return jnp.einsum('bse,de->bsd', o, Wo)
    x = x + _L0_cond_ref(x, L0_cond_W_gate, L0_cond_W_up, L0_cond_W_down, L0_cond_A_gate, L0_cond_B_gate, L0_cond_A_up, L0_cond_B_up, L0_cond_A_down, L0_cond_B_down, itok_B_2_6, 0)
    x = x + _L1_cond_ref(x, L1_cond_weight, L1_cond_bias, L1_cond_lora_a_weights, L1_cond_lora_b_weights, L1_cond_scaling_factors, itok_B_1_7)
    x = x + _L2_cond_ref(x, itok_B_0_23, L2_cond_W, L2_cond_b, L2_cond_lora_As, L2_cond_lora_Bs)
    x = x + _L3_cond_ref(x, L3_cond_Wq, L3_cond_Wk, L3_cond_Wv, L3_cond_Wo, L3_cond_q_norm_w, L3_cond_k_norm_w, L3_cond_k_cache, L3_cond_v_cache, itok_Bx16_0_63, itok_B_207_1644)
    return x

_drawn_inputs = setup_inputs


def setup_inputs(seed=0):
    import zlib

    import numpy as np

    out = dict(_drawn_inputs(seed))
    spreads = {}
    factors = {'L1_cond_bias': 8.0,
     'L1_cond_scaling_factors': 2.987,
     'L2_cond_b': 7.461,
     'L3_cond_Wq': 3.888,
     'L3_cond_Wk': 8.0,
     'L3_cond_Wv': 4.84,
     'L3_cond_q_norm_w': 6.765,
     'L3_cond_k_norm_w': 8.0,
     'L3_cond_k_cache': 4.065}
    for name, (base, spread) in spreads.items():
        noise = np.random.default_rng([zlib.crc32(name.encode()), seed]).standard_normal(out[name].shape)
        drawn = base * np.exp(spread * noise) if base else spread * noise
        out[name] = jnp.asarray(drawn.astype(out[name].dtype))
    for name, factor in factors.items():
        out[name] = (out[name] * factor).astype(out[name].dtype)
    return out
```

```python
from contextlib import ExitStack

import numpy as np

import concourse.bass as bass
from concourse import mybir

F32 = mybir.dt.float32
I32 = mybir.dt.int32
ALU = mybir.AluOpType
ACT = mybir.ActivationFunctionType
AX = mybir.AxisListType

P = 128
B, S, H = 8, 128, 512
KT = H // P
R = 16
F = 1376
FT = -(-F // P)
FROWS = [min(P, F - P * j) for j in range(FT)]
FSUB = 16
FPART = F // FSUB
OSUB = 4
BLK = 4
NBLK = B // BLK
TB = BLK * S
D, HQ, HK = 128, 32, 8
REP = HQ // HK
PAGES, PSIZE, NPP = 64, 32, 16
L = NPP * PSIZE
LT = L // P
NK = L + S
JT = NK // P
G = 2
NPAIR = HK // G
HP = G * REP
NH = HP + G
SCALE0, SCALE2 = 0.5, 2.0
SCALE = 1.0 / float(np.sqrt(D))
THETA, EPS = 10000.0, 1e-6
NEG = -1e30
TWO_PI = 2.0 * np.pi
ROUND = 1.5 * 2.0 ** 23


class Count:

    def __init__(self, sem, base=0):
        self.sem, self.base, self.n = sem, base, 0

    def inc(self, ins):
        self.n += 1
        return ins.then_inc(self.sem, 1)

    def value(self, back=0):
        return self.base + (self.n - back)


def build_program(nc, a):
    x, out = a["x"], a["out"]
    x_scratch = nc.dram_tensor("x3_transposed", [B, P, KT * S], F32).ap()

    ctx = ExitStack()
    with ctx:
        def sem(name):
            return ctx.enter_context(nc.semaphore(name))

        def tensor(scope, name, shape, dt=F32):
            return scope.enter_context(nc.sbuf_tensor(name, shape, dt))

        bank = [ctx.enter_context(nc.psum_tensor(f"bank{i}", [P, 512], F32)) for i in range(2)]
        wide = [ctx.enter_context(nc.psum_tensor(f"wide{i}", [P, 1024], F32)) for i in range(2)]
        tail = [ctx.enter_context(nc.psum_tensor(f"tail{i}", [P, 512], F32)) for i in range(2)]

        ident = tensor(ctx, "ident", [P, P])
        lane = tensor(ctx, "lane", [P, 1], I32)
        lane_f = tensor(ctx, "lane_f", [P, 1])
        lane16 = tensor(ctx, "lane16", [P, 1], I32)
        lane32 = tensor(ctx, "lane32", [P, 1], I32)
        hot16 = tensor(ctx, "hot16", [P, B])
        hot32 = tensor(ctx, "hot32", [P, P // PSIZE])
        mask0 = tensor(ctx, "mask0", [P, B])
        mask1 = tensor(ctx, "mask1", [P, B])
        mask2 = tensor(ctx, "mask2", [P, B])
        adapters = tensor(ctx, "adapters", [P, 3, B], I32)
        seqlens = tensor(ctx, "seqlens", [P, B], I32)
        table = tensor(ctx, "table", [P, B, LT, P // PSIZE], I32)
        picked = tensor(ctx, "picked", [P, B * LT, P // PSIZE])
        own = tensor(ctx, "own", [P, 3, B])
        own1 = tensor(ctx, "own1", [P, 4])
        own_slot = tensor(ctx, "own_slot", [P, 1], I32)
        row_r = tensor(ctx, "row_r", [P, 3], I32)
        row_f = tensor(ctx, "row_f", [P, B], I32)
        row_d = tensor(ctx, "row_d", [P, B], I32)
        row_o = tensor(ctx, "row_o", [P, B], I32)
        row_i = tensor(ctx, "row_i", [P, B, KT], I32)
        row_kv = tensor(ctx, "row_kv", [P, B * LT], I32)
        kv_f = tensor(ctx, "kv_f", [P, B * LT])
        scale1 = tensor(ctx, "scale1", [P, 1])
        x_acc = tensor(ctx, "x_acc", [P, B, H])

        s_const = sem("constants_made")
        s_small = sem("small_loaded")
        s_rows = sem("rows_ready")
        s_scale = sem("scale_gathered")
        s_dve = sem("dve_step")

        w012 = ExitStack()
        wgT = tensor(w012, "wgT", [P, KT, F])
        wuT = tensor(w012, "wuT", [P, KT, F])
        wdT = tensor(w012, "wdT", [P, FT, H])
        agT = tensor(w012, "agT", [P, KT, P])
        auT = tensor(w012, "auT", [P, KT, P])
        adT = tensor(w012, "adT", [P, FT, P])
        bgT = tensor(w012, "bgT", [P, F])
        buT = tensor(w012, "buT", [P, F])
        bdT = tensor(w012, "bdT", [P, H])
        w1T = tensor(w012, "w1T", [P, KT, H])
        w2T = tensor(w012, "w2T", [P, KT, H])
        a1T = tensor(w012, "a1T", [P, KT, P])
        a2T = tensor(w012, "a2T", [P, KT, B, R])
        b1T = tensor(w012, "b1T", [P, H])
        b2T = tensor(w012, "b2T", [P, H])
        bias1 = tensor(w012, "bias1", [P, H])
        bias2 = tensor(w012, "bias2", [P, H])

        raw = ExitStack()
        wgu_raw = tensor(raw, "wgu_raw", [P, FT, H])
        wd_raw = tensor(raw, "wd_raw", [P, KT, F])
        w1_raw = x_acc[:, 0:KT, :]
        w2_raw = x_acc[:, KT:2 * KT, :]
        ag_raw = tensor(raw, "ag_raw", [P, H])
        au_raw = tensor(raw, "au_raw", [P, H])
        a1_raw = tensor(raw, "a1_raw", [P, H])
        ad_raw = tensor(raw, "ad_raw", [P, F])
        b_raw = tensor(raw, "b_raw", [P, B, FSUB * R])
        b_perm = tensor(raw, "b_perm", [P, FSUB, B * R])
        raw.close()

        s_wg, s_wu, s_wd, s_w1, s_w2 = (sem(f"{n}_loaded") for n in ("wg", "wu", "wd", "w1", "w2"))
        s_a = sem("a_rows_gathered")
        s_b = sem("b_rows_gathered")
        s_perm = sem("b_rows_in_order")
        p_full = [sem(f"prep_full{i}") for i in range(2)]
        p_free = [sem(f"prep_free{i}") for i in range(2)]

        def w_tiles(w):
            return w.rearrange("(t p) h -> p t h", p=P)

        jobs = []

        def job(wait, pieces, rows, cols, dst):
            jobs.append((wait, pieces, rows, cols, dst))

        def transposed():
            i = len(jobs) - 1
            return p_full[i % 2], i // 2 + 1

        def gate_like(raw_t, wait, dst):
            for j, n in enumerate(FROWS):
                job(wait, [raw_t[0:n, j, k * P:(k + 1) * P] for k in range(KT)], P, n,
                    dst[:, :, j * P:j * P + n])

        b_used = []

        def spread(n, sub, dst):
            for c in range(0, sub, 4):
                job((s_perm, len(b_used) + 1), [b_perm[0:n, c + i, :] for i in range(4)], P, n,
                    dst.rearrange("q (p j) -> q j p", j=sub)[:, c:c + 4, :])
            b_used.append(transposed())

        gate_like(wgu_raw, (s_wg, 32), wgT)
        wg_used = transposed()
        for j, n in enumerate(FROWS):
            job((s_wd, 16), [wd_raw[:, t, j * P:j * P + n] for t in range(KT)], n, P,
                wdT[0:n, j, :].rearrange("p (t c) -> p t c", t=KT))
        job((s_a, 16), [ag_raw[:, k * P:(k + 1) * P] for k in range(KT)], P, P, agT[:, :, :])
        job((s_a, 32), [au_raw[:, k * P:(k + 1) * P] for k in range(KT)], P, P, auT[:, :, :])
        spread(FPART, FSUB, bgT[:, :])
        for j in range(0, FT - 1, 2):
            job((s_a, 48), [ad_raw[:, i * P:(i + 1) * P] for i in range(j, j + 2)], P, P,
                adT[:, j:j + 2, :])
        job((s_a, 48), [ad_raw[:, (FT - 1) * P:F]], FROWS[-1], P, adT[0:FROWS[-1], FT - 1:FT, :])
        gate_like(wgu_raw, (s_wu, 32), wuT)
        for raw_t, wait, dst in ((w1_raw, s_w1, w1T), (w2_raw, s_w2, w2T)):
            for t in range(KT):
                job((wait, 16), [raw_t[:, t, k * P:(k + 1) * P] for k in range(KT)], P, P,
                    dst[:, :, t * P:(t + 1) * P])
        job((s_a, 64), [a1_raw[:, k * P:(k + 1) * P] for k in range(KT)], P, P, a1T[:, :, :])
        spread(FPART, FSUB, buT[:, :])
        spread(P, OSUB, bdT[:, :])
        spread(P, OSUB, b1T[:, :])

        def prep_copies(eng, copy, which):
            n = 0
            for i, (_, pieces, rows, cols, dst) in enumerate(jobs):
                if i % 2 == which:
                    n += 1
                    eng.wait_ge(p_full[which], n)
                    src = bank[which][0:rows, 0:len(pieces) * P].rearrange("p (t c) -> p t c", c=P)
                    copy(dst, src[:, :, 0:cols]).then_inc(p_free[which], 1)

        with nc.Block() as block:
            @block.sync
            def _(sp):
                sp.dma_start(wgu_raw[:, 0:FT - 1, :], w_tiles(a["L0_cond_W_gate"][0:P * (FT - 1), :])).then_inc(s_wg, 16)
                sp.dma_start(wgu_raw[0:FROWS[-1], FT - 1, :], a["L0_cond_W_gate"][P * (FT - 1):F, :]).then_inc(s_wg, 16)
                sp.dma_start(wd_raw[:, :, :], a["L0_cond_W_down"].rearrange("(t p) f -> p t f", p=P)).then_inc(s_wd, 16)
                sp.dma_start(w1_raw, w_tiles(a["L1_cond_weight"])).then_inc(s_w1, 16)
                sp.dma_start(w2_raw, w_tiles(a["L2_cond_W"])).then_inc(s_w2, 16)
                sp.wait_ge(*wg_used)
                sp.dma_start(wgu_raw[:, 0:FT - 1, :], w_tiles(a["L0_cond_W_up"][0:P * (FT - 1), :])).then_inc(s_wu, 16)
                sp.dma_start(wgu_raw[0:FROWS[-1], FT - 1, :], a["L0_cond_W_up"][P * (FT - 1):F, :]).then_inc(s_wu, 16)

            @block.gpsimd
            def _(pool):
                nc.gpsimd.memset(ident[:, :], 0.0).then_inc(s_const, 1)
                nc.gpsimd.memset(hot16[:, :], 1.0).then_inc(s_const, 1)
                nc.gpsimd.memset(hot32[:, :], 1.0).then_inc(s_const, 1)
                nc.gpsimd.iota(lane[:, :], [[0, 1]], base=0, channel_multiplier=1).then_inc(s_const, 1)
                pool.wait_ge(s_const, 4)
                nc.gpsimd.affine_select(ident[:, :], ident[:, :], [[-1, P]], ALU.not_equal, 1.0, base=0,
                                        channel_multiplier=1).then_inc(s_const, 1)
                nc.gpsimd.affine_select(hot16[:, :], hot16[:, :], [[-R, B]], ALU.is_ge, 0.0, base=0,
                                        channel_multiplier=1).then_inc(s_const, 1)
                nc.gpsimd.affine_select(hot32[:, :], hot32[:, :], [[-PSIZE, P // PSIZE]], ALU.is_ge, 0.0, base=0,
                                        channel_multiplier=1).then_inc(s_const, 1)
                pool.wait_ge(s_const, 7)
                nc.gpsimd.affine_select(hot16[:, :], hot16[:, :], [[R, B]], ALU.is_ge, 0.0, base=R - 1,
                                        channel_multiplier=-1).then_inc(s_const, 1)
                nc.gpsimd.affine_select(hot32[:, :], hot32[:, :], [[PSIZE, P // PSIZE]], ALU.is_ge, 0.0, base=PSIZE - 1,
                                        channel_multiplier=-1).then_inc(s_const, 1)

                def gather(dst, rows, src, done):
                    nc.gpsimd.indirect_dma_start(
                        dst, None, src, bass.IndirectOffsetOnAxis(ap=rows, axis=0)).then_inc(done, 16)

                pool.wait_ge(s_rows, 1)
                gather(ag_raw[:, :], row_r[:, 0:1], a["L0_cond_A_gate"].rearrange("l a r h -> (l a r) h"), s_a)
                pool.wait_ge(s_a, 16)
                gather(au_raw[:, :], row_r[:, 0:1], a["L0_cond_A_up"].rearrange("l a r h -> (l a r) h"), s_a)
                pool.wait_ge(s_a, 32)
                gather(ad_raw[:, :], row_r[:, 0:1], a["L0_cond_A_down"].rearrange("l a r h -> (l a r) h"), s_a)
                pool.wait_ge(s_a, 48)
                gather(a1_raw[:, :], row_r[:, 1:2], a["L1_cond_lora_a_weights"].rearrange("a r h -> (a r) h"), s_a)
                gather(scale1[:, :], own_slot[:, :], a["L1_cond_scaling_factors"].rearrange("(a o) -> a o", o=1), s_scale)

                for i, (n, sub, rows, src) in enumerate((
                        (FPART, FSUB, row_f, a["L0_cond_B_gate"].rearrange("l a (p j) r -> (l a p) (j r)", j=FSUB)),
                        (FPART, FSUB, row_f, a["L0_cond_B_up"].rearrange("l a (p j) r -> (l a p) (j r)", j=FSUB)),
                        (P, OSUB, row_d, a["L0_cond_B_down"].rearrange("l a (p j) r -> (l a p) (j r)", j=OSUB)),
                        (P, OSUB, row_o, a["L1_cond_lora_b_weights"].rearrange("a (p j) r -> (a p) (j r)", j=OSUB)))):
                    if i:
                        pool.wait_ge(s_perm, i)
                    for b in range(B):
                        gather(b_raw[0:n, b, 0:sub * R], rows[0:n, b:b + 1], src, s_b)
                    pool.wait_ge(s_b, 16 * B * (i + 1))
                    if i:
                        pool.wait_ge(*b_used[i - 1])
                    nc.gpsimd.tensor_copy(b_perm[0:n, 0:sub, :].rearrange("p j (b r) -> p b j r", r=R),
                                          b_raw[0:n, :, 0:sub * R].rearrange("p b (j r) -> p b j r", r=R)).then_inc(s_perm, 1)
                gather(b2T[:, :], row_r[:, 2:3], a["L2_cond_lora_Bs"].rearrange("a r o -> (a r) o"), s_b)
                for b in range(B):
                    for k in range(KT):
                        gather(a2T[:, k, b, :], row_i[:, b, k:k + 1], a["L2_cond_lora_As"].rearrange("a i r -> (a i) r"), s_b)
                pool.wait_ge(s_b, 16 * (4 * B + 1 + B * KT))

            @block.tensor
            def _(pe):
                pe.wait_ge(s_const, 5)
                for i, (wait, pieces, rows, cols, _) in enumerate(jobs):
                    pe.wait_ge(*wait)
                    if i >= 2:
                        pe.wait_ge(p_free[i % 2], i // 2)
                    for c, piece in enumerate(pieces):
                        k = piece.shape[0]
                        last = nc.tensor.transpose(bank[i % 2][0:rows, c * P:c * P + cols], piece, ident[0:k, 0:k])
                    last.then_inc(p_full[i % 2], 1)

            @block.scalar
            def _(act):
                for i, n in enumerate(("itok_B_2_6", "itok_B_1_7", "itok_B_0_23")):
                    act.dma_start(adapters[:, i, :], a[n].rearrange("(o b) -> o b", o=1).to_broadcast([P, B])).then_inc(s_small, 16)
                act.dma_start(seqlens[:, :], a["itok_B_207_1644"].rearrange("(o b) -> o b", o=1).to_broadcast([P, B])).then_inc(s_small, 16)
                act.dma_start(table[:, :, :, :].rearrange("p b t g -> p (b t g)"),
                              a["itok_Bx16_0_63"].rearrange("(o b) n -> o (b n)", o=1).to_broadcast([P, B * NPP])).then_inc(s_small, 16)
                act.dma_start(bias1[:, :], a["L1_cond_bias"].rearrange("(o h) -> o h", o=1).to_broadcast([P, H])).then_inc(s_small, 16)
                act.dma_start(bias2[:, :], a["L2_cond_b"].rearrange("(o h) -> o h", o=1).to_broadcast([P, H])).then_inc(s_small, 16)
                prep_copies(act, nc.scalar.copy, 0)

            @block.vector
            def _(dve):
                step = Count(s_dve)

                def then(ins):
                    step.inc(ins)
                    dve.wait_ge(s_dve, step.value())

                v = nc.vector
                dve.wait_ge(s_const, 9)
                dve.wait_ge(s_small, 16 * 7)
                v.tensor_copy(lane_f[:, :], lane[:, :])
                v.tensor_scalar(lane16[:, :], lane[:, :], R - 1, None, ALU.bitwise_and)
                v.tensor_scalar(lane32[:, :], lane[:, :], PSIZE - 1, None, ALU.bitwise_and)
                for i in range(3):
                    last = v.tensor_tensor(own[:, i, :], adapters[:, i, :], hot16[:, :], ALU.mult)
                then(last)
                then(v.tensor_reduce(own1[:, 0:3], own[:, :, :], AX.X, ALU.add))
                v.tensor_copy(own_slot[:, :], own1[:, 1:2])
                for i in range(3):
                    v.scalar_tensor_tensor(row_r[:, i:i + 1], own1[:, i:i + 1], float(R), lane16[:, :], ALU.mult, ALU.add)
                v.tensor_scalar(row_f[:, :], adapters[:, 0, :], float(FPART), lane_f[:, 0:1], ALU.mult, ALU.add)
                v.tensor_scalar(row_d[:, :], adapters[:, 0, :], float(P), lane_f[:, 0:1], ALU.mult, ALU.add)
                v.tensor_scalar(row_o[:, :], adapters[:, 1, :], float(P), lane_f[:, 0:1], ALU.mult, ALU.add)
                for k in range(KT):
                    v.tensor_scalar(row_i[:, :, k], adapters[:, 2, :], float(H), float(k * P), ALU.mult, ALU.add)
                for g in range(P // PSIZE):
                    last = v.tensor_scalar(picked[:, :, g], table[:, :, :, g].rearrange("p b t -> p (b t)"),
                                           hot32[:, g:g + 1], None, ALU.mult)
                then(last)
                then(v.tensor_reduce(kv_f[:, :], picked[:, :, :], AX.X, ALU.add))
                v.tensor_scalar(kv_f[:, :], kv_f[:, :], float(PSIZE), None, ALU.mult)
                then(v.tensor_copy(own1[:, 3:4], lane32[:, :]))
                v.tensor_scalar(row_kv[:, :], kv_f[:, :], own1[:, 3:4], float(NPAIR), ALU.add, ALU.mult)
                then(v.tensor_scalar(row_i[:, :, :], row_i[:, :, :], lane_f[:, 0:1], None, ALU.add))
                v.tensor_scalar(mask0[:, :], hot16[:, :], SCALE0, None, ALU.mult)
                v.tensor_scalar(mask2[:, :], hot16[:, :], SCALE2, None, ALU.mult).then_inc(s_rows, 1)
                prep_copies(dve, v.tensor_copy, 1)
                dve.wait_ge(s_scale, 16)
                v.tensor_scalar(mask1[:, :], hot16[:, :], scale1[:, 0:1], None, ALU.mult)

        work = ExitStack()
        xb = tensor(work, "xb", [P, BLK, H])
        xT = tensor(work, "xT", [P, KT, TB])
        xres = tensor(work, "xres", [P, BLK, H])
        actT = tensor(work, "actT", [P, FT, TB])
        silu = tensor(work, "silu", [P, 2, TB])
        tg = tensor(work, "tg", [P, TB])
        tu = tensor(work, "tu", [P, TB])
        td = tensor(work, "td", [P, TB])
        work.close()
        w012.close()

        s_x = sem("x_loaded")
        s_xa = sem("x_acc_written")
        s_xs = sem("xT_stored")
        s_gu = sem("gate_up_full")
        s_si = sem("silu_ready")
        s_act = sem("act_ready")
        s_yf = sem("layer_out_full")
        s_x1 = sem("x_updated")
        s_res = sem("bias_added")
        m_full = [sem(f"xpose_full{i}") for i in range(2)]
        m_free = [sem(f"xpose_free{i}") for i in range(2)]
        NXT = 4
        NA, NB_ = 2 * NXT, 2 * NXT + 5
        NY = 3 * BLK

        def gate_bank(j):
            return wide[j % 2][:, 0:512]

        def up_bank(j):
            return wide[j % 2][:, 512:1024]

        with nc.Block() as block:
            @block.sync
            def _(sp):
                for t in range(NBLK):
                    if t:
                        sp.wait_ge(s_xa, t)
                    sp.dma_start(xb[:, :, :], x[t * BLK:(t + 1) * BLK].rearrange("b p h -> p b h")).then_inc(s_x, 16)
                    sp.wait_ge(m_free[0], (t + 1) * NA)
                    sp.wait_ge(m_free[1], (t + 1) * NB_)
                    for i in range(BLK):
                        sp.dma_start(x_scratch[t * BLK + i].rearrange("p (k c) -> p k c", k=KT),
                                     xT[:, :, i * S:(i + 1) * S]).then_inc(s_xs, 16)
                sp.wait_ge(s_xs, 16 * B)

            @block.gpsimd
            def _(pool):
                with pool.Fori(0, NBLK) as t:
                    for n, bias in enumerate((bias1, bias2)):
                        pool.wait_ge(s_x1, t * NY + BLK * (n + 1))
                        for i in range(BLK):
                            last = nc.gpsimd.tensor_tensor(xres[:, i, :], xb[:, i, :], bias[:, :], ALU.add)
                        last.then_inc(s_res, 1)
                    pool.wait_ge(s_x1, t * NY + NY)
                    nc.gpsimd.tensor_copy(x_acc[:, bass.ds(t * BLK, BLK), :], xb[:, :, :]).then_inc(s_xa, 1)

            @block.tensor
            def _(pe):
                with pe.Fori(0, NBLK) as t:
                    full = [Count(m_full[0], t * NA), Count(m_full[1], t * NB_)]
                    y = Count(s_yf, t * NY)

                    def begin(i):
                        pe.wait_ge(m_free[i], full[i].value())

                    def transpose_x():
                        for k in range(KT):
                            begin(k % 2)
                            for i in range(BLK):
                                last = nc.tensor.transpose(bank[k % 2][:, i * S:(i + 1) * S], xb[:, i, k * P:(k + 1) * P], ident[:, :])
                            full[k % 2].inc(last)
                        begin(0)
                        begin(1)

                    def lora_rows(aT, rhs, rows):
                        begin(1)
                        for k, n in enumerate(rows):
                            last = nc.tensor.matmul(bank[1][:, :], aT(k, n), rhs[0:n, k, :], start=(k == 0), stop=(k == len(rows) - 1))
                        full[1].inc(last)

                    def layer_out(i, lhs, rhs, rows, lora, loraB):
                        pe.wait_ge(s_x1, y.value(1) if y.n else y.value())
                        yb = tail[y.n % 2]
                        for k, n in enumerate(rows):
                            nc.tensor.matmul(yb[:, :], lhs[0:n, k, i * S:(i + 1) * S], rhs[0:n, k, :], start=(k == 0), stop=False)
                        y.inc(nc.tensor.matmul(yb[:, :], lora[:, i * S:(i + 1) * S], loraB[:, :], start=False, stop=True))

                    pe.wait_ge(s_x, t * 16 + 16)
                    transpose_x()
                    lora_rows(lambda k, n: agT[:, k, :], xT, [P] * KT)
                    lora_rows(lambda k, n: auT[:, k, :], xT, [P] * KT)
                    begin(1)
                    for j, n in enumerate(FROWS):
                        pe.wait_ge(s_act, t * FT + max(j - 1, 0))
                        for w, tl, bT, dst in ((wgT, tg, bgT, gate_bank(j)), (wuT, tu, buT, up_bank(j))):
                            for k in range(KT):
                                nc.tensor.matmul(dst[0:n, :], w[:, k, j * P:j * P + n], xT[:, k, :], start=(k == 0), stop=False)
                            last = nc.tensor.matmul(dst[0:n, :], bT[:, j * P:j * P + n], tl[:, :], start=False, stop=True)
                        last.then_inc(s_gu, 1)
                    pe.wait_ge(s_act, t * FT + FT)
                    lora_rows(lambda k, n: adT[0:n, k, :], actT, FROWS)
                    begin(1)
                    for i in range(BLK):
                        layer_out(i, actT, wdT, FROWS, td, bdT)
                    for n, (aT, w, bT) in enumerate(((a1T, w1T, b1T), (a2T, w2T, b2T))):
                        pe.wait_ge(s_x1, y.value())
                        transpose_x()
                        lora_rows(lambda k, m: aT[:, k].rearrange("p b r -> p (b r)") if aT is a2T else aT[:, k, :], xT, [P] * KT)
                        begin(1)
                        for i in range(BLK):
                            layer_out(i, xT, w, [P] * KT, tg, bT)
                    pe.wait_ge(s_x1, y.value())
                    transpose_x()

            @block.scalar
            def _(act):
                with act.Fori(0, NBLK) as t:
                    full = Count(m_full[0], t * NA)

                    def copy_x():
                        for k in range(0, KT, 2):
                            full.n += 1
                            act.wait_ge(m_full[0], full.value())
                            nc.scalar.copy(xT[:, k, :], bank[0][:, :]).then_inc(m_free[0], 1)

                    act.wait_ge(s_xs, t * (16 * BLK))
                    copy_x()
                    for j, n in enumerate(FROWS):
                        act.wait_ge(s_gu, t * FT + j + 1)
                        act.wait_ge(s_act, t * FT + max(j - 1, 0))
                        nc.scalar.activation(silu[0:n, j % 2, :], gate_bank(j)[0:n, :], ACT.Silu).then_inc(s_si, 1)
                    for _ in range(NXT - 1):
                        copy_x()

            @block.vector
            def _(dve):
                v = nc.vector
                with dve.Fori(0, NBLK) as t:
                    full = Count(m_full[1], t * NB_)
                    y = Count(s_yf, t * NY)

                    def arrive():
                        full.n += 1
                        dve.wait_ge(m_full[1], full.value())

                    def copy_x():
                        for k in range(1, KT, 2):
                            arrive()
                            v.tensor_copy(xT[:, k, :], bank[1][:, :]).then_inc(m_free[1], 1)

                    def mask_rows(dst, mask):
                        arrive()
                        v.tensor_tensor(dst[:, :].rearrange("p (b c) -> p b c", b=BLK), bank[1][:, :].rearrange("p (b c) -> p b c", b=BLK),
                                        mask[:, bass.ds(t * BLK, BLK)].rearrange("p (b o) -> p b o", o=1).to_broadcast([P, BLK, S]),
                                        ALU.mult).then_inc(m_free[1], 1)

                    def update(i, base):
                        y.n += 1
                        dve.wait_ge(s_yf, y.value())
                        v.tensor_tensor(xb[:, i, :], tail[(y.n - 1) % 2][:, :], base[:, i, :], ALU.add).then_inc(s_x1, 1)

                    dve.wait_ge(s_xs, t * (16 * BLK))
                    copy_x()
                    mask_rows(tg, mask0)
                    mask_rows(tu, mask0)
                    for j, n in enumerate(FROWS):
                        dve.wait_ge(s_si, t * FT + j + 1)
                        v.tensor_tensor(actT[0:n, j, :], silu[0:n, j % 2, :], up_bank(j)[0:n, :], ALU.mult).then_inc(s_act, 1)
                    mask_rows(td, mask0)
                    for i in range(BLK):
                        update(i, xb)
                    for n, mask in enumerate((mask1, mask2)):
                        copy_x()
                        mask_rows(tg, mask)
                        dve.wait_ge(s_res, t * 2 + n + 1)
                        for i in range(BLK):
                            update(i, xres)
                    copy_x()

        build_attention(nc, a, ctx, tensor, sem, bank, wide, tail, ident, lane_f, seqlens, row_kv, x_acc, x_scratch, out)


def build_attention(nc, a, ctx, tensor, sem, bank, wide, tail, ident, lane_f, seqlens, row_kv, x_acc, x_scratch, out):
    QW = HP * D
    wq_raw = tensor(ctx, "wq_raw", [P, HP, H])
    wkv_raw = tensor(ctx, "wkv_raw", [P, 2 * G, H])
    wo_raw = tensor(ctx, "wo_raw", [P, KT, QW])
    wqT = tensor(ctx, "wqT", [P, KT, QW])
    wkvT = tensor(ctx, "wkvT", [P, KT, 2 * G * D])
    woT = tensor(ctx, "woT", [P, HP, H])
    xTb = tensor(ctx, "xTb", [P, KT, S])
    k_raw = tensor(ctx, "k_raw", [P, LT, G * D])
    vt = tensor(ctx, "vt", [P, JT, G * D])
    rows_now = tensor(ctx, "rows_now", [P, LT], I32)
    qk = tensor(ctx, "qk", [P, NH, D])
    ra = tensor(ctx, "ra", [P, NH, D])
    rb = tensor(ctx, "rb", [P, NH, D])
    qT = tensor(ctx, "qT", [P, G, REP * S])
    kT = tensor(ctx, "kT", [P, G, NK])
    sm = tensor(ctx, "sm", [P, 2, NK])
    pr = tensor(ctx, "pr", [P, HP, NK])
    prT = tensor(ctx, "prT", [P, G, JT, REP * S])
    oT = tensor(ctx, "oT", [P, G, REP * S])
    rope = tensor(ctx, "rope", [P, B, 2, 2, D])
    trig = prT[:, 0, 0:4, :].rearrange("p c (b d) -> p c b d", b=B)
    normw = tensor(ctx, "normw", [P, 2, D])
    freq = tensor(ctx, "freq", [P, D // 2])
    pos = tensor(ctx, "pos", [P, B])
    seq_f = tensor(ctx, "seq_f", [P, B])
    key_no = tensor(ctx, "key_no", [P, NK])
    bias = tensor(ctx, "bias", [P, NK])
    ss = tensor(ctx, "ss", [P, NH])
    var = tensor(ctx, "var", [P, NH])
    rs = tensor(ctx, "rs", [P, NH])
    nt = tensor(ctx, "nt", [P, NH])
    mx = tensor(ctx, "mx", [P, HP])
    nm = tensor(ctx, "nm", [P, HP])
    den = tensor(ctx, "den", [P, HP])
    rden = tensor(ctx, "rden", [P, HP])
    tick = tensor(ctx, "tick", [P, 3])

    s_in = sem("norm_weights_loaded")
    s_w = sem("pair_weights_loaded")
    s_xt = sem("xTb_loaded")
    s_k = sem("cached_keys_loaded")
    s_v = sem("cached_values_loaded")
    s_rowsnow = sem("rows_now_ready")
    s_rowskv = sem("pair_rows_ready")
    s_carry = sem("pool_waits_carried")
    s_keyno = sem("key_numbers_made")
    s_trig = sem("angles_ready")
    s_sincos = sem("sines_ready")
    s_step = sem("dve_step3")
    s_kc = sem("new_keys_copied")
    s_sq = sem("squares_ready")
    s_rope = sem("rotated")
    s_sfull = sem("scores_full")
    s_sfree = sem("scores_masked")
    s_nm = sem("negative_max_ready")
    s_exp = sem("exp_done")
    s_rden = sem("denominator_ready")
    s_p = sem("probs_ready")
    s_pv = sem("values_summed")
    s_o = sem("values_copied")
    s_y = sem("out_share_full")
    s_yadd = sem("out_share_added")
    s_out = sem("out_stored")
    c_full = [sem(f"chunk_full{i}") for i in range(2)]
    c_free = [sem(f"chunk_free{i}") for i in range(2)]

    WCH = HP + 2 * G + HP
    UCH = 8 + G * JT
    assert WCH % 2 == 0 and UCH % 2 == 0
    WC, UC = WCH // 2, UCH // 2

    def weight_jobs():
        for t in range(HP):
            yield [wq_raw[:, t, k * P:(k + 1) * P] for k in range(KT)], wqT[:, :, t * P:(t + 1) * P]
        for t in range(2 * G):
            yield [wkv_raw[:, t, k * P:(k + 1) * P] for k in range(KT)], wkvT[:, :, t * P:(t + 1) * P]
        for h in range(HP):
            yield [wo_raw[:, t, h * D:(h + 1) * D] for t in range(KT)], woT[:, h, :].rearrange("p (t c) -> p t c", t=KT)

    k_rows = a["L3_cond_k_cache"].rearrange("a s (e g) d -> (a s e) (g d)", g=G)
    v_rows = a["L3_cond_v_cache"].rearrange("a s (e g) d -> (a s e) (g d)", g=G)

    def unit(pair, b):
        return pair * B + b

    def chunk_base(pair, b):
        return pair * (WC + B * UC) + b * UC + WC

    with nc.Block() as block:
        @block.sync
        def _(sp):
            sp.dma_start(normw[:, 0, :], a["L3_cond_q_norm_w"].rearrange("(o d) -> o d", o=1).to_broadcast([P, D])).then_inc(s_in, 16)
            sp.dma_start(normw[:, 1, :], a["L3_cond_k_norm_w"].rearrange("(o d) -> o d", o=1).to_broadcast([P, D])).then_inc(s_in, 16)
            sp.dma_start(freq[:, :], a["inv_freq"].rearrange("(o d) -> o d", o=1).to_broadcast([P, D // 2])).then_inc(s_in, 16)
            sp.wait_ge(s_yadd, NPAIR * B)
            sp.dma_start(out.rearrange("b p h -> p b h"), x_acc[:, :, :]).then_inc(s_out, 16)
            sp.wait_ge(s_out, 16)

        @block.gpsimd
        def _(pool):
            nc.gpsimd.iota(key_no[:, 0:L], [[1, L]], base=0, channel_multiplier=0,
                           allow_small_or_imprecise_dtypes=True).then_inc(s_keyno, 1)
            nc.gpsimd.memset(key_no[:, L:NK], -1.0).then_inc(s_keyno, 1)
            nc.gpsimd.memset(tick[:, 1:3], 0.0).then_inc(s_keyno, 1)
            pool.wait_ge(s_keyno, 3)
            NCARRY = 1 + 3 * B

            def carry(n):
                pool.wait_ge(s_carry, n)
                nc.gpsimd.tensor_tensor(tick[:, 2:3], tick[:, 1:2], tick[:, 1:2], ALU.add).then_inc(s_carry, 1)

            with pool.Fori(0, NPAIR) as pair:
                pool.wait_ge(s_sq, pair * (B * G))
                carry(pair * NCARRY)
                nc.gpsimd.dma_start(wq_raw[:, :, :], a["L3_cond_Wq"][bass.ds(pair * QW, QW)].rearrange("(t p) h -> p t h", p=P)).then_inc(s_w, 16)
                nc.gpsimd.dma_start(wkv_raw[:, 0:G, :], a["L3_cond_Wk"][bass.ds(pair * (G * D), G * D)].rearrange("(t p) h -> p t h", p=P)).then_inc(s_w, 16)
                nc.gpsimd.dma_start(wkv_raw[:, G:2 * G, :], a["L3_cond_Wv"][bass.ds(pair * (G * D), G * D)].rearrange("(t p) h -> p t h", p=P)).then_inc(s_w, 16)
                nc.gpsimd.dma_start(wo_raw[:, :, :], a["L3_cond_Wo"][:, bass.ds(pair * QW, QW)].rearrange("(t p) e -> p t e", p=P)).then_inc(s_w, 16)
                with pool.Fori(0, B) as b:
                    u = unit(pair, b)
                    pool.wait_ge(s_sq, u * G)
                    carry(pair * NCARRY + b * 3 + 1)
                    nc.gpsimd.dma_start(xTb[:, :, :].rearrange("p k c -> p (k c)"),
                                        x_scratch[bass.ds(b, 1)].rearrange("o p n -> (o p) n")).then_inc(s_xt, 16)
                    pool.wait_ge(s_rowskv, pair)
                    nc.gpsimd.tensor_copy(rows_now[:, :], row_kv[:, bass.ds(b * LT, LT)]).then_inc(s_rowsnow, 1)
                    pool.wait_ge(s_sfull, u * HP)
                    pool.wait_ge(s_rowsnow, u + 1)
                    carry(pair * NCARRY + b * 3 + 2)
                    for t in range(LT):
                        nc.gpsimd.indirect_dma_start(k_raw[:, t, :], None, k_rows,
                                                     bass.IndirectOffsetOnAxis(ap=rows_now[:, t:t + 1], axis=0)).then_inc(s_k, 16)
                    pool.wait_ge(s_pv, u * G)
                    carry(pair * NCARRY + b * 3 + 3)
                    for t in range(LT):
                        nc.gpsimd.indirect_dma_start(vt[:, t, :], None, v_rows,
                                                     bass.IndirectOffsetOnAxis(ap=rows_now[:, t:t + 1], axis=0)).then_inc(s_v, 16)
                    pool.wait_ge(s_v, (u + 1) * (16 * LT))

        @block.tensor
        def _(pe):
            with pe.Fori(0, NPAIR) as pair:
                full = [Count(c, pair * (WC + B * UC)) for c in c_full]
                pe.wait_ge(s_w, pair * 64 + 64)
                for i, (pieces, _) in enumerate(weight_jobs()):
                    pe.wait_ge(c_free[i % 2], full[i % 2].value())
                    for c, piece in enumerate(pieces):
                        last = nc.tensor.transpose(bank[i % 2][:, c * P:(c + 1) * P], piece, ident[:, :])
                    full[i % 2].inc(last)
                with pe.Fori(0, B) as b:
                    u = unit(pair, b)
                    full = [Count(c, chunk_base(pair, b)) for c in c_full]

                    def begin(i):
                        pe.wait_ge(c_free[i], full[i].value())

                    def project(i, w):
                        begin(i)
                        for k in range(KT):
                            last = nc.tensor.matmul(bank[i][:, :], xTb[:, k, :], w[:, k, :], start=(k == 0), stop=(k == KT - 1))
                        full[i].inc(last)
                        return last

                    def transposes(i, pieces):
                        begin(i)
                        for c, piece in enumerate(pieces):
                            last = nc.tensor.transpose(bank[i][:, c * P:(c + 1) * P], piece, ident[:, :])
                        full[i].inc(last)
                        return last

                    def score(h):
                        if h < 2:
                            pe.wait_ge(s_sfree, u * HP)
                        else:
                            pe.wait_ge(s_sfree, u * HP + (h - 1))
                        g, i = h // REP, h % REP
                        q = qT[:, g, i * S:(i + 1) * S]
                        nc.tensor.matmul(wide[h % 2][:, 0:L], q, kT[:, g, 0:L], start=True, stop=True)
                        nc.tensor.matmul(wide[h % 2][:, L:NK], q, kT[:, g, L:NK], start=True, stop=True).then_inc(s_sfull, 1)

                    begin(0)
                    begin(1)
                    pe.wait_ge(s_xt, u * 16 + 16)
                    project(0, wkvT)
                    project(1, wqT[:, :, 0:REP * D])
                    project(0, wqT[:, :, REP * D:QW])
                    pe.wait_ge(s_k, (u + 1) * (16 * LT))
                    transposes(1, [k_raw[:, t, 0:D] for t in range(LT)])
                    transposes(0, [k_raw[:, t, D:2 * D] for t in range(LT)])
                    pe.wait_ge(s_rope, u * G + 1)
                    transposes(1, [ra[:, i, :] for i in range(REP)])
                    transposes(0, [ra[:, REP + i, :] for i in range(G)])
                    begin(0)
                    begin(1)
                    for h in range(REP):
                        score(h)
                    pe.wait_ge(s_rope, u * G + 2)
                    transposes(1, [ra[:, REP + G + i, :] for i in range(REP)])
                    begin(1)
                    for h in range(REP, HP):
                        score(h)
                    for g in range(G):
                        pe.wait_ge(s_p, u * HP + (g + 1) * REP)
                        for j in range(JT):
                            transposes((g * JT + j) % 2, [pr[:, g * REP + i, j * P:(j + 1) * P] for i in range(REP)])
                        begin(0)
                        begin(1)
                        pe.wait_ge(s_o, u * G + g)
                        if g == 0:
                            pe.wait_ge(s_v, (u + 1) * (16 * LT))
                        for j in range(JT):
                            last = nc.tensor.matmul(tail[0][:, :], vt[:, j, g * D:(g + 1) * D], prT[:, g, j, :], start=(j == 0), stop=(j == JT - 1))
                        last.then_inc(s_pv, 1)
                    pe.wait_ge(s_yadd, u)
                    for h in range(HP):
                        if h % REP == 0:
                            pe.wait_ge(s_o, u * G + h // REP + 1)
                        last = nc.tensor.matmul(tail[1][:, :], oT[:, h // REP, (h % REP) * S:(h % REP + 1) * S], woT[:, h, :],
                                                start=(h == 0), stop=(h == HP - 1))
                    last.then_inc(s_y, 1)

        @block.scalar
        def _(act):
            ac = nc.scalar
            act.wait_ge(s_trig, 1)
            for i in range(2):
                last = ac.activation(trig[:, 2 + i, :, :], trig[:, i, :, :], ACT.Sin)
            last.then_inc(s_sincos, 1)
            with act.Fori(0, NPAIR) as pair:
                full = Count(c_full[0], pair * (WC + B * UC))

                for i, (_, dst) in enumerate(weight_jobs()):
                    if i % 2 == 0:
                        full.n += 1
                        act.wait_ge(c_full[0], full.value())
                        ac.copy(dst, bank[0][:, :].rearrange("p (t c) -> p t c", t=KT)).then_inc(c_free[0], 1)
                with act.Fori(0, B) as b:
                    u = unit(pair, b)
                    full0 = Count(c_full[0], chunk_base(pair, b))

                    def arrive():
                        full0.n += 1
                        act.wait_ge(c_full[0], full0.value())

                    def squares(h0, n):
                        for h in range(h0, h0 + n):
                            last = ac.activation(ra[:, h, :], qk[:, h, :], ACT.Square, accum_out=ss[:, h:h + 1])
                        last.then_inc(s_sq, 1)

                    arrive()
                    act.wait_ge(s_rope, u * G)
                    ac.copy(qk[:, REP:REP + G, :], bank[0][:, 0:G * D].rearrange("p (h d) -> p h d", d=D)).then_inc(s_kc, 1)
                    ac.copy(vt[:, LT, :], bank[0][:, G * D:2 * G * D]).then_inc(c_free[0], 1)
                    act.wait_ge(s_kc, u + 1)
                    act.wait_ge(c_free[1], chunk_base(pair, b) + 1)
                    squares(0, REP + G)
                    arrive()
                    ac.copy(qk[:, REP + G:NH, :], bank[0][:, :].rearrange("p (h d) -> p h d", d=D)).then_inc(c_free[0], 1)
                    act.wait_ge(c_free[0], full0.value())
                    squares(REP + G, REP)
                    arrive()
                    ac.copy(kT[:, 1, 0:L], bank[0][:, :]).then_inc(c_free[0], 1)
                    arrive()
                    ac.copy(kT[:, :, L:NK], bank[0][:, 0:G * S].rearrange("p (g c) -> p g c", g=G)).then_inc(c_free[0], 1)

                    def exponential(h):
                        act.wait_ge(s_nm, u * HP + h + 1)
                        if h % REP == 0:
                            act.wait_ge(s_pv, u * G)
                        ac.activation(pr[:, h, :], sm[:, h % 2, :], ACT.Exp, bias=nm[:, h:h + 1], scale=SCALE,
                                      accum_out=den[:, h:h + 1]).then_inc(s_exp, 1)

                    def normalise(h):
                        act.wait_ge(s_rden, u * HP + h + 1)
                        ac.activation(pr[:, h, :], pr[:, h, :], ACT.Copy, scale=rden[:, h:h + 1]).then_inc(s_p, 1)

                    def copy_probs(g):
                        for j in range(JT):
                            if (g * JT + j) % 2 == 0:
                                arrive()
                                ac.copy(prT[:, g, j, :], bank[0][:, :]).then_inc(c_free[0], 1)
                        act.wait_ge(s_pv, u * G + g + 1)
                        ac.copy(oT[:, g, :], tail[0][:, :]).then_inc(s_o, 1)

                    for h in range(HP):
                        exponential(h)
                        if h:
                            normalise(h - 1)
                    normalise(HP - 1)
                    for g in range(G):
                        copy_probs(g)

        @block.vector
        def _(dve):
            v = nc.vector
            step = Count(s_step)

            def then(ins):
                step.inc(ins)
                dve.wait_ge(s_step, step.value())

            dve.wait_ge(s_in, 48)
            v.tensor_copy(seq_f[:, :], seqlens[:, :])
            then(v.tensor_scalar(pos[:, :], seqlens[:, :], lane_f[:, 0:1], None, ALU.add))
            angle, turns = trig[:, 2, :, :], trig[:, 3, :, :]
            for b in range(B):
                last = v.tensor_scalar(angle[:, b, :], freq[:, :], pos[:, b:b + 1], None, ALU.mult)
            then(last)
            c1 = np.float32(6.28125)
            c2 = np.float32(np.floor((TWO_PI - float(c1)) * 2.0 ** 21) / 2.0 ** 21)
            c3 = np.float32(TWO_PI - float(c1) - float(c2))
            for i, quarter in ((0, 0.0), (1, 0.25)):
                red = trig[:, i, :, :]
                then(v.tensor_scalar(turns, angle, 1.0 / TWO_PI, quarter, ALU.mult, ALU.add))
                then(v.tensor_scalar(turns, turns, ROUND, ROUND, ALU.add, ALU.subtract))
                then(v.scalar_tensor_tensor(red, turns, -float(c1), angle, ALU.mult, ALU.add))
                then(v.scalar_tensor_tensor(red, turns, -float(c2), red, ALU.mult, ALU.add))
                then(v.scalar_tensor_tensor(red, turns, -float(c3), red, ALU.mult, ALU.add))
                then(v.tensor_scalar(red, red, quarter * TWO_PI, 3.1415925, ALU.add, ALU.min))
                then(v.tensor_scalar(red, red, -3.1415925, None, ALU.max))
            v.tensor_scalar(turns[:, 0, 0:1], pos[:, 0:1], 0.0, None, ALU.mult).then_inc(s_trig, 1)
            dve.wait_ge(s_sincos, 1)
            half = D // 2
            sin, cos = trig[:, 2, :, :], trig[:, 3, :, :]
            for i in range(2):
                w1 = normw[:, i:i + 1, 0:half].to_broadcast([P, B, half])
                w2 = normw[:, i:i + 1, half:D].to_broadcast([P, B, half])
                v.tensor_tensor(rope[:, :, i, 0, 0:half], cos, w1, ALU.mult)
                v.tensor_tensor(rope[:, :, i, 0, half:D], cos, w2, ALU.mult)
                v.scalar_tensor_tensor(rope[:, :, i, 1, 0:half], sin, -1.0, w2, ALU.mult, ALU.mult)
                last = v.tensor_tensor(rope[:, :, i, 1, half:D], sin, w1, ALU.mult)
            then(last)
            dve.wait_ge(s_keyno, 2)
            first_steps = step.n
            NSTEP = 33

            with dve.Fori(0, NPAIR) as pair:
                full = Count(c_full[1], pair * (WC + B * UC))
                for i, (_, dst) in enumerate(weight_jobs()):
                    if i % 2 == 1:
                        full.n += 1
                        dve.wait_ge(c_full[1], full.value())
                        v.tensor_copy(dst, bank[1][:, :].rearrange("p (t c) -> p t c", t=KT)).then_inc(c_free[1], 1)

                with dve.Fori(0, B) as b:
                    u = unit(pair, b)
                    full1 = Count(c_full[1], chunk_base(pair, b))
                    at = Count(s_step, u * NSTEP + first_steps)

                    def then(ins):
                        at.inc(ins)
                        dve.wait_ge(s_step, at.value())

                    def arrive():
                        full1.n += 1
                        dve.wait_ge(c_full[1], full1.value())

                    def rotate(part, h0, n, kinds):
                        dve.wait_ge(s_sq, u * G + part + 1)
                        x_, y_, t_ = var[:, h0:h0 + n], rs[:, h0:h0 + n], nt[:, h0:h0 + n]
                        then(v.tensor_scalar(x_, ss[:, h0:h0 + n], 1.0 / D, EPS, ALU.mult, ALU.add))
                        then(v.tensor_scalar(y_.bitcast(I32), x_.bitcast(I32), -0.5, float(0x5F3759DF), ALU.mult, ALU.add))
                        for _ in range(4):
                            then(v.tensor_tensor(t_, y_, y_, ALU.mult))
                            then(v.scalar_tensor_tensor(t_, t_, -0.5, x_, ALU.mult, ALU.mult))
                            then(v.scalar_tensor_tensor(y_, t_, 1.5, y_, ALU.add, ALU.mult))
                        for k0, m, kind in kinds:
                            q, o, s = qk[:, k0:k0 + m, :], ra[:, k0:k0 + m, :], rb[:, k0:k0 + m, :]
                            cos_w, sin_w = (rope[:, bass.ds(b, 1), kind, i, :] for i in range(2))
                            v.tensor_tensor(o, q, cos_w.to_broadcast([P, m, D]), ALU.mult)
                            v.tensor_tensor(s[:, :, 0:half], q[:, :, half:D], sin_w[:, :, 0:half].to_broadcast([P, m, half]), ALU.mult)
                            last = v.tensor_tensor(s[:, :, half:D], q[:, :, 0:half], sin_w[:, :, half:D].to_broadcast([P, m, half]), ALU.mult)
                        then(last)
                        o, s = ra[:, h0:h0 + n, :], rb[:, h0:h0 + n, :]
                        then(v.tensor_tensor(o, o, s, ALU.add))
                        v.tensor_tensor(o, o, y_.rearrange("p (h o) -> p h o", o=1).to_broadcast([P, n, D]), ALU.mult).then_inc(s_rope, 1)

                    def mask_max(h):
                        if h >= 2:
                            dve.wait_ge(s_exp, u * HP + h - 1)
                        dve.wait_ge(s_sfull, u * HP + h + 1)
                        v.memset(tick[:, 0:1], 0.0)
                        v.tensor_tensor_reduce(sm[:, h % 2, :], wide[h % 2][:, 0:NK], bias[:, :], 1.0, -3.0e38, ALU.add, ALU.max,
                                               mx[:, h:h + 1]).then_inc(s_sfree, 1)
                        dve.wait_ge(s_sfree, u * HP + h + 1)
                        v.tensor_scalar(nm[:, h:h + 1], mx[:, h:h + 1], -SCALE, None, ALU.mult).then_inc(s_nm, 1)

                    def reciprocal(h):
                        dve.wait_ge(s_exp, u * HP + h + 1)
                        v.reciprocal(rden[:, h:h + 1], den[:, h:h + 1]).then_inc(s_rden, 1)

                    then(v.tensor_scalar(bias[:, :], key_no[:, :], seq_f[:, bass.ds(b, 1)], NEG, ALU.is_ge, ALU.mult))
                    arrive()
                    v.tensor_copy(qk[:, 0:REP, :], bank[1][:, :].rearrange("p (h d) -> p h d", d=D)).then_inc(c_free[1], 1)
                    rotate(0, 0, REP + G, ((0, REP, 0), (REP, G, 1)))
                    arrive()
                    v.tensor_copy(kT[:, 0, 0:L], bank[1][:, :]).then_inc(c_free[1], 1)
                    arrive()
                    v.tensor_copy(qT[:, 0, :], bank[1][:, :]).then_inc(c_free[1], 1)
                    dve.wait_ge(s_p, u * HP)
                    mask_max(0)
                    mask_max(1)
                    reciprocal(0)
                    rotate(1, REP + G, REP, ((REP + G, REP, 0),))
                    for h in range(2, REP):
                        mask_max(h)
                        reciprocal(h - 1)
                    arrive()
                    v.tensor_copy(qT[:, 1, :], bank[1][:, :]).then_inc(c_free[1], 1)
                    for h in range(REP, HP):
                        mask_max(h)
                        reciprocal(h - 1)
                    reciprocal(HP - 1)
                    for g in range(G):
                        for j in range(JT):
                            if (g * JT + j) % 2 == 1:
                                arrive()
                                v.tensor_copy(prT[:, g, j, :], bank[1][:, :]).then_inc(c_free[1], 1)
                    dve.wait_ge(s_y, u + 1)
                    now = x_acc[:, bass.ds(b, 1), :]
                    v.tensor_tensor(now, tail[1][:, :].rearrange("p (o h) -> p o h", o=1), now, ALU.add).then_inc(s_yadd, 1)
                    assert at.n == NSTEP, at.n
                dve.wait_ge(s_v, (pair + 1) * (B * 16 * LT))
                v.tensor_scalar(row_kv[:, :], row_kv[:, :], 1.0, None, ALU.add).then_inc(s_rowskv, 1)


_NAMES = ["x", "itok_B_2_6", "itok_B_1_7", "itok_B_0_23", "itok_Bx16_0_63", "itok_B_207_1644",
          "L0_cond_W_gate", "L0_cond_W_up", "L0_cond_W_down", "L0_cond_A_gate", "L0_cond_B_gate", "L0_cond_A_up",
          "L0_cond_B_up", "L0_cond_A_down", "L0_cond_B_down", "L1_cond_weight", "L1_cond_bias", "L1_cond_lora_a_weights",
          "L1_cond_lora_b_weights", "L1_cond_scaling_factors", "L2_cond_W", "L2_cond_b", "L2_cond_lora_As",
          "L2_cond_lora_Bs", "L3_cond_Wq", "L3_cond_Wk", "L3_cond_Wv", "L3_cond_Wo", "L3_cond_q_norm_w",
          "L3_cond_k_norm_w", "L3_cond_k_cache", "L3_cond_v_cache"]


def kernel(**inputs):
    import concourse.bacc as bacc
    from concourse.bass_utils import run_bass_kernel_spmd

    nc = bacc.Bacc("TRN2", target_bir_lowering=False, num_devices=1)
    arrays = {n: np.ascontiguousarray(inputs[n]) for n in _NAMES}
    arrays["inv_freq"] = (np.float32(1.0) / np.power(np.float32(THETA), np.arange(0, D, 2, dtype=np.float32) / np.float32(D))).astype(np.float32)
    args = {n: nc.dram_tensor(n, v.shape, mybir.dt.from_np(v.dtype), kind="ExternalInput").ap() for n, v in arrays.items()}
    args["out"] = nc.dram_tensor("out", [B, S, H], F32, kind="ExternalOutput").ap()
    build_program(nc, args)
    r = run_bass_kernel_spmd(nc, [arrays], core_ids=[0])
    return r.results[0]["out"]
```

```python
from contextlib import ExitStack

import numpy as np

import concourse.bass as bass
from concourse import mybir

F32 = mybir.dt.float32
I32 = mybir.dt.int32
ALU = mybir.AluOpType
ACT = mybir.ActivationFunctionType
AX = mybir.AxisListType

P = 128
B, S, H = 8, 128, 512
KT = H // P
R = 16
F = 1376
FT = -(-F // P)
FROWS = [min(P, F - P * j) for j in range(FT)]
FSUB = 16
FPART = F // FSUB
OSUB = 4
BLK = 4
NBLK = B // BLK
TB = BLK * S
D, HQ, HK = 128, 32, 8
REP = HQ // HK
PAGES, PSIZE, NPP = 64, 32, 16
L = NPP * PSIZE
LT = L // P
NK = L + S
JT = NK // P
G = 2
NPAIR = HK // G
HP = G * REP
NH = HP + G
SCALE0, SCALE2 = 0.5, 2.0
SCALE = 1.0 / float(np.sqrt(D))
THETA, EPS = 10000.0, 1e-6
NEG = -1e30
TWO_PI = 2.0 * np.pi
FIRST = 1
ROUND = 1.5 * 2.0 ** 23


class Count:

    def __init__(self, sem, base=0):
        self.sem, self.base, self.n = sem, base, 0

    def inc(self, ins):
        self.n += 1
        return ins.then_inc(self.sem, 1)

    def value(self, back=0):
        return self.base + (self.n - back)


def build_program(nc, a):
    x, out = a["x"], a["out"]
    x_scratch = nc.dram_tensor("x3_transposed", [B, P, KT * S], F32).ap()

    ctx = ExitStack()
    with ctx:
        def sem(name):
            return ctx.enter_context(nc.semaphore(name))

        def tensor(scope, name, shape, dt=F32):
            return scope.enter_context(nc.sbuf_tensor(name, shape, dt))

        bank = [ctx.enter_context(nc.psum_tensor(f"bank{i}", [P, 512], F32)) for i in range(2)]
        wide = [ctx.enter_context(nc.psum_tensor(f"wide{i}", [P, 1024], F32)) for i in range(2)]
        tail = [ctx.enter_context(nc.psum_tensor(f"tail{i}", [P, 512], F32)) for i in range(2)]

        ident = tensor(ctx, "ident", [P, P])
        lane = tensor(ctx, "lane", [P, 1], I32)
        lane_f = tensor(ctx, "lane_f", [P, 1])
        lane16 = tensor(ctx, "lane16", [P, 1], I32)
        lane32 = tensor(ctx, "lane32", [P, 1], I32)
        hot16 = tensor(ctx, "hot16", [P, B])
        hot32 = tensor(ctx, "hot32", [P, P // PSIZE])
        mask0 = tensor(ctx, "mask0", [P, B])
        mask1 = tensor(ctx, "mask1", [P, B])
        mask2 = tensor(ctx, "mask2", [P, B])
        adapters = tensor(ctx, "adapters", [P, 3, B], I32)
        seqlens = tensor(ctx, "seqlens", [P, B], I32)
        table = tensor(ctx, "table", [P, B, LT, P // PSIZE], I32)
        picked = tensor(ctx, "picked", [P, B * LT, P // PSIZE])
        own = tensor(ctx, "own", [P, 3, B])
        own1 = tensor(ctx, "own1", [P, 4])
        own_slot = tensor(ctx, "own_slot", [P, 1], I32)
        row_r = tensor(ctx, "row_r", [P, 3], I32)
        row_f = tensor(ctx, "row_f", [P, B], I32)
        row_d = tensor(ctx, "row_d", [P, B], I32)
        row_o = tensor(ctx, "row_o", [P, B], I32)
        row_i = tensor(ctx, "row_i", [P, B, KT], I32)
        row_kv = tensor(ctx, "row_kv", [P, B * LT], I32)
        kv_f = tensor(ctx, "kv_f", [P, B * LT])
        scale1 = tensor(ctx, "scale1", [P, 1])
        prime = tensor(ctx, "prime", [P, 16])
        x_acc = tensor(ctx, "x_acc", [P, B, H])

        s_const = sem("constants_made")
        s_small = sem("small_loaded")
        s_rows = sem("rows_ready")
        s_scale = sem("scale_gathered")
        s_dve = sem("dve_step")

        w012 = ExitStack()
        wgT = tensor(w012, "wgT", [P, KT, F])
        wuT = tensor(w012, "wuT", [P, KT, F])
        wdT = tensor(w012, "wdT", [P, FT, H])
        agT = tensor(w012, "agT", [P, KT, P])
        auT = tensor(w012, "auT", [P, KT, P])
        adT = tensor(w012, "adT", [P, FT, P])
        bgT = tensor(w012, "bgT", [P, F])
        buT = tensor(w012, "buT", [P, F])
        bdT = tensor(w012, "bdT", [P, H])
        w1T = tensor(w012, "w1T", [P, KT, H])
        w2T = tensor(w012, "w2T", [P, KT, H])
        a1T = tensor(w012, "a1T", [P, KT, P])
        a2T = tensor(w012, "a2T", [P, KT, B, R])
        b1T = tensor(w012, "b1T", [P, H])
        b2T = tensor(w012, "b2T", [P, H])
        bias1 = tensor(w012, "bias1", [P, H])
        bias2 = tensor(w012, "bias2", [P, H])

        raw = ExitStack()
        wgu_raw = tensor(raw, "wgu_raw", [P, FT, H])
        wd_raw = tensor(raw, "wd_raw", [P, KT, F])
        w1_raw = x_acc[:, 0:KT, :]
        w2_raw = x_acc[:, KT:2 * KT, :]
        ag_raw = tensor(raw, "ag_raw", [P, H])
        au_raw = tensor(raw, "au_raw", [P, H])
        a1_raw = tensor(raw, "a1_raw", [P, H])
        ad_raw = tensor(raw, "ad_raw", [P, F])
        b_raw = tensor(raw, "b_raw", [P, B, FSUB * R])
        b_perm = tensor(raw, "b_perm", [P, FSUB, B * R])
        raw.close()

        s_wg, s_wu, s_wd, s_w1, s_w2 = (sem(f"{n}_loaded") for n in ("wg", "wu", "wd", "w1", "w2"))
        s_a = sem("a_rows_gathered")
        s_b = sem("b_rows_gathered")
        s_perm = sem("b_rows_in_order")
        p_full = [sem(f"prep_full{i}") for i in range(2)]
        p_free = [sem(f"prep_free{i}") for i in range(2)]

        def w_tiles(w):
            return w.rearrange("(t p) h -> p t h", p=P)

        jobs = []

        def job(wait, pieces, rows, cols, dst):
            jobs.append((wait, pieces, rows, cols, dst))

        def transposed():
            i = len(jobs) - 1
            return p_full[i % 2], i // 2 + 1

        def gate_like(raw_t, wait, dst):
            for j, n in enumerate(FROWS):
                job(wait, [raw_t[0:n, j, k * P:(k + 1) * P] for k in range(KT)], P, n,
                    dst[:, :, j * P:j * P + n])

        b_used = []

        def spread(n, sub, dst):
            for c in range(0, sub, 4):
                job((s_perm, len(b_used) + 1), [b_perm[0:n, c + i, :] for i in range(4)], P, n,
                    dst.rearrange("q (p j) -> q j p", j=sub)[:, c:c + 4, :])
            b_used.append(transposed())

        gate_like(wgu_raw, (s_wg, 32), wgT)
        wg_used = transposed()
        for j, n in enumerate(FROWS):
            job((s_wd, 16), [wd_raw[:, t, j * P:j * P + n] for t in range(KT)], n, P,
                wdT[0:n, j, :].rearrange("p (t c) -> p t c", t=KT))
        job((s_a, 16), [ag_raw[:, k * P:(k + 1) * P] for k in range(KT)], P, P, agT[:, :, :])
        job((s_a, 32), [au_raw[:, k * P:(k + 1) * P] for k in range(KT)], P, P, auT[:, :, :])
        spread(FPART, FSUB, bgT[:, :])
        for j in range(0, FT - 1, 2):
            job((s_a, 48), [ad_raw[:, i * P:(i + 1) * P] for i in range(j, j + 2)], P, P,
                adT[:, j:j + 2, :])
        job((s_a, 48), [ad_raw[:, (FT - 1) * P:F]], FROWS[-1], P, adT[0:FROWS[-1], FT - 1:FT, :])
        gate_like(wgu_raw, (s_wu, 32), wuT)
        for raw_t, wait, dst in ((w1_raw, s_w1, w1T), (w2_raw, s_w2, w2T)):
            for t in range(KT):
                job((wait, 16), [raw_t[:, t, k * P:(k + 1) * P] for k in range(KT)], P, P,
                    dst[:, :, t * P:(t + 1) * P])
        job((s_a, 64), [a1_raw[:, k * P:(k + 1) * P] for k in range(KT)], P, P, a1T[:, :, :])
        spread(FPART, FSUB, buT[:, :])
        spread(P, OSUB, bdT[:, :])
        spread(P, OSUB, b1T[:, :])

        def prep_copies(eng, copy, which):
            n = 0
            for i, (_, pieces, rows, cols, dst) in enumerate(jobs):
                if i % 2 == which:
                    n += 1
                    eng.wait_ge(p_full[which], n)
                    src = bank[which][0:rows, 0:len(pieces) * P].rearrange("p (t c) -> p t c", c=P)
                    copy(dst, src[:, :, 0:cols]).then_inc(p_free[which], 1)

        with nc.Block() as block:
            @block.sync
            def _(sp):
                sp.dma_start(wgu_raw[:, 0:FT - 1, :], w_tiles(a["L0_cond_W_gate"][0:P * (FT - 1), :])).then_inc(s_wg, 16)
                sp.dma_start(wgu_raw[0:FROWS[-1], FT - 1, :], a["L0_cond_W_gate"][P * (FT - 1):F, :]).then_inc(s_wg, 16)
                sp.dma_start(wd_raw[:, :, :], a["L0_cond_W_down"].rearrange("(t p) f -> p t f", p=P)).then_inc(s_wd, 16)
                sp.dma_start(w1_raw, w_tiles(a["L1_cond_weight"])).then_inc(s_w1, 16)
                sp.dma_start(w2_raw, w_tiles(a["L2_cond_W"])).then_inc(s_w2, 16)
                sp.wait_ge(*wg_used)
                sp.dma_start(wgu_raw[:, 0:FT - 1, :], w_tiles(a["L0_cond_W_up"][0:P * (FT - 1), :])).then_inc(s_wu, 16)
                sp.dma_start(wgu_raw[0:FROWS[-1], FT - 1, :], a["L0_cond_W_up"][P * (FT - 1):F, :]).then_inc(s_wu, 16)

            @block.gpsimd
            def _(pool):
                nc.gpsimd.memset(ident[:, :], 0.0).then_inc(s_const, 1)
                nc.gpsimd.memset(hot16[:, :], 1.0).then_inc(s_const, 1)
                nc.gpsimd.memset(hot32[:, :], 1.0).then_inc(s_const, 1)
                nc.gpsimd.iota(lane[:, :], [[0, 1]], base=0, channel_multiplier=1).then_inc(s_const, 1)
                pool.wait_ge(s_const, 4)
                nc.gpsimd.affine_select(ident[:, :], ident[:, :], [[-1, P]], ALU.not_equal, 1.0, base=0,
                                        channel_multiplier=1).then_inc(s_const, 1)
                nc.gpsimd.affine_select(hot16[:, :], hot16[:, :], [[-R, B]], ALU.is_ge, 0.0, base=0,
                                        channel_multiplier=1).then_inc(s_const, 1)
                nc.gpsimd.affine_select(hot32[:, :], hot32[:, :], [[-PSIZE, P // PSIZE]], ALU.is_ge, 0.0, base=0,
                                        channel_multiplier=1).then_inc(s_const, 1)
                pool.wait_ge(s_const, 7)
                nc.gpsimd.affine_select(hot16[:, :], hot16[:, :], [[R, B]], ALU.is_ge, 0.0, base=R - 1,
                                        channel_multiplier=-1).then_inc(s_const, 1)
                nc.gpsimd.affine_select(hot32[:, :], hot32[:, :], [[PSIZE, P // PSIZE]], ALU.is_ge, 0.0, base=PSIZE - 1,
                                        channel_multiplier=-1).then_inc(s_const, 1)

                def gather(dst, rows, src, done):
                    nc.gpsimd.indirect_dma_start(
                        dst, None, src, bass.IndirectOffsetOnAxis(ap=rows, axis=0)).then_inc(done, 16)

                pool.wait_ge(s_rows, 1)
                gather(ag_raw[:, :], row_r[:, 0:1], a["L0_cond_A_gate"].rearrange("l a r h -> (l a r) h"), s_a)
                pool.wait_ge(s_a, 16)
                gather(au_raw[:, :], row_r[:, 0:1], a["L0_cond_A_up"].rearrange("l a r h -> (l a r) h"), s_a)
                pool.wait_ge(s_a, 32)
                gather(ad_raw[:, :], row_r[:, 0:1], a["L0_cond_A_down"].rearrange("l a r h -> (l a r) h"), s_a)
                pool.wait_ge(s_a, 48)
                gather(a1_raw[:, :], row_r[:, 1:2], a["L1_cond_lora_a_weights"].rearrange("a r h -> (a r) h"), s_a)
                gather(scale1[:, :], own_slot[:, :], a["L1_cond_scaling_factors"].rearrange("(a o) -> a o", o=1), s_scale)

                for i, (n, sub, rows, src) in enumerate((
                        (FPART, FSUB, row_f, a["L0_cond_B_gate"].rearrange("l a (p j) r -> (l a p) (j r)", j=FSUB)),
                        (FPART, FSUB, row_f, a["L0_cond_B_up"].rearrange("l a (p j) r -> (l a p) (j r)", j=FSUB)),
                        (P, OSUB, row_d, a["L0_cond_B_down"].rearrange("l a (p j) r -> (l a p) (j r)", j=OSUB)),
                        (P, OSUB, row_o, a["L1_cond_lora_b_weights"].rearrange("a (p j) r -> (a p) (j r)", j=OSUB)))):
                    if i:
                        pool.wait_ge(s_perm, i)
                    for b in range(B):
                        gather(b_raw[0:n, b, 0:sub * R], rows[0:n, b:b + 1], src, s_b)
                    pool.wait_ge(s_b, 16 * B * (i + 1))
                    if i:
                        pool.wait_ge(*b_used[i - 1])
                    nc.gpsimd.tensor_copy(b_perm[0:n, 0:sub, :].rearrange("p j (b r) -> p b j r", r=R),
                                          b_raw[0:n, :, 0:sub * R].rearrange("p b (j r) -> p b j r", r=R)).then_inc(s_perm, 1)
                gather(b2T[:, :], row_r[:, 2:3], a["L2_cond_lora_Bs"].rearrange("a r o -> (a r) o"), s_b)
                for b in range(B):
                    for k in range(KT):
                        gather(a2T[:, k, b, :], row_i[:, b, k:k + 1], a["L2_cond_lora_As"].rearrange("a i r -> (a i) r"), s_b)
                pool.wait_ge(s_b, 16 * (4 * B + 1 + B * KT))

            @block.tensor
            def _(pe):
                pe.wait_ge(s_const, 5)
                for i, (wait, pieces, rows, cols, _) in enumerate(jobs):
                    pe.wait_ge(*wait)
                    if i >= 2:
                        pe.wait_ge(p_free[i % 2], i // 2)
                    for c, piece in enumerate(pieces):
                        k = piece.shape[0]
                        last = nc.tensor.transpose(bank[i % 2][0:rows, c * P:c * P + cols], piece, ident[0:k, 0:k])
                    last.then_inc(p_full[i % 2], 1)

            @block.scalar
            def _(act):
                for i, n in enumerate(("itok_B_2_6", "itok_B_1_7", "itok_B_0_23")):
                    act.dma_start(adapters[:, i, :], a[n].rearrange("(o b) -> o b", o=1).to_broadcast([P, B])).then_inc(s_small, 16)
                act.dma_start(seqlens[:, :], a["itok_B_207_1644"].rearrange("(o b) -> o b", o=1).to_broadcast([P, B])).then_inc(s_small, 16)
                act.dma_start(table[:, :, :, :].rearrange("p b t g -> p (b t g)"),
                              a["itok_Bx16_0_63"].rearrange("(o b) n -> o (b n)", o=1).to_broadcast([P, B * NPP])).then_inc(s_small, 16)
                act.dma_start(bias1[:, :], a["L1_cond_bias"].rearrange("(o h) -> o h", o=1).to_broadcast([P, H])).then_inc(s_small, 16)
                act.dma_start(bias2[:, :], a["L2_cond_b"].rearrange("(o h) -> o h", o=1).to_broadcast([P, H])).then_inc(s_small, 16)
                prep_copies(act, nc.scalar.copy, 0)

            @block.vector
            def _(dve):
                step = Count(s_dve)

                def then(ins):
                    step.inc(ins)
                    dve.wait_ge(s_dve, step.value())

                v = nc.vector
                dve.wait_ge(s_const, 9)
                dve.wait_ge(s_small, 16 * 7)
                v.tensor_copy(lane_f[:, :], lane[:, :])
                v.tensor_scalar(lane16[:, :], lane[:, :], R - 1, None, ALU.bitwise_and)
                v.tensor_scalar(lane32[:, :], lane[:, :], PSIZE - 1, None, ALU.bitwise_and)
                for i in range(3):
                    last = v.tensor_tensor(own[:, i, :], adapters[:, i, :], hot16[:, :], ALU.mult)
                then(last)
                then(v.tensor_reduce(own1[:, 0:3], own[:, :, :], AX.X, ALU.add))
                v.tensor_copy(own_slot[:, :], own1[:, 1:2])
                for i in range(3):
                    v.scalar_tensor_tensor(row_r[:, i:i + 1], own1[:, i:i + 1], float(R), lane16[:, :], ALU.mult, ALU.add)
                v.tensor_scalar(row_f[:, :], adapters[:, 0, :], float(FPART), lane_f[:, 0:1], ALU.mult, ALU.add)
                v.tensor_scalar(row_d[:, :], adapters[:, 0, :], float(P), lane_f[:, 0:1], ALU.mult, ALU.add)
                v.tensor_scalar(row_o[:, :], adapters[:, 1, :], float(P), lane_f[:, 0:1], ALU.mult, ALU.add)
                for k in range(KT):
                    v.tensor_scalar(row_i[:, :, k], adapters[:, 2, :], float(H), float(k * P), ALU.mult, ALU.add)
                for g in range(P // PSIZE):
                    last = v.tensor_scalar(picked[:, :, g], table[:, :, :, g].rearrange("p b t -> p (b t)"),
                                           hot32[:, g:g + 1], None, ALU.mult)
                then(last)
                then(v.tensor_reduce(kv_f[:, :], picked[:, :, :], AX.X, ALU.add))
                v.tensor_scalar(kv_f[:, :], kv_f[:, :], float(PSIZE), None, ALU.mult)
                then(v.tensor_copy(own1[:, 3:4], lane32[:, :]))
                v.tensor_scalar(row_kv[:, :], kv_f[:, :], own1[:, 3:4], float(NPAIR), ALU.add, ALU.mult)
                then(v.tensor_scalar(row_i[:, :, :], row_i[:, :, :], lane_f[:, 0:1], None, ALU.add))
                v.tensor_scalar(mask0[:, :], hot16[:, :], SCALE0, None, ALU.mult)
                v.tensor_scalar(mask2[:, :], hot16[:, :], SCALE2, None, ALU.mult).then_inc(s_rows, 1)
                prep_copies(dve, v.tensor_copy, 1)
                dve.wait_ge(s_scale, 16)
                v.tensor_scalar(mask1[:, :], hot16[:, :], scale1[:, 0:1], None, ALU.mult)

        work = ExitStack()
        xb = tensor(work, "xb", [P, BLK, H])
        xT = tensor(work, "xT", [P, KT, TB])
        xres = tensor(work, "xres", [P, BLK, H])
        actT = tensor(work, "actT", [P, FT, TB])
        silu = tensor(work, "silu", [P, 2, TB])
        tg = tensor(work, "tg", [P, TB])
        tu = tensor(work, "tu", [P, TB])
        td = tensor(work, "td", [P, TB])
        work.close()
        w012.close()

        s_x = sem("x_loaded")
        s_xa = sem("x_acc_written")
        s_xs = sem("xT_stored")
        s_gu = sem("gate_up_full")
        s_si = sem("silu_ready")
        s_act = sem("act_ready")
        s_yf = sem("layer_out_full")
        s_x1 = sem("x_updated")
        s_res = sem("bias_added")
        m_full = [sem(f"xpose_full{i}") for i in range(2)]
        m_free = [sem(f"xpose_free{i}") for i in range(2)]
        NXT = 4
        NA, NB_ = 2 * NXT, 2 * NXT + 5
        NY = 3 * BLK

        def gate_bank(j):
            return wide[j % 2][:, 0:512]

        def up_bank(j):
            return wide[j % 2][:, 512:1024]

        with nc.Block() as block:
            @block.sync
            def _(sp):
                for t in range(NBLK):
                    if t:
                        sp.wait_ge(s_xa, t)
                        sp.wait_ge(s_xs, t * (16 * BLK))
                    sp.dma_start(xb[:, :, :], x[t * BLK:(t + 1) * BLK].rearrange("b p h -> p b h")).then_inc(s_x, 16)
                    sp.wait_ge(m_free[0], (t + 1) * NA + FIRST)
                    sp.wait_ge(m_free[1], (t + 1) * NB_ + FIRST)
                    for i in range(BLK):
                        sp.dma_start(x_scratch[t * BLK + i].rearrange("p (k c) -> p k c", k=KT),
                                     xT[:, :, i * S:(i + 1) * S]).then_inc(s_xs, 16)
                sp.wait_ge(s_xs, 16 * B)

            @block.gpsimd
            def _(pool):
                for i, primed in enumerate((m_free[0], m_free[1], s_act, s_x1)):
                    nc.gpsimd.memset(prime[:, i:i + 1], 0.0).then_inc(primed, FIRST)
                with pool.Fori(0, NBLK) as t:
                    for n, bias in enumerate((bias1, bias2)):
                        pool.wait_ge(s_x1, t * NY + BLK * (n + 1) + FIRST)
                        for i in range(BLK):
                            last = nc.gpsimd.tensor_tensor(xres[:, i, :], xb[:, i, :], bias[:, :], ALU.add)
                        last.then_inc(s_res, 1)
                    pool.wait_ge(s_x1, t * NY + NY + FIRST)
                    nc.gpsimd.tensor_copy(x_acc[:, bass.ds(t * BLK, BLK), :], xb[:, :, :]).then_inc(s_xa, 1)

            @block.tensor
            def _(pe):
                with pe.Fori(0, NBLK) as t:
                    full = [Count(m_full[0], t * NA), Count(m_full[1], t * NB_)]
                    y = Count(s_yf, t * NY)

                    def begin(i):
                        pe.wait_ge(m_free[i], full[i].value() + FIRST)

                    def transpose_x():
                        for k in range(KT):
                            begin(k % 2)
                            for i in range(BLK):
                                last = nc.tensor.transpose(bank[k % 2][:, i * S:(i + 1) * S], xb[:, i, k * P:(k + 1) * P], ident[:, :])
                            full[k % 2].inc(last)
                        begin(0)
                        begin(1)

                    def lora_rows(aT, rhs, rows):
                        begin(1)
                        for k, n in enumerate(rows):
                            last = nc.tensor.matmul(bank[1][:, :], aT(k, n), rhs[0:n, k, :], start=(k == 0), stop=(k == len(rows) - 1))
                        full[1].inc(last)

                    def layer_out(i, lhs, rhs, rows, lora, loraB):
                        pe.wait_ge(s_x1, (y.value(1) if y.n else y.value()) + FIRST)
                        yb = tail[y.n % 2]
                        for k, n in enumerate(rows):
                            nc.tensor.matmul(yb[:, :], lhs[0:n, k, i * S:(i + 1) * S], rhs[0:n, k, :], start=(k == 0), stop=False)
                        y.inc(nc.tensor.matmul(yb[:, :], lora[:, i * S:(i + 1) * S], loraB[:, :], start=False, stop=True))

                    pe.wait_ge(s_x, t * 16 + 16)
                    transpose_x()
                    lora_rows(lambda k, n: agT[:, k, :], xT, [P] * KT)
                    lora_rows(lambda k, n: auT[:, k, :], xT, [P] * KT)
                    begin(1)
                    for j, n in enumerate(FROWS):
                        pe.wait_ge(s_act, t * FT + max(j - 1, 0) + FIRST)
                        for w, tl, bT, dst in ((wgT, tg, bgT, gate_bank(j)), (wuT, tu, buT, up_bank(j))):
                            for k in range(KT):
                                nc.tensor.matmul(dst[0:n, :], w[:, k, j * P:j * P + n], xT[:, k, :], start=(k == 0), stop=False)
                            last = nc.tensor.matmul(dst[0:n, :], bT[:, j * P:j * P + n], tl[:, :], start=False, stop=True)
                        last.then_inc(s_gu, 1)
                    pe.wait_ge(s_act, t * FT + FT + FIRST)
                    lora_rows(lambda k, n: adT[0:n, k, :], actT, FROWS)
                    begin(1)
                    for i in range(BLK):
                        layer_out(i, actT, wdT, FROWS, td, bdT)
                    for n, (aT, w, bT) in enumerate(((a1T, w1T, b1T), (a2T, w2T, b2T))):
                        pe.wait_ge(s_x1, y.value() + FIRST)
                        transpose_x()
                        lora_rows(lambda k, m: aT[:, k].rearrange("p b r -> p (b r)") if aT is a2T else aT[:, k, :], xT, [P] * KT)
                        begin(1)
                        for i in range(BLK):
                            layer_out(i, xT, w, [P] * KT, tg, bT)
                    pe.wait_ge(s_x1, y.value() + FIRST)
                    transpose_x()

            @block.scalar
            def _(act):
                with act.Fori(0, NBLK) as t:
                    full = Count(m_full[0], t * NA)

                    def copy_x():
                        for k in range(0, KT, 2):
                            full.n += 1
                            act.wait_ge(m_full[0], full.value())
                            nc.scalar.copy(xT[:, k, :], bank[0][:, :]).then_inc(m_free[0], 1)

                    copy_x()
                    for j, n in enumerate(FROWS):
                        act.wait_ge(s_gu, t * FT + j + 1)
                        act.wait_ge(s_act, t * FT + max(j - 1, 0) + FIRST)
                        nc.scalar.activation(silu[0:n, j % 2, :], gate_bank(j)[0:n, :], ACT.Silu).then_inc(s_si, 1)
                    for _ in range(NXT - 1):
                        copy_x()

            @block.vector
            def _(dve):
                v = nc.vector
                with dve.Fori(0, NBLK) as t:
                    full = Count(m_full[1], t * NB_)
                    y = Count(s_yf, t * NY)

                    def arrive():
                        full.n += 1
                        dve.wait_ge(m_full[1], full.value())

                    def copy_x():
                        for k in range(1, KT, 2):
                            arrive()
                            v.tensor_copy(xT[:, k, :], bank[1][:, :]).then_inc(m_free[1], 1)

                    def mask_rows(dst, mask):
                        arrive()
                        v.tensor_tensor(dst[:, :].rearrange("p (b c) -> p b c", b=BLK), bank[1][:, :].rearrange("p (b c) -> p b c", b=BLK),
                                        mask[:, bass.ds(t * BLK, BLK)].rearrange("p (b o) -> p b o", o=1).to_broadcast([P, BLK, S]),
                                        ALU.mult).then_inc(m_free[1], 1)

                    def update(i, base):
                        y.n += 1
                        dve.wait_ge(s_yf, y.value())
                        v.tensor_tensor(xb[:, i, :], tail[(y.n - 1) % 2][:, :], base[:, i, :], ALU.add).then_inc(s_x1, 1)

                    copy_x()
                    mask_rows(tg, mask0)
                    mask_rows(tu, mask0)
                    for j, n in enumerate(FROWS):
                        dve.wait_ge(s_si, t * FT + j + 1)
                        v.tensor_tensor(actT[0:n, j, :], silu[0:n, j % 2, :], up_bank(j)[0:n, :], ALU.mult).then_inc(s_act, 1)
                    mask_rows(td, mask0)
                    for i in range(BLK):
                        update(i, xb)
                    for n, mask in enumerate((mask1, mask2)):
                        copy_x()
                        mask_rows(tg, mask)
                        dve.wait_ge(s_res, t * 2 + n + 1)
                        for i in range(BLK):
                            update(i, xres)
                    copy_x()

        build_attention(nc, a, ctx, tensor, sem, bank, wide, tail, ident, lane_f, seqlens, row_kv, prime, x_acc, x_scratch, out)


def build_attention(nc, a, ctx, tensor, sem, bank, wide, tail, ident, lane_f, seqlens, row_kv, prime, x_acc, x_scratch, out):
    QW = HP * D
    wq_raw = tensor(ctx, "wq_raw", [P, HP, H])
    wkv_raw = tensor(ctx, "wkv_raw", [P, 2 * G, H])
    wo_raw = tensor(ctx, "wo_raw", [P, KT, QW])
    wqT = tensor(ctx, "wqT", [P, KT, QW])
    wkvT = tensor(ctx, "wkvT", [P, KT, 2 * G * D])
    woT = tensor(ctx, "woT", [P, HP, H])
    xTb = tensor(ctx, "xTb", [P, KT, S])
    k_raw = tensor(ctx, "k_raw", [P, LT, G * D])
    vt = tensor(ctx, "vt", [P, JT, G * D])
    rows_now = tensor(ctx, "rows_now", [P, LT], I32)
    qk = tensor(ctx, "qk", [P, NH, D])
    ra = tensor(ctx, "ra", [P, NH, D])
    rb = tensor(ctx, "rb", [P, NH, D])
    qT = tensor(ctx, "qT", [P, G, REP * S])
    kT = tensor(ctx, "kT", [P, G, NK])
    sm = tensor(ctx, "sm", [P, 2, NK])
    pr = tensor(ctx, "pr", [P, HP, NK])
    prT = tensor(ctx, "prT", [P, G, JT, REP * S])
    oT = tensor(ctx, "oT", [P, G, REP * S])
    rope = tensor(ctx, "rope", [P, B, 2, 2, D])
    trig = prT[:, 0, 0:4, :].rearrange("p c (b d) -> p c b d", b=B)
    normw = tensor(ctx, "normw", [P, 2, D])
    freq = tensor(ctx, "freq", [P, D // 2])
    pos = tensor(ctx, "pos", [P, B])
    seq_f = tensor(ctx, "seq_f", [P, B])
    key_no = tensor(ctx, "key_no", [P, NK])
    bias = tensor(ctx, "bias", [P, NK])
    ss = tensor(ctx, "ss", [P, NH])
    var = tensor(ctx, "var", [P, NH])
    rs = tensor(ctx, "rs", [P, NH])
    nt = tensor(ctx, "nt", [P, NH])
    mx = tensor(ctx, "mx", [P, HP])
    nm = tensor(ctx, "nm", [P, HP])
    den = tensor(ctx, "den", [P, HP])
    rden = tensor(ctx, "rden", [P, HP])
    tick = tensor(ctx, "tick", [P, 3])

    s_in = sem("norm_weights_loaded")
    s_w = sem("pair_weights_loaded")
    s_xt = sem("xTb_loaded")
    s_k = sem("cached_keys_loaded")
    s_v = sem("cached_values_loaded")
    s_rowsnow = sem("rows_now_ready")
    s_rowskv = sem("pair_rows_ready")
    s_carry = sem("pool_waits_carried")
    s_keyno = sem("key_numbers_made")
    s_trig = sem("angles_ready")
    s_sincos = sem("sines_ready")
    s_step = sem("dve_step3")
    s_kc = sem("new_keys_copied")
    s_sq = sem("squares_ready")
    s_rope = sem("rotated")
    s_sfull = sem("scores_full")
    s_sfree = sem("scores_masked")
    s_nm = sem("negative_max_ready")
    s_exp = sem("exp_done")
    s_rden = sem("denominator_ready")
    s_p = sem("probs_ready")
    s_pv = sem("values_summed")
    s_o = sem("values_copied")
    s_y = sem("out_share_full")
    s_yadd = sem("out_share_added")
    s_out = sem("out_stored")
    t_full = [sem(f"probs_transposed{i}") for i in range(2)]
    t_free = [sem(f"probs_copied{i}") for i in range(2)]
    c_full = [sem(f"chunk_full{i}") for i in range(2)]
    c_free = [sem(f"chunk_free{i}") for i in range(2)]

    WC = (HP + 2 * G + HP) // 2
    FRONT, BACK = (5, 4), (1, 1)
    PAIRC = [WC + B * (FRONT[i] + BACK[i]) for i in range(2)]

    def weight_jobs():
        for t in range(HP):
            yield [wq_raw[:, t, k * P:(k + 1) * P] for k in range(KT)], wqT[:, :, t * P:(t + 1) * P]
        for t in range(2 * G):
            yield [wkv_raw[:, t, k * P:(k + 1) * P] for k in range(KT)], wkvT[:, :, t * P:(t + 1) * P]
        for h in range(HP):
            yield [wo_raw[:, t, h * D:(h + 1) * D] for t in range(KT)], woT[:, h, :].rearrange("p (t c) -> p t c", t=KT)

    k_rows = a["L3_cond_k_cache"].rearrange("a s (e g) d -> (a s e) (g d)", g=G)
    v_rows = a["L3_cond_v_cache"].rearrange("a s (e g) d -> (a s e) (g d)", g=G)

    def unit(pair, b):
        return pair * B + b

    def uses(i, pair, b):
        if isinstance(b, int) and b == 0:
            return pair * PAIRC[i] + WC
        return pair * PAIRC[i] + (b - 1) * (FRONT[i] + BACK[i]) + (WC + FRONT[i])

    def turns(eng, pair, turn):
        turn(pair, 0, True, False)
        with eng.Fori(0, B - 1) as last:
            turn(pair, last + 1, True, True)
        turn(pair, B, False, True)

    with nc.Block() as block:
        @block.sync
        def _(sp):
            sp.dma_start(normw[:, 0, :], a["L3_cond_q_norm_w"].rearrange("(o d) -> o d", o=1).to_broadcast([P, D])).then_inc(s_in, 16)
            sp.dma_start(normw[:, 1, :], a["L3_cond_k_norm_w"].rearrange("(o d) -> o d", o=1).to_broadcast([P, D])).then_inc(s_in, 16)
            sp.dma_start(freq[:, :], a["inv_freq"].rearrange("(o d) -> o d", o=1).to_broadcast([P, D // 2])).then_inc(s_in, 16)
            sp.wait_ge(s_yadd, NPAIR * B + FIRST)
            sp.dma_start(out.rearrange("b p h -> p b h"), x_acc[:, :, :]).then_inc(s_out, 16)
            sp.wait_ge(s_out, 16)

        @block.gpsimd
        def _(pool):
            for i, primed in enumerate((s_rowskv, s_sq, s_pv, s_carry, c_free[0], c_free[1], t_free[0], t_free[1],
                                        s_sfree, s_o, s_yadd, s_rope, s_p)):
                nc.gpsimd.memset(prime[:, i:i + 1], 0.0).then_inc(primed, FIRST)
            nc.gpsimd.memset(prime[:, 15:16], 0.0).then_inc(s_sfull, HP)
            nc.gpsimd.iota(key_no[:, 0:L], [[1, L]], base=0, channel_multiplier=0,
                           allow_small_or_imprecise_dtypes=True).then_inc(s_keyno, 1)
            nc.gpsimd.memset(key_no[:, L:NK], -1.0).then_inc(s_keyno, 1)
            nc.gpsimd.memset(tick[:, 1:3], 0.0).then_inc(s_keyno, 1)
            pool.wait_ge(s_keyno, 3)
            NCARRY = 1 + 3 * B

            def carry(n):
                pool.wait_ge(s_carry, n + FIRST)
                nc.gpsimd.tensor_tensor(tick[:, 2:3], tick[:, 1:2], tick[:, 1:2], ALU.add).then_inc(s_carry, 1)

            with pool.Fori(0, NPAIR) as pair:
                pool.wait_ge(s_sq, pair * (B * G) + FIRST)
                carry(pair * NCARRY)
                nc.gpsimd.dma_start(wq_raw[:, :, :], a["L3_cond_Wq"][bass.ds(pair * QW, QW)].rearrange("(t p) h -> p t h", p=P)).then_inc(s_w, 16)
                nc.gpsimd.dma_start(wkv_raw[:, 0:G, :], a["L3_cond_Wk"][bass.ds(pair * (G * D), G * D)].rearrange("(t p) h -> p t h", p=P)).then_inc(s_w, 16)
                nc.gpsimd.dma_start(wkv_raw[:, G:2 * G, :], a["L3_cond_Wv"][bass.ds(pair * (G * D), G * D)].rearrange("(t p) h -> p t h", p=P)).then_inc(s_w, 16)
                nc.gpsimd.dma_start(wo_raw[:, :, :], a["L3_cond_Wo"][:, bass.ds(pair * QW, QW)].rearrange("(t p) e -> p t e", p=P)).then_inc(s_w, 16)
                with pool.Fori(0, B) as b:
                    u = unit(pair, b)
                    pool.wait_ge(s_sfull, u * HP + 1)
                    carry(pair * NCARRY + b * 3 + 1)
                    nc.gpsimd.dma_start(xTb[:, :, :].rearrange("p k c -> p (k c)"),
                                        x_scratch[bass.ds(b, 1)].rearrange("o p n -> (o p) n")).then_inc(s_xt, 16)
                    pool.wait_ge(s_rowskv, pair + FIRST)
                    nc.gpsimd.tensor_copy(rows_now[:, :], row_kv[:, bass.ds(b * LT, LT)]).then_inc(s_rowsnow, 1)
                    pool.wait_ge(s_rowsnow, u + 1)
                    carry(pair * NCARRY + b * 3 + 2)
                    for t in range(LT):
                        nc.gpsimd.indirect_dma_start(k_raw[:, t, :], None, k_rows,
                                                     bass.IndirectOffsetOnAxis(ap=rows_now[:, t:t + 1], axis=0)).then_inc(s_k, 16)
                    pool.wait_ge(s_pv, u * G + FIRST)
                    carry(pair * NCARRY + b * 3 + 3)
                    for t in range(LT):
                        nc.gpsimd.indirect_dma_start(vt[:, t, :], None, v_rows,
                                                     bass.IndirectOffsetOnAxis(ap=rows_now[:, t:t + 1], axis=0)).then_inc(s_v, 16)
                    pool.wait_ge(s_v, (u + 1) * (16 * LT))

        @block.tensor
        def _(pe):
            def turn(pair, b, front, back):
                n, u = unit(pair, b), unit(pair, b - 1)
                full = [Count(c, uses(i, pair, b)) for i, c in enumerate(c_full)]

                def begin(i):
                    pe.wait_ge(c_free[i], full[i].value() + FIRST)

                def project(i, w, width):
                    begin(i)
                    for k in range(KT):
                        last = nc.tensor.matmul(bank[i][:, 0:width], xTb[:, k, :], w[:, k, :], start=(k == 0), stop=(k == KT - 1))
                    full[i].inc(last)

                def transposes(i, pieces):
                    begin(i)
                    for c, piece in enumerate(pieces):
                        last = nc.tensor.transpose(bank[i][:, c * P:(c + 1) * P], piece, ident[:, :])
                    full[i].inc(last)

                def probs_of(g, j):
                    return [pr[:, g * REP + i, j * P:(j + 1) * P] for i in range(REP)]

                def probs_wide(g, w):
                    pe.wait_ge(s_p, u * HP + (g + 1) * REP + FIRST)
                    pe.wait_ge(t_free[w], u * G + g + FIRST)
                    for c, piece in enumerate(probs_of(g, 2 * w) + probs_of(g, 2 * w + 1)):
                        last = nc.tensor.transpose(wide[w][:, c * P:(c + 1) * P], piece, ident[:, :])
                    last.then_inc(t_full[w], 1)

                def values(g, w):
                    pe.wait_ge(t_free[w], u * G + g + 1 + FIRST)
                    for j in (2 * w, 2 * w + 1):
                        nc.tensor.matmul(tail[g][:, :], vt[:, j, g * D:(g + 1) * D], prT[:, g, j, :], start=(j == 0), stop=False)

                def values_new(g, i):
                    begin(i)
                    j = JT - 1
                    nc.tensor.matmul(tail[g][:, :], vt[:, j, g * D:(g + 1) * D], prT[:, g, j, :], start=False, stop=True).then_inc(s_pv, 1)

                def score(h):
                    if h < 2:
                        pe.wait_ge(t_free[h], n * G + FIRST)
                        pe.wait_ge(s_sfree, n * HP + FIRST)
                    else:
                        pe.wait_ge(s_sfree, n * HP + (h - 1) + FIRST)
                    g, i = h // REP, h % REP
                    q = qT[:, g, i * S:(i + 1) * S]
                    nc.tensor.matmul(wide[h % 2][:, 0:L], q, kT[:, g, 0:L], start=True, stop=True)
                    nc.tensor.matmul(wide[h % 2][:, L:NK], q, kT[:, g, L:NK], start=True, stop=True).then_inc(s_sfull, 1)

                if front:
                    begin(0)
                    begin(1)
                    pe.wait_ge(s_xt, n * 16 + 16)
                    project(0, wkvT[:, :, 0:G * D], G * D)
                    project(1, wqT[:, :, 0:REP * D], REP * D)
                if back:
                    pe.wait_ge(s_sfree, u * HP + HP + FIRST)
                    probs_wide(0, 0)
                    probs_wide(0, 1)
                    transposes(1, probs_of(0, JT - 1))
                if front:
                    project(0, wqT[:, :, REP * D:QW], REP * D)
                if back:
                    pe.wait_ge(s_yadd, u + FIRST)
                    pe.wait_ge(s_v, u * (16 * LT) + 16 * LT)
                    values(0, 0)
                    probs_wide(1, 0)
                    values(0, 1)
                    probs_wide(1, 1)
                    values_new(0, 1)
                    transposes(0, probs_of(1, JT - 1))
                if front:
                    pe.wait_ge(s_k, n * (16 * LT) + 16 * LT)
                    transposes(1, [k_raw[:, t, 0:D] for t in range(LT)])
                if back:
                    pe.wait_ge(s_o, u * G + FIRST)
                    values(1, 0)
                    values(1, 1)
                    values_new(1, 0)
                if front:
                    transposes(0, [k_raw[:, t, D:2 * D] for t in range(LT)])
                    project(0, wkvT[:, :, G * D:2 * G * D], G * D)
                if back:
                    for h in range(HP):
                        if h % REP == 0:
                            pe.wait_ge(s_o, u * G + h // REP + 1 + FIRST)
                        last = nc.tensor.matmul(tail[0][:, :], oT[:, h // REP, (h % REP) * S:(h % REP + 1) * S], woT[:, h, :],
                                                start=(h == 0), stop=(h == HP - 1))
                    last.then_inc(s_y, 1)
                if front:
                    pe.wait_ge(s_rope, n * G + 1 + FIRST)
                    transposes(1, [ra[:, i, :] for i in range(REP)])
                    transposes(0, [ra[:, REP + i, :] for i in range(G)])
                    pe.wait_ge(s_rope, n * G + 2 + FIRST)
                    transposes(1, [ra[:, REP + G + i, :] for i in range(REP)])
                    begin(0)
                    begin(1)
                    for h in range(HP):
                        score(h)

            with pe.Fori(0, NPAIR) as pair:
                full = [Count(c, pair * PAIRC[i]) for i, c in enumerate(c_full)]
                pe.wait_ge(s_w, pair * 64 + 64)
                for i, (pieces, _) in enumerate(weight_jobs()):
                    pe.wait_ge(c_free[i % 2], full[i % 2].value() + FIRST)
                    for c, piece in enumerate(pieces):
                        last = nc.tensor.transpose(bank[i % 2][:, c * P:(c + 1) * P], piece, ident[:, :])
                    full[i % 2].inc(last)
                turns(pe, pair, turn)

        @block.scalar
        def _(act):
            ac = nc.scalar
            act.wait_ge(s_trig, 1)
            for i in range(2):
                last = ac.activation(trig[:, 2 + i, :, :], trig[:, i, :, :], ACT.Sin)
            last.then_inc(s_sincos, 1)

            def turn(pair, b, front, back):
                n, u = unit(pair, b), unit(pair, b - 1)
                full0 = Count(c_full[0], uses(0, pair, b))

                def arrive():
                    full0.n += 1
                    act.wait_ge(c_full[0], full0.value())

                def squares(h0, m):
                    for h in range(h0, h0 + m):
                        last = ac.activation(ra[:, h, :], qk[:, h, :], ACT.Square, accum_out=ss[:, h:h + 1])
                    last.then_inc(s_sq, 1)

                def copy_probs(g):
                    act.wait_ge(t_full[0], u * G + g + 1)
                    ac.copy(prT[:, g, 0:2, :], wide[0][:, :].rearrange("p (j c) -> p j c", j=2)).then_inc(t_free[0], 1)

                def copy_values(g):
                    act.wait_ge(s_pv, u * G + g + 1 + FIRST)
                    ac.copy(oT[:, g, :], tail[g][:, :]).then_inc(s_o, 1)

                def exponential(h):
                    act.wait_ge(s_nm, n * HP + h + 1)
                    if h % REP == 0:
                        act.wait_ge(s_pv, n * G + FIRST)
                    ac.activation(pr[:, h, :], sm[:, h % 2, :], ACT.Exp, bias=nm[:, h:h + 1], scale=SCALE,
                                  accum_out=den[:, h:h + 1]).then_inc(s_exp, 1)

                def normalise(h):
                    act.wait_ge(s_rden, n * HP + h + 1)
                    ac.activation(pr[:, h, :], pr[:, h, :], ACT.Copy, scale=rden[:, h:h + 1]).then_inc(s_p, 1)

                if front:
                    arrive()
                    act.wait_ge(s_rope, n * G + FIRST)
                    ac.copy(qk[:, REP:REP + G, :], bank[0][:, 0:G * D].rearrange("p (h d) -> p h d", d=D)).then_inc(c_free[0], 1)
                if back:
                    copy_probs(0)
                if front:
                    act.wait_ge(c_free[0], full0.value() + FIRST)
                    act.wait_ge(c_free[1], uses(1, pair, b) + 1 + FIRST)
                    squares(0, REP + G)
                    arrive()
                    ac.copy(qk[:, REP + G:NH, :], bank[0][:, :].rearrange("p (h d) -> p h d", d=D)).then_inc(c_free[0], 1)
                    act.wait_ge(c_free[0], full0.value() + FIRST)
                    squares(REP + G, REP)
                if back:
                    copy_probs(1)
                    copy_values(0)
                    arrive()
                    ac.copy(prT[:, 1, JT - 1, :], bank[0][:, :]).then_inc(c_free[0], 1)
                    copy_values(1)
                if front:
                    arrive()
                    ac.copy(kT[:, 1, 0:L], bank[0][:, :]).then_inc(c_free[0], 1)
                    arrive()
                    ac.copy(vt[:, LT, :], bank[0][:, 0:G * D]).then_inc(c_free[0], 1)
                    arrive()
                    ac.copy(kT[:, :, L:NK], bank[0][:, 0:G * S].rearrange("p (g c) -> p g c", g=G)).then_inc(c_free[0], 1)
                    for h in range(HP):
                        exponential(h)
                        if h:
                            normalise(h - 1)
                    normalise(HP - 1)

            with act.Fori(0, NPAIR) as pair:
                full = Count(c_full[0], pair * PAIRC[0])
                for i, (_, dst) in enumerate(weight_jobs()):
                    if i % 2 == 0:
                        full.n += 1
                        act.wait_ge(c_full[0], full.value())
                        ac.copy(dst, bank[0][:, :].rearrange("p (t c) -> p t c", t=KT)).then_inc(c_free[0], 1)
                turns(act, pair, turn)

        @block.vector
        def _(dve):
            v = nc.vector
            step = Count(s_step)

            def then(ins):
                step.inc(ins)
                dve.wait_ge(s_step, step.value())

            dve.wait_ge(s_in, 48)
            v.tensor_copy(seq_f[:, :], seqlens[:, :])
            then(v.tensor_scalar(pos[:, :], seqlens[:, :], lane_f[:, 0:1], None, ALU.add))
            angle, turned = trig[:, 2, :, :], trig[:, 3, :, :]
            for b in range(B):
                last = v.tensor_scalar(angle[:, b, :], freq[:, :], pos[:, b:b + 1], None, ALU.mult)
            then(last)
            c1 = np.float32(6.28125)
            c2 = np.float32(np.floor((TWO_PI - float(c1)) * 2.0 ** 21) / 2.0 ** 21)
            c3 = np.float32(TWO_PI - float(c1) - float(c2))
            for i, quarter in ((0, 0.0), (1, 0.25)):
                red = trig[:, i, :, :]
                then(v.tensor_scalar(turned, angle, 1.0 / TWO_PI, quarter, ALU.mult, ALU.add))
                then(v.tensor_scalar(turned, turned, ROUND, ROUND, ALU.add, ALU.subtract))
                then(v.scalar_tensor_tensor(red, turned, -float(c1), angle, ALU.mult, ALU.add))
                then(v.scalar_tensor_tensor(red, turned, -float(c2), red, ALU.mult, ALU.add))
                then(v.scalar_tensor_tensor(red, turned, -float(c3), red, ALU.mult, ALU.add))
                then(v.tensor_scalar(red, red, quarter * TWO_PI, 3.1415925, ALU.add, ALU.min))
                then(v.tensor_scalar(red, red, -3.1415925, None, ALU.max))
            v.tensor_scalar(turned[:, 0, 0:1], pos[:, 0:1], 0.0, None, ALU.mult).then_inc(s_trig, 1)
            dve.wait_ge(s_sincos, 1)
            half = D // 2
            sin, cos = trig[:, 2, :, :], trig[:, 3, :, :]
            for i in range(2):
                w1 = normw[:, i:i + 1, 0:half].to_broadcast([P, B, half])
                w2 = normw[:, i:i + 1, half:D].to_broadcast([P, B, half])
                v.tensor_tensor(rope[:, :, i, 0, 0:half], cos, w1, ALU.mult)
                v.tensor_tensor(rope[:, :, i, 0, half:D], cos, w2, ALU.mult)
                v.scalar_tensor_tensor(rope[:, :, i, 1, 0:half], sin, -1.0, w2, ALU.mult, ALU.mult)
                last = v.tensor_tensor(rope[:, :, i, 1, half:D], sin, w1, ALU.mult)
            then(last)
            dve.wait_ge(s_keyno, 2)
            first_steps = step.n
            NSTEP = 33

            def turn(pair, b, front, back):
                n, u = unit(pair, b), unit(pair, b - 1)
                full1 = Count(c_full[1], uses(1, pair, b))
                at = Count(s_step, n * NSTEP + first_steps)

                def then(ins):
                    at.inc(ins)
                    dve.wait_ge(s_step, at.value())

                def arrive():
                    full1.n += 1
                    dve.wait_ge(c_full[1], full1.value())

                def rotate(part, h0, m0, kinds):
                    dve.wait_ge(s_sq, n * G + part + 1 + FIRST)
                    x_, y_, t_ = var[:, h0:h0 + m0], rs[:, h0:h0 + m0], nt[:, h0:h0 + m0]
                    then(v.tensor_scalar(x_, ss[:, h0:h0 + m0], 1.0 / D, EPS, ALU.mult, ALU.add))
                    then(v.tensor_scalar(y_.bitcast(I32), x_.bitcast(I32), -0.5, float(0x5F3759DF), ALU.mult, ALU.add))
                    for _ in range(4):
                        then(v.tensor_tensor(t_, y_, y_, ALU.mult))
                        then(v.scalar_tensor_tensor(t_, t_, -0.5, x_, ALU.mult, ALU.mult))
                        then(v.scalar_tensor_tensor(y_, t_, 1.5, y_, ALU.add, ALU.mult))
                    for k0, m, kind in kinds:
                        q, o, s = qk[:, k0:k0 + m, :], ra[:, k0:k0 + m, :], rb[:, k0:k0 + m, :]
                        cos_w, sin_w = (rope[:, bass.ds(b, 1), kind, i, :] for i in range(2))
                        v.tensor_tensor(o, q, cos_w.to_broadcast([P, m, D]), ALU.mult)
                        v.tensor_tensor(s[:, :, 0:half], q[:, :, half:D], sin_w[:, :, 0:half].to_broadcast([P, m, half]), ALU.mult)
                        last = v.tensor_tensor(s[:, :, half:D], q[:, :, 0:half], sin_w[:, :, half:D].to_broadcast([P, m, half]), ALU.mult)
                    then(last)
                    o, s = ra[:, h0:h0 + m0, :], rb[:, h0:h0 + m0, :]
                    then(v.tensor_tensor(o, o, s, ALU.add))
                    v.tensor_tensor(o, o, y_.rearrange("p (h o) -> p h o", o=1).to_broadcast([P, m0, D]), ALU.mult).then_inc(s_rope, 1)

                def copy_probs(g):
                    dve.wait_ge(t_full[1], u * G + g + 1)
                    v.tensor_copy(prT[:, g, 2:4, :], wide[1][:, :].rearrange("p (j c) -> p j c", j=2)).then_inc(t_free[1], 1)

                def mask_max(h):
                    if h >= 2:
                        dve.wait_ge(s_exp, n * HP + h - 1)
                    dve.wait_ge(s_sfull, n * HP + h + 1 + HP)
                    v.memset(tick[:, 0:1], 0.0)
                    v.tensor_tensor_reduce(sm[:, h % 2, :], wide[h % 2][:, 0:NK], bias[:, :], 1.0, -3.0e38, ALU.add, ALU.max,
                                           mx[:, h:h + 1]).then_inc(s_sfree, 1)
                    dve.wait_ge(s_sfree, n * HP + h + 1 + FIRST)
                    v.tensor_scalar(nm[:, h:h + 1], mx[:, h:h + 1], -SCALE, None, ALU.mult).then_inc(s_nm, 1)

                def reciprocal(h):
                    dve.wait_ge(s_exp, n * HP + h + 1)
                    v.reciprocal(rden[:, h:h + 1], den[:, h:h + 1]).then_inc(s_rden, 1)

                if front:
                    then(v.tensor_scalar(bias[:, :], key_no[:, :], seq_f[:, bass.ds(b, 1)], NEG, ALU.is_ge, ALU.mult))
                    arrive()
                    v.tensor_copy(qk[:, 0:REP, :], bank[1][:, :].rearrange("p (h d) -> p h d", d=D)).then_inc(c_free[1], 1)
                if back:
                    copy_probs(0)
                    arrive()
                    v.tensor_copy(prT[:, 0, JT - 1, :], bank[1][:, :]).then_inc(c_free[1], 1)
                if front:
                    rotate(0, 0, REP + G, ((0, REP, 0), (REP, G, 1)))
                if back:
                    copy_probs(1)
                if front:
                    arrive()
                    v.tensor_copy(kT[:, 0, 0:L], bank[1][:, :]).then_inc(c_free[1], 1)
                    rotate(1, REP + G, REP, ((REP + G, REP, 0),))
                if back:
                    dve.wait_ge(s_y, u + 1)
                    now = x_acc[:, bass.ds(b - 1, 1), :]
                    v.tensor_tensor(now, tail[0][:, :].rearrange("p (o h) -> p o h", o=1), now, ALU.add).then_inc(s_yadd, 1)
                if front:
                    for g in range(G):
                        arrive()
                        v.tensor_copy(qT[:, g, :], bank[1][:, :]).then_inc(c_free[1], 1)
                    dve.wait_ge(s_p, n * HP + FIRST)
                    for h in range(HP):
                        mask_max(h)
                        if h:
                            reciprocal(h - 1)
                    reciprocal(HP - 1)
                    assert at.n == NSTEP, at.n

            with dve.Fori(0, NPAIR) as pair:
                full = Count(c_full[1], pair * PAIRC[1])
                for i, (_, dst) in enumerate(weight_jobs()):
                    if i % 2 == 1:
                        full.n += 1
                        dve.wait_ge(c_full[1], full.value())
                        v.tensor_copy(dst, bank[1][:, :].rearrange("p (t c) -> p t c", t=KT)).then_inc(c_free[1], 1)
                turns(dve, pair, turn)
                dve.wait_ge(s_v, (pair + 1) * (B * 16 * LT))
                v.tensor_scalar(row_kv[:, :], row_kv[:, :], 1.0, None, ALU.add).then_inc(s_rowskv, 1)


_NAMES = ["x", "itok_B_2_6", "itok_B_1_7", "itok_B_0_23", "itok_Bx16_0_63", "itok_B_207_1644",
          "L0_cond_W_gate", "L0_cond_W_up", "L0_cond_W_down", "L0_cond_A_gate", "L0_cond_B_gate", "L0_cond_A_up",
          "L0_cond_B_up", "L0_cond_A_down", "L0_cond_B_down", "L1_cond_weight", "L1_cond_bias", "L1_cond_lora_a_weights",
          "L1_cond_lora_b_weights", "L1_cond_scaling_factors", "L2_cond_W", "L2_cond_b", "L2_cond_lora_As",
          "L2_cond_lora_Bs", "L3_cond_Wq", "L3_cond_Wk", "L3_cond_Wv", "L3_cond_Wo", "L3_cond_q_norm_w",
          "L3_cond_k_norm_w", "L3_cond_k_cache", "L3_cond_v_cache"]


def kernel(**inputs):
    import concourse.bacc as bacc
    from concourse.bass_utils import run_bass_kernel_spmd

    nc = bacc.Bacc("TRN2", target_bir_lowering=False, num_devices=1)
    arrays = {n: np.ascontiguousarray(inputs[n]) for n in _NAMES}
    arrays["inv_freq"] = (np.float32(1.0) / np.power(np.float32(THETA), np.arange(0, D, 2, dtype=np.float32) / np.float32(D))).astype(np.float32)
    args = {n: nc.dram_tensor(n, v.shape, mybir.dt.from_np(v.dtype), kind="ExternalInput").ap() for n, v in arrays.items()}
    args["out"] = nc.dram_tensor("out", [B, S, H], F32, kind="ExternalOutput").ap()
    build_program(nc, args)
    r = run_bass_kernel_spmd(nc, [arrays], core_ids=[0])
    return r.results[0]["out"]
```

```python
from contextlib import ExitStack

import numpy as np

import concourse.bass as bass
from concourse import mybir

F32 = mybir.dt.float32
F32R = mybir.dt.float32r
I32 = mybir.dt.int32
ALU = mybir.AluOpType
ACT = mybir.ActivationFunctionType
AX = mybir.AxisListType

P = 128
B, S, H = 8, 128, 512
KT = H // P
R = 16
F = 1376
FT = -(-F // P)
FROWS = [min(P, F - P * j) for j in range(FT)]
FSUB = 16
FPART = F // FSUB
OSUB = 4
BLK = 4
NT = B * S
TB = BLK * S
D, HQ, HK = 128, 32, 8
REP = HQ // HK
PAGES, PSIZE, NPP = 64, 32, 16
L = NPP * PSIZE
LT = L // P
NK = L + S
JT = NK // P
G = 2
NPAIR = HK // G
HP = G * REP
NH = HP + G
SCALE0, SCALE2 = 0.5, 2.0
SCALE = 1.0 / float(np.sqrt(D))
THETA, EPS = 10000.0, 1e-6
NEG = -1e30
TWO_PI = 2.0 * np.pi
FIRST = 1
ROUND = 1.5 * 2.0 ** 23


class Count:

    def __init__(self, sem, base=0):
        self.sem, self.base, self.n = sem, base, 0

    def inc(self, ins):
        self.n += 1
        return ins.then_inc(self.sem, 1)

    def value(self, back=0):
        return self.base + (self.n - back)


def build_program(nc, a):
    x, out = a["x"], a["out"]
    x_scratch = nc.dram_tensor("x3_transposed", [B, P, 2 * KT * S], F32).ap()
    rope_scratch = nc.dram_tensor("rope_tables", [B, P, 4 * D], F32).ap()

    ctx = ExitStack()
    with ctx:
        def sem(name):
            return ctx.enter_context(nc.semaphore(name))

        def tensor(scope, name, shape, dt=F32):
            return scope.enter_context(nc.sbuf_tensor(name, shape, dt))

        bank = [ctx.enter_context(nc.psum_tensor(f"bank{i}", [P, 512], F32)) for i in range(2)]
        wide = [ctx.enter_context(nc.psum_tensor(f"wide{i}", [P, 1024], F32)) for i in range(2)]
        tail = [ctx.enter_context(nc.psum_tensor(f"tail{i}", [P, 512], F32)) for i in range(2)]

        ident = tensor(ctx, "ident", [P, P])
        lane = tensor(ctx, "lane", [P, 1], I32)
        lane_f = tensor(ctx, "lane_f", [P, 1])
        lane16 = tensor(ctx, "lane16", [P, 1], I32)
        lane32 = tensor(ctx, "lane32", [P, 1], I32)
        hot16 = tensor(ctx, "hot16", [P, B])
        hot32 = tensor(ctx, "hot32", [P, P // PSIZE])
        mask0 = tensor(ctx, "mask0", [P, B])
        mask1 = tensor(ctx, "mask1", [P, B])
        mask2 = tensor(ctx, "mask2", [P, B])
        adapters = tensor(ctx, "adapters", [P, 3, B], I32)
        seqlens = tensor(ctx, "seqlens", [P, B], I32)
        table = tensor(ctx, "table", [P, B, LT, P // PSIZE], I32)
        picked = tensor(ctx, "picked", [P, B * LT, P // PSIZE])
        own = tensor(ctx, "own", [P, 3, B])
        own1 = tensor(ctx, "own1", [P, 4])
        own_slot = tensor(ctx, "own_slot", [P, 1], I32)
        row_r = tensor(ctx, "row_r", [P, 3], I32)
        row_f = tensor(ctx, "row_f", [P, B], I32)
        row_d = tensor(ctx, "row_d", [P, B], I32)
        row_o = tensor(ctx, "row_o", [P, B], I32)
        row_i = tensor(ctx, "row_i", [P, B, KT], I32)
        row_kv = tensor(ctx, "row_kv", [P, B * LT], I32)
        kv_f = tensor(ctx, "kv_f", [P, B * LT])
        scale1 = tensor(ctx, "scale1", [P, 1])
        prime = tensor(ctx, "prime", [P, 16])
        seq_f = tensor(ctx, "seq_f", [P, B])
        arena = tensor(ctx, "arena", [P, FT * NT])

        s_const = sem("constants_made")
        s_small = sem("small_loaded")
        s_rows = sem("rows_ready")
        s_scale = sem("scale_gathered")
        s_dve = sem("dve_step")

        w012 = ExitStack()
        xT = tensor(w012, "xT", [P, KT, NT])
        xh = tensor(w012, "xh", [P, 2, KT, NT], F32R)
        act = arena[:, :].rearrange("p (j n) -> p j n", j=FT)
        tg = tensor(w012, "tg", [P, NT])
        tu = tensor(w012, "tu", [P, NT])
        agT = tensor(w012, "agT", [P, KT, P])
        auT = tensor(w012, "auT", [P, KT, P])
        adT = tensor(w012, "adT", [P, FT, P])
        bgT = tensor(w012, "bgT", [P, F])
        buT = tensor(w012, "buT", [P, F])
        bdT = tensor(w012, "bdT", [P, H])
        a1T = tensor(w012, "a1T", [P, KT, P])
        a2T = tensor(w012, "a2T", [P, KT, B, R])
        b1T = tensor(w012, "b1T", [P, H])
        b2T = tensor(w012, "b2T", [P, H])
        x_tok = tensor(w012, "x_tokens", [P, B, H])
        normw = tensor(w012, "normw", [P, 2, D])
        freq = tensor(w012, "freq", [P, D // 2])
        pos = tensor(w012, "pos", [P, B])
        bias1 = tensor(w012, "bias1", [P, KT])
        bias2 = tensor(w012, "bias2", [P, KT])
        w_raw = tensor(w012, "w_raw012", [P, 2, 2, H])
        wT = tensor(w012, "wT", [P, 2, 2, 2, KT, P], F32R)
        b_ring = tensor(w012, "b_ring", [P, 2, 2, 2, P], F32R)
        silu = tensor(w012, "silu", [P, 2, TB])
        wd_raw = tensor(w012, "wd_raw", [P, 2, KT, P])
        down_ring = tensor(w012, "down_ring", [P, 2, 2, 2, TB], F32R)
        wdT, act_hl = down_ring[:, 0], down_ring[:, 1]
        ad_ring = tensor(w012, "ad_ring", [P, 2, 2, P], F32R)
        w012.close()

        def flat(t, names):
            return t.rearrange(f"p {names} -> p ({names})")

        w12_raw = flat(w_raw[:, :, :, :], "s w h").rearrange("p (t h) -> p t h", t=KT)
        w1T = flat(wT[:, :, :, :, :, :], "s w i k c").rearrange("p (i k o) -> p i k o", i=2, k=KT)
        w2T = flat(down_ring[:, :, :, :, :], "t s i n").rearrange("p (i k o) -> p i k o", i=2, k=KT)
        tg_hl, tu_hl = (flat(down_ring[:, t], "s i n").rearrange("p (i n) -> p i n", i=2) for t in range(2))
        early = arena[:, :]
        NB = FSUB * B * R
        ag_raw, au_raw = early[:, 0:H], early[:, H:2 * H]
        bgu_raw = [early[:, 2 * H + i * NB:2 * H + (i + 1) * NB].rearrange("p (b c) -> p b c", b=B) for i in range(2)]
        bgu_perm = [early[:, 2 * H + (2 + i) * NB:2 * H + (3 + i) * NB].rearrange("p (j c) -> p j c", j=FSUB) for i in range(2)]
        late = x_tok[:, :, :].rearrange("p b h -> p (b h)")
        NO = OSUB * B * R
        ad_raw, a1_raw = late[:, 0:F], late[:, F:F + H]
        bo_raw = [late[:, F + H + i * NO:F + H + (i + 1) * NO].rearrange("p (b c) -> p b c", b=B) for i in range(2)]
        bo_perm = [late[:, F + H + (2 + i) * NO:F + H + (3 + i) * NO].rearrange("p (j c) -> p j c", j=OSUB) for i in range(2)]

        w_raw3 = arena[:, 0:HP * H].rearrange("p (t h) -> p t h", t=HP)
        wkv_raw = arena[:, HP * H:(HP + 2 * G) * H].rearrange("p (t h) -> p t h", t=2 * G)
        pr_flat = arena[:, (HP + 2 * G) * H:(HP + 2 * G) * H + HP * NK]
        pr = pr_flat.rearrange("p (h k) -> p h k", h=HP)
        rope_all = pr_flat[:, 0:B * 4 * D].rearrange("p (b i j d) -> p b i j d", b=B, i=2, j=2)
        trig_in = silu[:, :, :].rearrange("p g (b d) -> p g b d", b=B)
        trig_out = flat(wd_raw[:, :, :, :], "s t c").rearrange("p (g b d) -> p g b d", g=2, b=B)

        s_in = sem("norm_weights_loaded")
        s_w = sem("pair_weights_loaded")
        s_trig = sem("angles_ready")
        s_sincos = sem("sines_ready")
        s_ropemade = sem("rope_tables_made")
        s_ropest = sem("rope_tables_stored")
        s_init = sem("out_started")
        s_x = [sem(f"x_half{i}_loaded") for i in range(2)]
        s_wr = [sem(f"gate_up_tile_loaded{i}") for i in range(2)]
        s_wdr = [sem(f"down_tile_loaded{i}") for i in range(2)]
        s_w12 = [sem(f"w{i}_loaded") for i in (1, 2)]
        s_ag, s_au, s_ad, s_a1 = (sem(f"{n}_rows_gathered") for n in ("ag", "au", "ad", "a1"))
        s_bgu = [sem(f"b_{n}_rows_gathered") for n in ("gate", "up")]
        s_bo = [sem(f"b_{n}_rows_gathered") for n in ("down", "1")]
        s_bias = sem("biases_loaded")
        s_perm = sem("b_gate_up_rows_in_order")
        s_permo = sem("b_rows_in_order")
        s_l2 = sem("layer2_adapters_gathered")
        s_xlo = sem("x_low_part_ready")
        s_tf = sem("lora_rows_full")
        s_mask = sem("lora_rows_masked")
        s_thi = sem("masked_rows_high_part_ready")
        s_tlo = sem("masked_rows_low_part_ready")
        s_ring = sem("b_columns_high_part_ready")
        s_ringlo = sem("b_columns_low_part_ready")
        s_hi = sem("weights_high_part_ready012")
        s_gu = sem("gate_up_full")
        s_si = sem("silu_ready")
        s_act = sem("act_ready")
        s_ah = sem("act_high_part_ready")
        s_al = sem("act_low_part_ready")
        s_d = sem("down_tile_used")
        s_grp = sem("layer_out_full")
        s_x1 = sem("x_updated")
        s_xh = sem("x_updated_high_part")
        s_xl = sem("x_updated_low_part")
        s_xs = sem("x_stored")
        m_full = [sem(f"bank_full{i}") for i in range(2)]
        m_free = [sem(f"bank_free{i}") for i in range(2)]
        NLOOP = (FT - 5) // 2

        class Uses:

            def __init__(self):
                self.n, self.loop = [0, 0, 0], [0, 0, 0]

            def value(self, i):
                return self.loop[i] + self.n[i]

            def take(self, i):
                self.n[i] += 1
                return self.value(i)

        def in_steps(eng, uses, step, prepare, use, between=None, first=None):
            prepare(0, 0)
            prepare(1, 1)
            if first:
                first()
            use(0, 0)
            with eng.Fori(0, NLOOP) as i:
                uses.loop = [i * n for n in step]
                for s in range(2):
                    prepare(i * 2 + (s + 2), s)
                    use(i * 2 + (s + 1), 1 - s)
            uses.loop = [0, 0, 0]
            uses.n = [n + (NLOOP - 1) * m for n, m in zip(uses.n, step)]
            if between:
                between()
            for j in range(2 * NLOOP + 1, FT):
                if j + 1 < FT:
                    prepare(j + 1, (j + 1) % 2)
                use(j, j % 2)

        GATE_STEP, DOWN_STEP = (2, 2, 4), (1, 1, 2)

        def rows(j):
            return FROWS[j] if isinstance(j, int) else P

        def tile(t, j):
            return t[:, j] if isinstance(j, int) else t[:, bass.ds(j, 1)].rearrange("p o n -> p (o n)")

        def half(c):
            return slice(c * TB, (c + 1) * TB)

        def quarter(i):
            return wide[i // 2][:, (i % 2) * TB:(i % 2 + 1) * TB]

        def spread(wait, perm, n, sub, dst):
            return [(wait, [perm[0:n, c + i, :] for i in range(4)], P, n,
                     dst.rearrange("q (p j) -> q j p", j=sub)[:, c:c + 4, :]) for c in range(0, sub, 4)]

        early_jobs = [((s_ag, 16), [ag_raw[:, k * P:(k + 1) * P] for k in range(KT)], P, P, agT[:, :, :]),
                      ((s_au, 16), [au_raw[:, k * P:(k + 1) * P] for k in range(KT)], P, P, auT[:, :, :])]
        gate_up_jobs = [j for i, t in enumerate((bgT, buT)) for j in spread((s_perm, i + 1), bgu_perm[i], FPART, FSUB, t[:, :])]
        late_jobs = [((s_ad, 16), [ad_raw[:, i * P:(i + 1) * P] for i in range(j, j + 2)], P, P, adT[:, j:j + 2, :])
                     for j in range(0, FT - 1, 2)]
        late_jobs.append(((s_ad, 16), [ad_raw[:, (FT - 1) * P:F]], FROWS[-1], P, adT[0:FROWS[-1], FT - 1:FT, :]))
        late_jobs.append(((s_a1, 16), [a1_raw[:, k * P:(k + 1) * P] for k in range(KT)], P, P, a1T[:, :, :]))
        for i, t in enumerate((bdT, b1T)):
            late_jobs += spread((s_permo, i + 1), bo_perm[i], P, OSUB, t[:, :])

        def copy_jobs(eng, copy, which, uses, jobs):
            for i, (_, pieces, n, cols, dst) in enumerate(jobs):
                v = uses.take(i % 2)
                if i % 2 == which:
                    eng.wait_ge(m_full[which], v)
                    src = bank[which][0:n, 0:len(pieces) * P].rearrange("p (t c) -> p t c", c=P)
                    copy(dst, src[:, :, 0:cols]).then_inc(m_free[which], 1)

        def w12_dst(w, t):
            return w[:, :, :, t * P:(t + 1) * P]

        def gate_tile(name, j):
            return a[name][j * P:j * P + rows(j), :] if isinstance(j, int) else a[name][bass.ds(j * P, P), :]

        def down_tile(j):
            w = a["L0_cond_W_down"]
            return (w[:, j * P:j * P + rows(j)] if isinstance(j, int) else w[:, bass.ds(j * P, P)]).rearrange("(t p) f -> p t f", p=P)

        def load_gate_up(eng, j, buf):
            n = rows(j)
            for w, name in enumerate(("L0_cond_W_gate", "L0_cond_W_up")):
                eng.dma_start(w_raw[0:n, buf, w, :], gate_tile(name, j)).then_inc(s_wr[buf], 16)

        def back_uses(i):
            n = i % 2
            jobs = early_jobs, gate_up_jobs, late_jobs
            return (2 * KT // 2 + sum(len(j[n::2]) for j in jobs) + FT + 2 * len(range(n, FT, 2)) + 2 * (KT // 2) + i // 2 + 1)

        def load_down(eng, j, buf):
            eng.dma_start(wd_raw[:, buf, :, 0:rows(j)], down_tile(j)).then_inc(s_wdr[buf], 16)

        with nc.Block() as block:
            @block.sync
            def _(sp):
                sp.wait_ge(s_small, 16 * 5)
                for c in range(2):
                    sp.dma_start(x_tok[:, c * BLK:(c + 1) * BLK, :], x[c * BLK:(c + 1) * BLK].rearrange("b p h -> p b h")).then_inc(s_x[c], 16)
                for j in range(2):
                    load_gate_up(sp, j, j)
                for j in range(2):
                    load_down(sp, j, j)
                sp.dma_start(normw[:, 0, :], a["L3_cond_q_norm_w"].rearrange("(o d) -> o d", o=1).to_broadcast([P, D])).then_inc(s_in, 16)
                sp.dma_start(normw[:, 1, :], a["L3_cond_k_norm_w"].rearrange("(o d) -> o d", o=1).to_broadcast([P, D])).then_inc(s_in, 16)
                sp.dma_start(freq[:, :], a["inv_freq"].rearrange("(o d) -> o d", o=1).to_broadcast([P, D // 2])).then_inc(s_in, 16)
                sp.wait_ge(s_ropemade, 1)
                sp.dma_start(rope_scratch.rearrange("b p n -> p b n"), rope_all.rearrange("p b i j d -> p b (i j d)")).then_inc(s_ropest, 16)
                for c in range(2):
                    sp.wait_ge(s_xl, 2 * 2 * KT + (c + 1) * KT)
                    for i in range(c * BLK, (c + 1) * BLK):
                        sp.dma_start(x_scratch[i].rearrange("p (t c) -> p t c", t=2 * KT),
                                     xh[:, :, :, i * S:(i + 1) * S].rearrange("p i k c -> p (i k) c").bitcast(F32)).then_inc(s_xs, 16)
                    for i in range(c * BLK, (c + 1) * BLK):
                        sp.wait_ge(m_free[i % 2], back_uses(i))
                        sp.dma_start(out[i], x_tok[:, i, :]).then_inc(s_init, 16)
                sp.wait_ge(s_ropest, 16)

            @block.gpsimd
            def _(pool):
                nc.gpsimd.memset(ident[:, :], 0.0).then_inc(s_const, 1)
                nc.gpsimd.memset(hot16[:, :], 1.0).then_inc(s_const, 1)
                nc.gpsimd.memset(hot32[:, :], 1.0).then_inc(s_const, 1)
                nc.gpsimd.iota(lane[:, :], [[0, 1]], base=0, channel_multiplier=1).then_inc(s_const, 1)
                pool.wait_ge(s_const, 4)
                nc.gpsimd.affine_select(ident[:, :], ident[:, :], [[-1, P]], ALU.not_equal, 1.0, base=0,
                                        channel_multiplier=1).then_inc(s_const, 1)
                nc.gpsimd.affine_select(hot16[:, :], hot16[:, :], [[-R, B]], ALU.is_ge, 0.0, base=0,
                                        channel_multiplier=1).then_inc(s_const, 1)
                nc.gpsimd.affine_select(hot32[:, :], hot32[:, :], [[-PSIZE, P // PSIZE]], ALU.is_ge, 0.0, base=0,
                                        channel_multiplier=1).then_inc(s_const, 1)
                pool.wait_ge(s_const, 7)
                nc.gpsimd.affine_select(hot16[:, :], hot16[:, :], [[R, B]], ALU.is_ge, 0.0, base=R - 1,
                                        channel_multiplier=-1).then_inc(s_const, 1)
                nc.gpsimd.affine_select(hot32[:, :], hot32[:, :], [[PSIZE, P // PSIZE]], ALU.is_ge, 0.0, base=PSIZE - 1,
                                        channel_multiplier=-1).then_inc(s_const, 1)

                def gather(dst, index, src, done):
                    nc.gpsimd.indirect_dma_start(
                        dst, None, src, bass.IndirectOffsetOnAxis(ap=index, axis=0)).then_inc(done, 16)

                pool.wait_ge(s_rows, 1)
                gather(ag_raw, row_r[:, 0:1], a["L0_cond_A_gate"].rearrange("l a r h -> (l a r) h"), s_ag)
                gather(au_raw, row_r[:, 0:1], a["L0_cond_A_up"].rearrange("l a r h -> (l a r) h"), s_au)
                for i, name in enumerate(("L0_cond_B_gate", "L0_cond_B_up")):
                    for b in range(B):
                        gather(bgu_raw[i][0:FPART, b, :], row_f[0:FPART, b:b + 1],
                               a[name].rearrange("l a (p j) r -> (l a p) (j r)", j=FSUB), s_bgu[i])
                for i in range(2):
                    pool.wait_ge(m_full[i], KT)
                gather(ad_raw, row_r[:, 0:1], a["L0_cond_A_down"].rearrange("l a r h -> (l a r) h"), s_ad)
                gather(a1_raw, row_r[:, 1:2], a["L1_cond_lora_a_weights"].rearrange("a r h -> (a r) h"), s_a1)
                gather(scale1[:, :], own_slot[:, :], a["L1_cond_scaling_factors"].rearrange("(a o) -> a o", o=1), s_scale)
                for i, (index, src) in enumerate(((row_d, a["L0_cond_B_down"].rearrange("l a (p j) r -> (l a p) (j r)", j=OSUB)),
                                                  (row_o, a["L1_cond_lora_b_weights"].rearrange("a (p j) r -> (a p) (j r)", j=OSUB)))):
                    for b in range(B):
                        gather(bo_raw[i][:, b, :], index[:, b:b + 1], src, s_bo[i])
                for i in range(2):
                    pool.wait_ge(s_bo[i], 16 * B)
                    nc.gpsimd.tensor_copy(bo_perm[i].rearrange("p j (b r) -> p b j r", r=R),
                                          bo_raw[i].rearrange("p b (j r) -> p b j r", r=R)).then_inc(s_permo, 1)
                gather(b2T[:, :], row_r[:, 2:3], a["L2_cond_lora_Bs"].rearrange("a r o -> (a r) o"), s_l2)
                for b in range(B):
                    for k in range(KT):
                        gather(a2T[:, k, b, :], row_i[:, b, k:k + 1], a["L2_cond_lora_As"].rearrange("a i r -> (a i) r"), s_l2)

                pool.wait_ge(s_d, 2 * FT)
                load_projections(nc, a, 0, w_raw3, wkv_raw, s_w)

            @block.tensor
            def _(pe):
                uses = Uses()

                def begin(i):
                    v = uses.value(i)
                    if not (isinstance(v, int) and v == 0):
                        pe.wait_ge(m_free[i], v)

                def fill(i, pieces, n, cols):
                    begin(i)
                    for c, piece in enumerate(pieces):
                        m = piece.shape[0]
                        last = nc.tensor.transpose(bank[i][0:n, c * P:c * P + cols], piece, ident[0:m, 0:m])
                    uses.take(i)
                    last.then_inc(m_full[i], 1)

                def jobs_of(jobs):
                    for i, (wait, pieces, n, cols, _) in enumerate(jobs):
                        pe.wait_ge(*wait)
                        fill(i % 2, pieces, n, cols)

                def lora_rows(aT, c, t, masked):
                    if masked:
                        pe.wait_ge(s_mask, masked)
                    for k in range(KT):
                        last = nc.tensor.matmul(tail[t][:, :], aT(k), xT[:, k, half(c)], start=(k == 0), stop=(k == KT - 1))
                    last.then_inc(s_tf, 1)

                def both_parts(out, w, rhs, start, stop=False):
                    for w_part, r_part in ((0, 0), (0, 1), (1, 0)):
                        last = nc.tensor.matmul(out, w(w_part), rhs(r_part), start=(start and w_part + r_part == 0),
                                                stop=(stop and w_part == 1))
                    return last

                pe.wait_ge(s_const, 5)
                for c in range(2):
                    pe.wait_ge(s_x[c], 16)
                    for k in range(KT):
                        fill(k % 2, [x_tok[:, c * BLK + i, k * P:(k + 1) * P] for i in range(BLK)], P, P)
                jobs_of(early_jobs)
                begin(0)
                begin(1)
                for c in range(2):
                    for i, w in enumerate((agT, auT)):
                        lora_rows(lambda k: w[:, k, :], c, i, 2 * c + i - 1 if c else 0)
                jobs_of(gate_up_jobs)
                pe.wait_ge(s_xlo, 2 * KT)
                def gate_prepare(j, buf):
                    n = rows(j)
                    pe.wait_ge(s_wr[buf], (j - buf) * 16 + 32)
                    for w in range(2):
                        fill(w, [w_raw[0:n, buf, w, k * P:(k + 1) * P] for k in range(KT)], P, n)

                def gate_use(j, buf):
                    n = rows(j)
                    if isinstance(j, int) and j == FT - 1:
                        begin(0)
                        begin(1)
                    pe.wait_ge(s_ringlo, j + 1)
                    for c in range(2):
                        if not isinstance(j, int) or j:
                            pe.wait_ge(s_act, j * 2 + (c - 1))
                        for w, t in enumerate((tg_hl, tu_hl)):
                            out = wide[c][0:n, w * TB:(w + 1) * TB]
                            for k in range(KT):
                                both_parts(out, lambda i: wT[:, buf, w, i, k, 0:n], lambda i: xh[:, i, k, half(c)], k == 0)
                            if isinstance(j, int) and j == 0:
                                pe.wait_ge(s_tlo, 2 * c + w + 1)
                            last = both_parts(out, lambda i: b_ring[:, buf, w, i, 0:n], lambda i: t[:, i, half(c)], False, True)
                        last.then_inc(s_gu, 1)

                in_steps(pe, uses, GATE_STEP, gate_prepare, gate_use, lambda: jobs_of(late_jobs))

                def w12_jobs(i, tiles):
                    pe.wait_ge(s_w12[i], 16)
                    for t in tiles:
                        fill(t % 2, [w12_raw[:, t, k * P:(k + 1) * P] for k in range(KT)], P, P)

                for c in range(2):
                    def down_prepare(j, buf):
                        n = rows(j)
                        pe.wait_ge(s_wdr[buf], (j - buf) * 8 + (c * (FT // 2 + 1 - buf) + 1) * 16)
                        fill(buf, [wd_raw[:, buf, t, 0:n] for t in range(KT)], n, P)

                    def down_use(j, buf):
                        n = rows(j)
                        first, end = (isinstance(j, int) and j == e for e in (0, FT - 1))
                        if first:
                            pe.wait_ge(s_act, 2 * FT)
                            if c:
                                pe.wait_ge(s_x1, c * KT)
                            pe.wait_ge(s_mask, 3 + c)
                        pe.wait_ge(m_free[buf], uses.value(buf))
                        pe.wait_ge(s_al, j + (c * FT + 1))
                        ins = both_parts(tail[c][:, :], lambda i: ad_ring[0:n, buf, i, :], lambda i: act_hl[0:n, buf, i, :], first, end)
                        if end:
                            ins.then_inc(s_tf, 1)
                        for h in range(KT):
                            last = both_parts(quarter(h), lambda i: wdT[0:n, buf, i, h * P:(h + 1) * P], lambda i: act_hl[0:n, buf, i, :], first)
                        last.then_inc(s_d, 1)

                    in_steps(pe, uses, DOWN_STEP, down_prepare, down_use)
                    if c == 0:
                        w12_jobs(0, (0, 1))
                    else:
                        pe.wait_ge(s_x1, KT)
                        lora_rows(lambda k: a1T[:, k, :], 0, 0, 5)
                    pe.wait_ge(s_mask, 5 + c)
                    for h in range(KT):
                        nc.tensor.matmul(quarter(h), bdT[:, h * P:(h + 1) * P], tg[:, half(c)], start=False, stop=True).then_inc(s_grp, 1)
                    w12_jobs(c, (0, 1) if c else (2, 3))

                def to_tokens(c):
                    pe.wait_ge(s_x1, 2 * 2 * KT + (c + 1) * KT)
                    for i in range(c * BLK, (c + 1) * BLK):
                        fill(i % 2, [xT[:, k, i * S:(i + 1) * S] for k in range(KT)], P, P)

                for n, (aT, w, bT, t) in enumerate(((lambda k: a1T[:, k, :], w1T, b1T, tu),
                                                    (lambda k: a2T[:, k].rearrange("p b r -> p (b r)"), w2T, b2T, tg))):
                    if n:
                        pe.wait_ge(s_l2, 16 * (1 + B * KT))
                        begin(0)
                        begin(1)
                    for c in range(2):
                        done = 2 * KT * n + c * KT + KT
                        if n or c:
                            pe.wait_ge(s_x1, done)
                            lora_rows(aT, c, c, 5 + 2 * n + c)
                        pe.wait_ge(s_xl, done)
                        for h in range(KT):
                            pe.wait_ge(s_x1, done + h + 1)
                            for k in range(KT):
                                both_parts(quarter(h), lambda i: w[:, i, k, h * P:(h + 1) * P], lambda i: xh[:, i, k, half(c)], k == 0)
                            if h == 0:
                                pe.wait_ge(s_mask, 7 + 2 * n + c)
                            nc.tensor.matmul(quarter(h), bT[:, h * P:(h + 1) * P], t[:, half(c)], start=False, stop=True).then_inc(s_grp, 1)
                            if n == c == 0 and h == 0:
                                w12_jobs(1, (2, 3))
                            if n == c == 1 and h == 1:
                                to_tokens(0)
                to_tokens(1)

            @block.scalar
            def _(act_e):
                ac = nc.scalar
                uses = Uses()
                for i, n in enumerate(("itok_B_2_6", "itok_B_1_7", "itok_B_0_23")):
                    act_e.dma_start(adapters[:, i, :], a[n].rearrange("(o b) -> o b", o=1).to_broadcast([P, B])).then_inc(s_small, 16)
                act_e.dma_start(seqlens[:, :], a["itok_B_207_1644"].rearrange("(o b) -> o b", o=1).to_broadcast([P, B])).then_inc(s_small, 16)
                act_e.dma_start(table[:, :, :, :].rearrange("p b t g -> p (b t g)"),
                                a["itok_Bx16_0_63"].rearrange("(o b) n -> o (b n)", o=1).to_broadcast([P, B * NPP])).then_inc(s_small, 16)
                act_e.dma_start(bias1[:, :], a["L1_cond_bias"].rearrange("(t p) -> p t", p=P), allow_slow_non_contiguous=True).then_inc(s_bias, 16)
                act_e.dma_start(bias2[:, :], a["L2_cond_b"].rearrange("(t p) -> p t", p=P), allow_slow_non_contiguous=True).then_inc(s_bias, 16)

                def high(i, dst, src):
                    act_e.wait_ge(m_full[i], uses.take(i))
                    uses.take(2)
                    ac.copy(dst, src).then_inc(s_hi, 1)

                for c in range(2):
                    for k in range(KT):
                        act_e.wait_ge(m_full[k % 2], uses.take(k % 2))
                        ac.copy(xT[:, k, half(c)], bank[k % 2][:, :])
                        ac.copy(xh[:, 0, k, half(c)], bank[k % 2][:, :]).then_inc(m_free[k % 2], 1)
                copy_jobs(act_e, ac.copy, 0, uses, early_jobs)

                def high_row(i):
                    act_e.wait_ge(s_mask, i + 1)
                    ac.copy((tg_hl, tu_hl)[i % 2][:, 0, half(i // 2)], (tg, tu)[i % 2][:, half(i // 2)]).then_inc(s_thi, 1)

                for i in range(3):
                    high_row(i)
                copy_jobs(act_e, ac.copy, 0, uses, gate_up_jobs)
                high_row(3)
                for i in range(2):
                    act_e.wait_ge(m_free[i], uses.value(i))

                def gate_prepare(j, buf):
                    n = rows(j)
                    for w in range(2):
                        high(w, wT[:, buf, w, 0, :, 0:n], bank[w][:, :].rearrange("p (k c) -> p k c", k=KT)[:, :, 0:n])
                    if not isinstance(j, int) or j + 2 < FT:
                        load_gate_up(act_e, j + 2, buf)
                    for w, t in enumerate((bgT, buT)):
                        cols = t[:, j * P:j * P + n] if isinstance(j, int) else t[:, bass.ds(j * P, P)]
                        last = ac.copy(b_ring[:, buf, w, 0, 0:n], cols)
                    last.then_inc(s_ring, 1)

                def gate_use(j, buf):
                    n = rows(j)
                    for c in range(2):
                        act_e.wait_ge(s_gu, j * 2 + (c + 1))
                        ac.activation(silu[0:n, c, :], wide[c][0:n, 0:TB], ACT.Silu).then_inc(s_si, 1)

                in_steps(act_e, uses, GATE_STEP, gate_prepare, gate_use, lambda: copy_jobs(act_e, ac.copy, 0, uses, late_jobs))
                act_e.dma_start(w12_raw, a["L1_cond_weight"].rearrange("(t p) h -> p t h", p=P)).then_inc(s_w12[0], 16)
                act_e.wait_ge(m_free[1], uses.value(1))
                def w12_jobs(w):
                    for t in range(KT):
                        high(t % 2, w12_dst(w, t)[:, 0], bank[t % 2][:, :].rearrange("p (k c) -> p k c", k=KT))

                def updated(n, c):
                    act_e.wait_ge(s_grp, 2 * KT * n + KT * c + KT)
                    for h in range(KT):
                        act_e.wait_ge(s_x1, 2 * KT * n + KT * c + h + 1)
                        ac.copy(xh[:, 0, h, half(c)], xT[:, h, half(c)]).then_inc(s_xh, 1)

                for c in range(2):
                    def down_prepare(j, buf):
                        n = rows(j)
                        if not isinstance(j, int) or j >= 2:
                            act_e.wait_ge(s_d, j + (c * FT - 1))
                        elif c:
                            act_e.wait_ge(s_d, FT)
                        else:
                            act_e.wait_ge(s_act, 2 * j + 1)
                        ac.copy(ad_ring[0:n, buf, 0, :], tile(adT, j)[0:n, :])
                        ac.copy(act_hl[0:n, buf, 0, :], tile(act, j)[0:n, half(c)]).then_inc(s_ah, 1)
                        high(buf, wdT[0:n, buf, 0, :], bank[buf][0:n, :])
                        if not isinstance(j, int) or j + 2 < FT:
                            load_down(act_e, j + 2, buf)
                        elif c == 0:
                            load_down(act_e, buf, buf)

                    in_steps(act_e, uses, DOWN_STEP, down_prepare, lambda j, buf: None,
                             first=(lambda: updated(0, 0)) if c else (lambda: act_e.wait_ge(s_act, 2 * FT)))
                    if c == 0:
                        w12_jobs(w1T)
                        act_e.dma_start(w12_raw, a["L2_cond_W"].rearrange("(t p) h -> p t h", p=P)).then_inc(s_w12[1], 16)
                w12_jobs(w2T)
                updated(0, 1)
                act_e.wait_ge(s_trig, 1)
                for i in range(2):
                    last = ac.activation(trig_out[:, i, :, :], trig_in[:, i, :, :], ACT.Sin)
                last.then_inc(s_sincos, 1)
                for n in (1, 2):
                    for c in range(2):
                        updated(n, c)
                        for i in range(c * BLK, (c + 1) * BLK) if n == 2 else ():
                            v = uses.take(i % 2)
                            if i % 2 == 0:
                                act_e.wait_ge(m_full[0], v)
                                ac.copy(x_tok[:, i, :], bank[0][:, :]).then_inc(m_free[0], 1)

            @block.vector
            def _(dve):
                step = Count(s_dve)
                uses = Uses()

                def then(ins):
                    step.inc(ins)
                    dve.wait_ge(s_dve, step.value())

                v = nc.vector
                dve.wait_ge(s_const, 9)
                dve.wait_ge(s_small, 16 * 5)
                v.tensor_copy(lane_f[:, :], lane[:, :])
                v.tensor_scalar(lane16[:, :], lane[:, :], R - 1, None, ALU.bitwise_and)
                v.tensor_scalar(lane32[:, :], lane[:, :], PSIZE - 1, None, ALU.bitwise_and)
                for i in range(3):
                    last = v.tensor_tensor(own[:, i, :], adapters[:, i, :], hot16[:, :], ALU.mult)
                then(last)
                then(v.tensor_reduce(own1[:, 0:3], own[:, :, :], AX.X, ALU.add))
                v.tensor_copy(own_slot[:, :], own1[:, 1:2])
                for i in range(3):
                    v.scalar_tensor_tensor(row_r[:, i:i + 1], own1[:, i:i + 1], float(R), lane16[:, :], ALU.mult, ALU.add)
                v.tensor_scalar(row_f[:, :], adapters[:, 0, :], float(FPART), lane_f[:, 0:1], ALU.mult, ALU.add)
                v.tensor_scalar(row_d[:, :], adapters[:, 0, :], float(P), lane_f[:, 0:1], ALU.mult, ALU.add)
                v.tensor_scalar(row_o[:, :], adapters[:, 1, :], float(P), lane_f[:, 0:1], ALU.mult, ALU.add)
                for k in range(KT):
                    v.tensor_scalar(row_i[:, :, k], adapters[:, 2, :], float(H), float(k * P), ALU.mult, ALU.add)
                for g in range(P // PSIZE):
                    last = v.tensor_scalar(picked[:, :, g], table[:, :, :, g].rearrange("p b t -> p (b t)"),
                                           hot32[:, g:g + 1], None, ALU.mult)
                then(last)
                then(v.tensor_reduce(kv_f[:, :], picked[:, :, :], AX.X, ALU.add))
                v.tensor_scalar(kv_f[:, :], kv_f[:, :], float(PSIZE), None, ALU.mult)
                then(v.tensor_copy(own1[:, 3:4], lane32[:, :]))
                v.tensor_scalar(row_kv[:, :], kv_f[:, :], own1[:, 3:4], float(NPAIR), ALU.add, ALU.mult)
                then(v.tensor_scalar(row_i[:, :, :], row_i[:, :, :], lane_f[:, 0:1], None, ALU.add))
                v.tensor_scalar(mask0[:, :], hot16[:, :], SCALE0, None, ALU.mult)
                v.tensor_scalar(mask2[:, :], hot16[:, :], SCALE2, None, ALU.mult).then_inc(s_rows, 1)

                for c in range(2):
                    for k in range(KT):
                        dve.wait_ge(m_free[k % 2], uses.take(k % 2))
                        v.tensor_tensor(xh[:, 1, k, half(c)], xT[:, k, half(c)], xh[:, 0, k, half(c)], ALU.subtract).then_inc(s_xlo, 1)
                copy_jobs(dve, v.tensor_copy, 1, uses, early_jobs)

                def order(i):
                    dve.wait_ge(s_bgu[i], 16 * B)
                    v.tensor_copy(bgu_perm[i][0:FPART].rearrange("p j (b r) -> p b j r", r=R),
                                  bgu_raw[i][0:FPART].rearrange("p b (j r) -> p b j r", r=R)).then_inc(s_perm, 1)

                masks = Count(s_tf)

                def mask_rows(dst, t, c, mask):
                    masks.n += 1
                    dve.wait_ge(s_tf, masks.value())
                    v.tensor_tensor(dst[:, half(c)].rearrange("p (b c) -> p b c", b=BLK), tail[t][:, :].rearrange("p (b c) -> p b c", b=BLK),
                                    mask[:, c * BLK:(c + 1) * BLK].rearrange("p (b o) -> p b o", o=1).to_broadcast([P, BLK, S]),
                                    ALU.mult).then_inc(s_mask, 1)

                order(0)
                for c in range(2):
                    for i, t in enumerate((tg, tu)):
                        mask_rows(t, i, c, mask0)
                order(1)
                copy_jobs(dve, v.tensor_copy, 1, uses, gate_up_jobs)

                def low(i, dst, src, hi):
                    uses.take(i)
                    dve.wait_ge(s_hi, uses.take(2))
                    v.tensor_tensor(dst, src, hi, ALU.subtract).then_inc(m_free[i], 1)

                def gate_prepare(j, buf):
                    n = rows(j)
                    for w in range(2):
                        low(w, wT[:, buf, w, 1, :, 0:n], bank[w][:, :].rearrange("p (k c) -> p k c", k=KT)[:, :, 0:n], wT[:, buf, w, 0, :, 0:n])
                    dve.wait_ge(s_ring, j + 1)
                    for w, t in enumerate((bgT, buT)):
                        cols = t[:, j * P:j * P + n] if isinstance(j, int) else t[:, bass.ds(j * P, P)]
                        last = v.tensor_tensor(b_ring[:, buf, w, 1, 0:n], cols, b_ring[:, buf, w, 0, 0:n], ALU.subtract)
                    last.then_inc(s_ringlo, 1)

                def gate_use(j, buf):
                    n = rows(j)
                    for c in range(2):
                        dve.wait_ge(s_si, j * 2 + (c + 1))
                        v.tensor_tensor(tile(act, j)[0:n, half(c)], silu[0:n, c, :], wide[c][0:n, TB:2 * TB], ALU.mult).then_inc(s_act, 1)

                def low_rows():
                    for i in range(4):
                        dve.wait_ge(s_thi, i + 1)
                        v.tensor_tensor((tg_hl, tu_hl)[i % 2][:, 1, half(i // 2)], (tg, tu)[i % 2][:, half(i // 2)],
                                        (tg_hl, tu_hl)[i % 2][:, 0, half(i // 2)], ALU.subtract).then_inc(s_tlo, 1)

                in_steps(dve, uses, GATE_STEP, gate_prepare, gate_use, lambda: copy_jobs(dve, v.tensor_copy, 1, uses, late_jobs), low_rows)
                dve.wait_ge(s_scale, 16)
                then(v.tensor_scalar(mask1[:, :], hot16[:, :], scale1[:, 0:1], None, ALU.mult))

                def w12_jobs(w, tiles):
                    for t in tiles:
                        low(t % 2, w12_dst(w, t)[:, 1], bank[t % 2][:, :].rearrange("p (k c) -> p k c", k=KT), w12_dst(w, t)[:, 0])

                def update(n, c, bias):
                    for h in range(KT):
                        dve.wait_ge(s_grp, 2 * KT * n + KT * c + h + 1)
                        if bias is None:
                            ins = v.tensor_tensor(xT[:, h, half(c)], quarter(h), xT[:, h, half(c)], ALU.add)
                        else:
                            ins = v.scalar_tensor_tensor(xT[:, h, half(c)], quarter(h), bias[:, h:h + 1], xT[:, h, half(c)], ALU.add, ALU.add)
                        ins.then_inc(s_x1, 1)

                def low_x(n, c):
                    for h in range(KT):
                        dve.wait_ge(s_xh, 2 * KT * n + KT * c + h + 1)
                        v.tensor_tensor(xh[:, 1, h, half(c)], xT[:, h, half(c)], xh[:, 0, h, half(c)], ALU.subtract).then_inc(s_xl, 1)

                for c in range(2):
                    def down_prepare(j, buf):
                        n = rows(j)
                        dve.wait_ge(s_ah, j + (c * FT + 1))
                        v.tensor_tensor(ad_ring[0:n, buf, 1, :], tile(adT, j)[0:n, :], ad_ring[0:n, buf, 0, :], ALU.subtract)
                        v.tensor_tensor(act_hl[0:n, buf, 1, :], tile(act, j)[0:n, half(c)], act_hl[0:n, buf, 0, :], ALU.subtract).then_inc(s_al, 1)
                        low(buf, wdT[0:n, buf, 1, :], bank[buf][0:n, :], wdT[0:n, buf, 0, :])

                    in_steps(dve, uses, DOWN_STEP, down_prepare, lambda j, buf: None,
                             first=(lambda: low_x(0, 0)) if c else None)
                    mask_rows(tg, c, c, mask0)
                    if c == 0:
                        w12_jobs(w1T, (0, 1))
                        update(0, c, None)
                        w12_jobs(w1T, (2, 3))
                mask_rows(tu, 0, 0, mask1)
                update(0, 1, None)
                w12_jobs(w2T, range(KT))
                low_x(0, 1)
                dve.wait_ge(s_in, 48)
                v.tensor_copy(seq_f[:, :], seqlens[:, :])
                then(v.tensor_scalar(pos[:, :], seqlens[:, :], lane_f[:, 0:1], None, ALU.add))
                angle, turned = trig_out[:, 0, :, :], trig_out[:, 1, :, :]
                for b in range(B):
                    last = v.tensor_scalar(angle[:, b, :], freq[:, :], pos[:, b:b + 1], None, ALU.mult)
                then(last)
                c1 = np.float32(6.28125)
                c2 = np.float32(np.floor((TWO_PI - float(c1)) * 2.0 ** 21) / 2.0 ** 21)
                c3 = np.float32(TWO_PI - float(c1) - float(c2))
                for i, shift in ((0, 0.0), (1, 0.25)):
                    red = trig_in[:, i, :, :]
                    then(v.tensor_scalar(turned, angle, 1.0 / TWO_PI, shift, ALU.mult, ALU.add))
                    then(v.tensor_scalar(turned, turned, ROUND, ROUND, ALU.add, ALU.subtract))
                    then(v.scalar_tensor_tensor(red, turned, -float(c1), angle, ALU.mult, ALU.add))
                    then(v.scalar_tensor_tensor(red, turned, -float(c2), red, ALU.mult, ALU.add))
                    then(v.scalar_tensor_tensor(red, turned, -float(c3), red, ALU.mult, ALU.add))
                    then(v.tensor_scalar(red, red, shift * TWO_PI, 3.1415925, ALU.add, ALU.min))
                    then(v.tensor_scalar(red, red, -3.1415925, None, ALU.max))
                v.tensor_scalar(turned[:, 0, 0:1], pos[:, 0:1], 0.0, None, ALU.mult).then_inc(s_trig, 1)
                dve.wait_ge(s_bias, 32)
                update(1, 0, bias1)
                mask_rows(tu, 1, 1, mask1)
                low_x(1, 0)
                update(1, 1, bias1)
                mask_rows(tg, 0, 0, mask2)
                low_x(1, 1)
                dve.wait_ge(s_sincos, 1)
                hd = D // 2
                sin, cos = trig_out[:, 0, :, :], trig_out[:, 1, :, :]
                for i in range(2):
                    w1 = normw[:, i:i + 1, 0:hd].to_broadcast([P, B, hd])
                    w2 = normw[:, i:i + 1, hd:D].to_broadcast([P, B, hd])
                    v.tensor_tensor(rope_all[:, :, i, 0, 0:hd], cos, w1, ALU.mult)
                    v.tensor_tensor(rope_all[:, :, i, 0, hd:D], cos, w2, ALU.mult)
                    v.scalar_tensor_tensor(rope_all[:, :, i, 1, 0:hd], sin, -1.0, w2, ALU.mult, ALU.mult)
                    last = v.tensor_tensor(rope_all[:, :, i, 1, hd:D], sin, w1, ALU.mult)
                last.then_inc(s_ropemade, 1)
                update(2, 0, bias2)
                mask_rows(tg, 1, 1, mask2)
                low_x(2, 0)

                def to_tokens(c):
                    for i in range(c * BLK, (c + 1) * BLK):
                        n = uses.take(i % 2)
                        if i % 2 == 1:
                            dve.wait_ge(m_full[1], n)
                            v.tensor_copy(x_tok[:, i, :], bank[1][:, :]).then_inc(m_free[1], 1)

                to_tokens(0)
                update(2, 1, bias2)
                low_x(2, 1)
                to_tokens(1)

        build_attention(nc, a, ctx, tensor, sem, bank, wide, tail, ident, seq_f, row_kv, prime, w_raw3, wkv_raw, pr, s_w, s_ropest, s_xs, s_init, x_scratch, rope_scratch, out)


def load_projections(nc, a, pair, w_raw, wkv_raw, loaded):
    rows = HP * D
    nc.gpsimd.dma_start(w_raw, a["L3_cond_Wq"][bass.ds(pair * rows, rows)].rearrange("(t p) h -> p t h", p=P)).then_inc(loaded, 16)
    for i, w in enumerate(("L3_cond_Wk", "L3_cond_Wv")):
        nc.gpsimd.dma_start(wkv_raw[:, i * G:(i + 1) * G, :],
                            a[w][bass.ds(pair * (G * D), G * D)].rearrange("(t p) h -> p t h", p=P)).then_inc(loaded, 16)


def build_attention(nc, a, ctx, tensor, sem, bank, wide, tail, ident, seq_f, row_kv, prime, w_raw3, wkv_raw, pr, s_w, s_ropest, s_xs, s_init, x_scratch, rope_scratch, out):
    QW = HP * D
    w_raw = w_raw3
    wo_raw = w_raw[:, :, :].rearrange("p t h -> p (t h)").rearrange("p (t e) -> p t e", t=KT)
    woT = tensor(ctx, "woT", [P, 2, HP, H], F32R)
    prT = tensor(ctx, "prT", [P, 2, JT, REP * S], F32R)
    wkvT = tensor(ctx, "wkvT", [P, 2, KT, 2 * G * D], F32R)
    xTb = tensor(ctx, "xTb", [P, 2, KT, S], F32R)
    k_raw = tensor(ctx, "k_raw", [P, LT, G * D])
    v_raw = tensor(ctx, "v_raw", [P, JT, G * D])
    qk = tensor(ctx, "qk", [P, NH, D])
    vt = tensor(ctx, "vt", [P, 2, JT, G * D], F32R)
    oT = tensor(ctx, "oT", [P, 2, G, REP * S], F32R)
    wqT = tensor(ctx, "wqT", [P, 2, KT, QW], F32R)
    rows_now = tensor(ctx, "rows_now", [P, LT], I32)
    ra = tensor(ctx, "ra", [P, NH, D])
    rb = tensor(ctx, "rb", [P, REP + G, D])
    qT = tensor(ctx, "qT", [P, G, REP * S], F32R)
    kT = tensor(ctx, "kT", [P, G, NK], F32R)
    qT_low = oT[:, :, 0, :]
    kT_low = prT[:, :, :, :].rearrange("p i j c -> p (i j c)")[:, 0:G * NK].rearrange("p (g k) -> p g k", g=G)
    y = tensor(ctx, "y", [P, H])
    rope = tensor(ctx, "rope", [P, 4, D])
    bias = tensor(ctx, "bias", [P, NK])
    ss = tensor(ctx, "ss", [P, NH])
    var = tensor(ctx, "var", [P, NH])
    rs = tensor(ctx, "rs", [P, NH])
    nt = tensor(ctx, "nt", [P, NH])
    mx = tensor(ctx, "mx", [P, HP])
    nm = tensor(ctx, "nm", [P, HP])
    den = tensor(ctx, "den", [P, HP])
    rden = tensor(ctx, "rden", [P, HP])
    q_scale = tensor(ctx, "q_scale", [P, 2, NH])
    tick = tensor(ctx, "tick", [P, 4])

    s_xt = sem("xTb_loaded")
    s_ropel = sem("rope_loaded")
    s_high = sem("keys_and_queries_high_part_ready")
    s_k = sem("cached_keys_loaded")
    s_v = sem("cached_values_loaded")
    s_rowsnow = sem("rows_now_ready")
    s_rowskv = sem("pair_rows_ready")
    s_carry = sem("pool_waits_carried")
    s_keyno = sem("key_numbers_made")
    s_step = sem("dve_step3")
    s_wo = sem("out_weights_loaded")
    s_wohi = sem("out_weights_high_part_ready")
    s_whi = sem("weights_high_part_ready")
    s_vnew = sem("new_values_copied")
    s_vhi = sem("values_high_part_ready")
    s_vs = sem("values_split")
    s_phi = sem("probs_high_part_ready")
    s_kc = sem("new_keys_copied")
    s_q0 = sem("first_queries_copied")
    s_q1 = sem("second_queries_copied")
    s_rope = sem("rotated")
    s_sfull = sem("scores_full")
    s_sfree = sem("scores_masked")
    s_nm = sem("negative_max_ready")
    s_exp = sem("exp_done")
    s_rden = sem("denominator_ready")
    s_p = [sem(f"probs_ready{i}") for i in range(G)]
    s_pv = sem("values_summed")
    s_o = sem("values_copied")
    s_y = sem("out_share_full")
    s_yadd = sem("out_share_copied")
    s_out = sem("out_share_stored")
    s_added = sem("last_shares_added")
    s_ohi = sem("values_high_part_copied")
    t_full = [sem(f"probs_transposed{i}") for i in range(2)]
    t_free = [sem(f"probs_copied{i}") for i in range(2)]
    j_full = sem("new_probs_transposed")
    j_free = sem("new_probs_copied")
    w_full = [sem(f"weights_transposed{i}") for i in range(4)]
    w_free = [sem(f"weights_split{i}") for i in range(4)]
    c_full = [sem(f"chunk_full{i}") for i in range(2)]
    c_free = [sem(f"chunk_free{i}") for i in range(2)]

    LATE = 2
    SOON = HP - LATE
    NWJ = HP + 2 * G
    w_place = [tail[0][:, :], tail[1][:, :], wide[0][:, 0:H], wide[1][:, 0:H]]
    WP = NWJ // len(w_place)
    WC, WO = NWJ // 2, HP // 2
    FRONT, BACK = (4, 4), (1, 0)
    NSTEP = 22
    TURN = [FRONT[i] + BACK[i] for i in range(2)]

    def weight_jobs():
        for t in (*range(REP), *range(HP, NWJ), *range(REP, HP)):
            raw, dst, c = (w_raw, wqT, t) if t < HP else (wkv_raw, wkvT, t - HP)
            yield [raw[:, c, k * P:(k + 1) * P] for k in range(KT)], dst[:, :, :, c * P:(c + 1) * P]

    def out_job(h):
        return [wo_raw[:, t, h * D:(h + 1) * D] for t in range(KT)], woT[:, :, h, :].rearrange("p i (t c) -> p i t c", t=KT)

    k_rows = a["L3_cond_k_cache"].rearrange("a s (e g) d -> (a s e) (g d)", g=G)
    v_rows = a["L3_cond_v_cache"].rearrange("a s (e g) d -> (a s e) (g d)", g=G)

    def unit(pair, b):
        return pair * B + b

    def turns(eng, turn):
        turn(0, 0, [0, 0], True, False, "out", False, True)
        with eng.Fori(0, NPAIR - 1) as pair:
            with eng.Fori(0, B - 2) as last:
                turn(pair, last + 1, [pair * (B * TURN[i]) + last * TURN[i] + FRONT[i] for i in range(2)], True, True, None, True, True)
            turn(pair, B - 1, [pair * (B * TURN[i]) + ((B - 2) * TURN[i] + FRONT[i]) for i in range(2)], True, True, "next", True, True)
            turn(pair + 1, 0, [pair * (B * TURN[i]) + ((B - 1) * TURN[i] + FRONT[i]) for i in range(2)], True, True, "out", True, True)
        pair = NPAIR - 1
        done = [pair * B * TURN[i] + FRONT[i] for i in range(2)]
        with eng.Fori(0, B - 2) as last:
            turn(pair, last + 1, [last * TURN[i] + done[i] for i in range(2)], True, True, None, True, True)
        turn(pair, B - 1, [(B - 2) * TURN[i] + done[i] for i in range(2)], True, True, None, True, False)
        turn(NPAIR, 0, [(B - 1) * TURN[i] + done[i] for i in range(2)], False, True, None, False, False)

    def weights_done(pair, extra):
        return pair * (WO + WC) + (WP + (WO if extra == "next" else 0))

    def head(h):
        i = h if h < REP else h + G
        return slice(i, i + 1)

    def chunks(extra, h):
        if extra == "next":
            return [(i, job) for i, job in enumerate(weight_jobs()) if i * HP // NWJ == h]
        return [(h, out_job(h))] if extra == "out" else []

    with nc.Block() as block:
        @block.gpsimd
        def _(pool):
            for i, primed in enumerate((s_rowskv, s_vs, s_pv, s_carry, c_free[0], c_free[1], t_free[0], t_free[1],
                                        s_sfree, s_o, s_yadd, s_rope, s_p[0], s_p[1])):
                nc.gpsimd.memset(prime[:, i:i + 1], 0.0).then_inc(primed, FIRST)
            nc.gpsimd.memset(prime[:, 15:16], 0.0).then_inc(s_sfull, HP)
            nc.gpsimd.memset(bias[:, L:NK], 0.0).then_inc(s_keyno, 1)
            nc.gpsimd.memset(tick[:, 1:3], 0.0).then_inc(s_keyno, 1)
            pool.wait_ge(s_keyno, 2)
            NCARRY = 1 + 6 * B

            def carry(n):
                pool.wait_ge(s_carry, n + FIRST)
                nc.gpsimd.tensor_tensor(tick[:, 2:3], tick[:, 1:2], tick[:, 1:2], ALU.add).then_inc(s_carry, 1)

            def loads(pair, b, n):
                u = unit(pair, b)
                pool.wait_ge(s_rowskv, pair + FIRST)
                pool.wait_ge(s_sfull, u * HP + 1)
                pool.wait_ge(s_vs, u + FIRST)
                carry(n)
                nc.gpsimd.tensor_copy(rows_now[:, :], row_kv[:, bass.ds(b * LT, LT)]).then_inc(s_rowsnow, 1)
                pool.wait_ge(s_rowsnow, u + 1)
                carry(n + 1)
                pool.wait_ge(s_ropest, 16)
                nc.gpsimd.dma_start(rope[:, :, :].rearrange("p i d -> p (i d)"),
                                    rope_scratch[bass.ds(b, 1)].rearrange("o p n -> (o p) n")).then_inc(s_ropel, 16)
                for t in range(LT):
                    nc.gpsimd.indirect_dma_start(k_raw[:, t, :], None, k_rows,
                                                 bass.IndirectOffsetOnAxis(ap=rows_now[:, t:t + 1], axis=0)).then_inc(s_k, 16)
                for t in range(LT):
                    nc.gpsimd.indirect_dma_start(v_raw[:, t, :], None, v_rows,
                                                 bass.IndirectOffsetOnAxis(ap=rows_now[:, t:t + 1], axis=0)).then_inc(s_v, 16)

            def load_x(b):
                nc.gpsimd.dma_start(xTb[:, :, :, :].rearrange("p i k c -> p (i k c)"),
                                    x_scratch[bass.ds(b, 1)].rearrange("o p n -> (o p) n")).then_inc(s_xt, 16)

            def add_share(u, b, n):
                pool.wait_ge(s_yadd, u + 1 + FIRST)
                carry(n)
                nc.gpsimd.dma_start(out[bass.ds(b, 1)].rearrange("o p h -> (o p) h"), y[:, :], accum_op=ALU.add).then_inc(s_out, 16)

            def split_values(pair, b, n, then_x, shared=True):
                u = unit(pair, b)
                if shared:
                    pool.wait_ge(s_out, u * 16 - 16)
                pool.wait_ge(s_sfree, u * HP + FIRST)
                carry(n)
                nc.gpsimd.iota(bias[:, 0:L], [[1, L]], base=0, channel_multiplier=0,
                               allow_small_or_imprecise_dtypes=True).then_inc(s_keyno, 1)
                if then_x is not None:
                    pool.wait_ge(s_q1, u + 1)
                    carry(n + 1)
                    load_x(then_x)
                pool.wait_ge(s_pv, u * G + FIRST)
                pool.wait_ge(s_vnew, u + 1)
                pool.wait_ge(s_v, u * (16 * LT) + 16 * LT)
                carry(n + (1 if then_x is None else 2))
                nc.gpsimd.tensor_copy(vt[:, 0, :, :], v_raw[:, :, :]).then_inc(s_vhi, 1)
                pool.wait_ge(s_vhi, u + 1)
                nc.gpsimd.tensor_tensor(vt[:, 1, :, :], v_raw[:, :, :], vt[:, 0, :, :], ALU.subtract).then_inc(s_vs, 1)

            def load_output(pair, n):
                pool.wait_ge(s_whi, pair * NWJ + NWJ)
                carry(n)
                nc.gpsimd.dma_start(wo_raw, a["L3_cond_Wo"][:, bass.ds(pair * QW, QW)].rearrange("(t p) e -> p t e", p=P)).then_inc(s_wo, 16)

            def turn(pair, b, n, share, then_x, then_load=None):
                loads(pair, b, n)
                if share is not None:
                    add_share(unit(pair, b) - 2, share, n + 2)
                    n = n + 1
                if then_load:
                    then_load()
                split_values(pair, b, n + 2, then_x, share is not None)

            pool.wait_ge(s_xs, 16 * B)
            load_x(0)
            pool.wait_ge(s_init, 16 * B)
            loads(0, 0, 0)
            load_output(0, 2)
            split_values(0, 0, 3, 1, False)
            turn(0, 1, 6, None, 2)
            START = 11
            with pool.Fori(0, NPAIR - 1) as pair:
                n = pair * NCARRY + START
                turn(pair, 2, n, 0, 3, lambda: load_projections(nc, a, pair + 1, w_raw, wkv_raw, s_w))
                with pool.Fori(0, B - 4) as b:
                    turn(pair, b + 3, pair * NCARRY + b * 6 + (START + 6), b + 1, b + 4)
                turn(pair, B - 1, pair * NCARRY + (START + 6 * (B - 3)), B - 3, 0)
                m = pair * NCARRY + (START + 6 * (B - 2))
                loads(pair + 1, 0, m)
                add_share(unit(pair + 1, 0) - 2, B - 2, m + 2)
                load_output(pair + 1, m + 3)
                split_values(pair + 1, 0, m + 4, 1)
                turn(pair + 1, 1, m + 7, B - 1, 2)
            pair = NPAIR - 1
            with pool.Fori(0, B - 3) as b:
                turn(pair, b + 2, b * 6 + (pair * NCARRY + START), b, b + 3)
            turn(pair, B - 1, pair * NCARRY + (START + 6 * (B - 3)), B - 3, None)
            n = pair * NCARRY + (START + 6 * (B - 2) - 1)
            for i in (2, 1):
                add_share(NPAIR * B - i, B - i, n + 2 - i)
                pool.wait_ge(s_out, 16 * (NPAIR * B - i + 1))
                nc.gpsimd.memset(tick[:, 3:4], 0.0).then_inc(s_added, 1)

        @block.tensor
        def _(pe):
            def turn(pair, b, before, front, back, extra, projected, ahead):
                n, u = unit(pair, b), unit(pair, b - 1)
                full = [Count(c, before[i]) for i, c in enumerate(c_full)]

                def begin(i):
                    pe.wait_ge(c_free[i], full[i].value() + FIRST)

                first_turn = isinstance(b, int) and b == 0
                weights_now = weights_done(pair, "out") if front and first_turn else weights_done(NPAIR - 1 if first_turn else pair, "next")
                PASSES = ((0, 0), (0, 1), (1, 0))
                NPROD = KT * len(PASSES)
                AHEAD = [0] + [1 + 3 * h for h in range(HP - 1)] + [2 * NPROD]
                AHEAD_NEXT = [0] * 4 + [NPROD // 3 * i for i in range(1, HP - 3)] + [2 * NPROD]

                def project(i, w, first=0, count=NPROD):
                    if first == 0:
                        begin(i)
                    for step in range(first, first + count):
                        k, (x_part, w_part) = step // 3, PASSES[step % 3]
                        last = nc.tensor.matmul(bank[i][:, :], xTb[:, x_part, k, :], w[:, w_part, k, :],
                                                start=(step == 0), stop=(step == NPROD - 1))
                    if first + count == NPROD:
                        full[i].inc(last)

                first_two = ((0, wkvT), (1, wqT[:, :, :, 0:REP * D]))

                def project_ahead(first, end):
                    if first == 0 and end:
                        pe.wait_ge(s_xt, n * 16 + 32)
                    while first < end:
                        which, step = divmod(first, NPROD)
                        count = min(end - first, NPROD - step)
                        if extra == "next":
                            if step == 0:
                                for t in range(2):
                                    pe.wait_ge(w_free[t], weights_done(pair, extra) + (which + 1) * (WC // 3))
                            which = 1 - which
                        project(*first_two[which], step, count)
                        first += count

                def weights(i, pieces):
                    if i < 2 and back:
                        pe.wait_ge(*((s_o, u * G + G + FIRST) if i else (s_yadd, u + 1 + FIRST)))
                    pe.wait_ge(w_free[i % 2], weights_done(pair, extra) + i // 2)
                    for c, piece in enumerate(pieces):
                        last = nc.tensor.transpose(w_place[i % 2][:, c * P:(c + 1) * P], piece, ident[:, :])
                    last.then_inc(w_full[i % 2], 1)

                def transposes(i, pieces):
                    begin(i)
                    for c, piece in enumerate(pieces):
                        last = nc.tensor.transpose(bank[i][:, c * P:(c + 1) * P], piece, ident[:, :])
                    full[i].inc(last)

                def probs_of(g, j):
                    return [pr[:, g * REP + i, j * P:(j + 1) * P] for i in range(REP)]

                def probs_wide(g, w):
                    pe.wait_ge(s_p[0], u * SOON + (SOON if g else REP) + FIRST)
                    if g:
                        pe.wait_ge(s_p[1], u * LATE + LATE + FIRST)
                    pe.wait_ge(t_free[w], u * G + g + FIRST)
                    for c, piece in enumerate(probs_of(g, 2 * w) + probs_of(g, 2 * w + 1)):
                        last = nc.tensor.transpose(wide[w][:, c * P:(c + 1) * P], piece, ident[:, :])
                    last.then_inc(t_full[w], 1)

                def sums(g, j):
                    for v_part, p_part in ((0, 0), (0, 1), (1, 0)):
                        last = nc.tensor.matmul(tail[g][:, :], vt[:, v_part, j, g * D:(g + 1) * D], prT[:, p_part, j, :],
                                                start=(j == 0 and v_part + p_part == 0), stop=(j == JT - 1 and v_part == 1))
                    return last

                def values(g, w):
                    pe.wait_ge(t_free[w], u * G + g + 1 + FIRST)
                    for j in (2 * w, 2 * w + 1):
                        sums(g, j)

                def values_new(g):
                    if g == 0:
                        pe.wait_ge(j_free, u + 1)
                    else:
                        begin(0)
                    sums(g, JT - 1).then_inc(s_pv, 1)

                def score(h):
                    if h < 2:
                        pe.wait_ge(t_free[h], n * G + FIRST)
                        pe.wait_ge(s_sfree, n * HP + FIRST)
                    else:
                        pe.wait_ge(s_sfree, n * HP + (h - 1) + FIRST)
                    g, i = h // REP, h % REP
                    for c in range(2):
                        out = wide[h % 2][:, c * H:c * H + NK // 2]
                        for q_part, k_part in PASSES:
                            last = nc.tensor.matmul(out, (qT, qT_low)[q_part][:, g, i * S:(i + 1) * S],
                                                    (kT, kT_low)[k_part][:, g, c * (NK // 2):(c + 1) * (NK // 2)],
                                                    start=(q_part + k_part == 0), stop=(q_part == 1))
                    last.then_inc(s_sfull, 1)

                if projected:
                    for i in range(2):
                        full[i].n += 1
                elif front:
                    pe.wait_ge(s_xt, n * 16 + 16)
                    for part in range(2):
                        for place in w_free:
                            pe.wait_ge(place, part + 1)
                        project(*first_two[1 - part])
                if back:
                    pe.wait_ge(s_sfree, u * HP + HP + FIRST)
                    probs_wide(0, 0)
                    probs_wide(0, 1)
                    pe.wait_ge(s_o, u * G + FIRST)
                    pe.wait_ge(w_free[1], weights_now)
                    for c, piece in enumerate(probs_of(0, JT - 1)):
                        last = nc.tensor.transpose(tail[1][:, c * P:(c + 1) * P], piece, ident[:, :])
                    last.then_inc(j_full, 1)
                if front:
                    if first_turn:
                        for i in range(2):
                            pe.wait_ge(w_free[i], weights_done(pair, "out"))
                            if not back:
                                pe.wait_ge(w_free[2 + i], WP)
                    project(0, wqT[:, :, :, REP * D:QW])
                if back:
                    pe.wait_ge(s_yadd, u + FIRST)
                    pe.wait_ge(s_vs, u + 1 + FIRST)
                    pe.wait_ge(w_free[0], weights_now)
                    values(0, 0)
                    probs_wide(1, 0)
                    values(0, 1)
                    probs_wide(1, 1)
                    values_new(0)
                    transposes(0, probs_of(1, JT - 1))
                if front:
                    pe.wait_ge(s_k, n * (16 * LT) + 16 * LT)
                    transposes(1, [k_raw[:, t, 0:D] for t in range(LT)])
                if back:
                    values(1, 0)
                    values(1, 1)
                    values_new(1)
                if front:
                    transposes(0, [k_raw[:, t, D:2 * D] for t in range(LT)])
                def output(h0, m):
                    for h in range(h0, h0 + m):
                        if h % REP == 0:
                            pe.wait_ge(s_o, u * G + h // REP + 1 + FIRST)
                        for o_part, w_part in ((0, 0), (0, 1), (1, 0)):
                            last = nc.tensor.matmul(tail[0][:, :], oT[:, o_part, h // REP, (h % REP) * S:(h % REP + 1) * S], woT[:, w_part, h, :],
                                                    start=(h == 0 and o_part + w_part == 0), stop=(h == HP - 1 and o_part == 1))
                    return last

                if back:
                    output(0, REP)
                if front:
                    pe.wait_ge(s_rope, n * G + 1 + FIRST)
                    transposes(1, [ra[:, i, :] for i in range(REP)])
                if back:
                    output(REP, REP // 2)
                if front:
                    transposes(0, [ra[:, REP + i, :] for i in range(G)])
                if back:
                    output(REP + REP // 2, REP // 2).then_inc(s_y, 1)
                if front:
                    pe.wait_ge(s_rope, n * G + 2 + FIRST)
                    transposes(1, [ra[:, REP + G + i, :] for i in range(REP)])
                    rotated = full[1].value()
                    begin(0)
                    for h in range(HP):
                        if h == REP:
                            pe.wait_ge(c_free[1], rotated + FIRST)
                        score(h)
                        for i, (pieces, _) in chunks(extra, h):
                            if i == 0:
                                pe.wait_ge(*((s_w, pair * 48 + 96) if extra == "next" else (s_wo, pair * 16 + 16)))
                            weights(i, pieces)
                        if ahead:
                            ahead_to = AHEAD_NEXT if extra == "next" else AHEAD
                            project_ahead(ahead_to[h], ahead_to[h + 1])

            pe.wait_ge(s_w, 48)
            n_place = len(w_place)
            for i, (pieces, _) in enumerate(weight_jobs()):
                if i >= n_place:
                    pe.wait_ge(w_free[i % n_place], i // n_place)
                for c, piece in enumerate(pieces):
                    last = nc.tensor.transpose(w_place[i % n_place][:, c * P:(c + 1) * P], piece, ident[:, :])
                last.then_inc(w_full[i % n_place], 1)
            turns(pe, turn)

        @block.scalar
        def _(act):
            ac = nc.scalar
            def high_weights(i, count, dst, done):
                act.wait_ge(w_full[i], count)
                ac.copy(dst[:, 0], w_place[i].rearrange("p (t c) -> p t c", t=KT)).then_inc(done, 1)

            def turn(pair, b, before, front, back, extra, projected, ahead):
                n, u = unit(pair, b), unit(pair, b - 1)
                full0 = Count(c_full[0], before[0])

                def arrive():
                    full0.n += 1
                    act.wait_ge(c_full[0], full0.value())

                def squares(i, h0, m):
                    for h in range(m):
                        head = bank[i][:, h * D:(h + 1) * D]
                        last = ac.activation(head, head, ACT.Square, accum_out=ss[:, h0 + h:h0 + h + 1])
                    last.then_inc(c_free[i], 1)

                def high(bank_no, nth, dst, src):
                    act.wait_ge(c_full[bank_no], before[bank_no] + nth)
                    ac.copy(dst, src).then_inc(s_high, 1)

                def high_probs(g, w):
                    act.wait_ge(t_full[w], u * G + g + 1)
                    ac.copy(prT[:, 0, 2 * w:2 * w + 2, :], wide[w][:, :].rearrange("p (j c) -> p j c", j=2)).then_inc(s_phi, 1)

                def copy_values(g):
                    act.wait_ge(s_pv, u * G + g + 1 + FIRST)
                    ac.copy(oT[:, 0, g, :], tail[g][:, :]).then_inc(s_ohi, 1)

                def exponential(h):
                    act.wait_ge(s_nm, n * HP + h + 1)
                    ac.activation(pr[:, h, :], pr[:, h, :], ACT.Exp, bias=nm[:, h:h + 1], scale=q_scale[:, 0, head(h)],
                                  accum_out=den[:, h:h + 1]).then_inc(s_exp, 1)

                def normalise(of, h):
                    if h < SOON:
                        act.wait_ge(s_step, of * NSTEP + (NSTEP - SOON + h + 1))
                    else:
                        act.wait_ge(s_rden, of * LATE + h - SOON + 1)
                    ac.activation(pr[:, h, :], pr[:, h, :], ACT.Copy, scale=rden[:, h:h + 1]).then_inc(s_p[h // SOON], 1)

                def new_keys_values(n):
                    arrive()
                    act.wait_ge(s_vs, n + FIRST)
                    ac.copy(v_raw[:, LT, :], bank[0][:, G * D:2 * G * D]).then_inc(s_vnew, 1)
                    act.wait_ge(s_rope, n * G + FIRST)
                    ac.copy(qk[:, REP:REP + G, :], bank[0][:, 0:G * D].rearrange("p (h d) -> p h d", d=D)).then_inc(s_kc, 1)
                    act.wait_ge(s_kc, n + 1)
                    squares(0, REP, G)

                if projected:
                    full0.n += 1
                elif front:
                    new_keys_values(n)
                if back:
                    high_probs(0, 0)
                    high_probs(0, 1)
                    act.wait_ge(j_full, u + 1)
                    ac.copy(prT[:, 0, JT - 1, :], tail[1][:, :]).then_inc(s_phi, 1)
                    for h in range(SOON, HP):
                        normalise(u, h)
                if front:
                    act.wait_ge(s_q0, n + 1)
                    squares(1, 0, REP)
                    arrive()
                    ac.copy(qk[:, REP + G:NH, :], bank[0][:, :].rearrange("p (h d) -> p h d", d=D)).then_inc(s_q1, 1)
                    act.wait_ge(s_q1, n + 1)
                    squares(0, REP + G, REP)
                if back:
                    high_probs(1, 0)
                    high_probs(1, 1)
                    arrive()
                    ac.copy(prT[:, 0, JT - 1, :], bank[0][:, :]).then_inc(s_phi, 1)
                    copy_values(0)
                own = BACK[0] if back else 0
                if front:
                    high(1, 2, kT[:, 0, 0:L], bank[1][:, :])
                if back:
                    copy_values(1)
                if front:
                    high(0, 3 + own, kT[:, 1, 0:L], bank[0][:, :])
                    high(1, 3, qT[:, 0, :], bank[1][:, :])
                    high(0, 4 + own, kT[:, :, L:NK], bank[0][:, 0:G * S].rearrange("p (g c) -> p g c", g=G))
                    high(1, 4, qT[:, 1, :], bank[1][:, :])
                if back:
                    act.wait_ge(*((s_keyno, n + 3) if front else (s_added, 1)))
                    act.wait_ge(s_y, u + 1)
                    ac.copy(y[:, :], tail[0][:, :]).then_inc(s_yadd, 1)
                if front:
                    for h in range(HP):
                        for i, (_, dst) in chunks(extra, h):
                            high_weights(i % 2, weights_done(pair, extra) + (i // 2 + 1), dst, s_whi if extra == "next" else s_wohi)
                        exponential(h)
                        if extra == "next" and h >= REP:
                            normalise(n, h - REP)
                        if ahead and h == (HP - 1 if extra else REP + 1):
                            full0.n = (TURN if back else FRONT)[0]
                            new_keys_values(n + 1)
                    if extra == "next":
                        for h in range(REP, SOON):
                            normalise(n, h)

            for i, (_, dst) in enumerate(weight_jobs()):
                high_weights(i % len(w_place), i // len(w_place) + 1, dst, s_whi)
            turns(act, turn)

        @block.vector
        def _(dve):
            v = nc.vector
            half = D // 2

            def low_weights(ready, count, i, dst):
                dve.wait_ge(ready, count)
                v.tensor_tensor(dst[:, 1], w_place[i].rearrange("p (t c) -> p t c", t=KT), dst[:, 0],
                                ALU.subtract).then_inc(w_free[i], 1)

            def turn(pair, b, before, front, back, extra, projected, ahead):
                n, u = unit(pair, b), unit(pair, b - 1)
                full1 = Count(c_full[1], before[1])
                at = Count(s_step, n * NSTEP)

                def then(ins):
                    at.inc(ins)
                    dve.wait_ge(s_step, at.value())

                def arrive():
                    full1.n += 1
                    dve.wait_ge(c_full[1], full1.value())

                def root_begin():
                    dve.wait_ge(c_free[0], before[0] + 2 + FIRST)
                    then(v.tensor_scalar(var[:, :], ss[:, :], 1.0 / D, EPS, ALU.mult, ALU.add))
                    then(v.tensor_scalar(rs[:, :].bitcast(I32), var[:, :].bitcast(I32), -0.5, float(0x5F3759DF), ALU.mult, ALU.add))

                def root_end():
                    x_, y_, t_ = var[:, :], rs[:, :], nt[:, :]
                    for _ in range(3):
                        then(v.tensor_tensor(t_, y_, y_, ALU.mult))
                        then(v.scalar_tensor_tensor(t_, t_, -0.5, x_, ALU.mult, ALU.mult))
                        then(v.scalar_tensor_tensor(y_, t_, 1.5, y_, ALU.add, ALU.mult))
                    v.tensor_scalar(q_scale[:, 0, :], rs[:, :], SCALE, None, ALU.mult)
                    then(v.tensor_scalar(q_scale[:, 1, :], rs[:, :], -SCALE, None, ALU.mult))

                def rotate(h0, m0, kinds):
                    for k0, m, kind in kinds:
                        q, o, s = qk[:, k0:k0 + m, :], ra[:, k0:k0 + m, :], rb[:, k0 - h0:k0 - h0 + m, :]
                        cos_w, sin_w = (rope[:, 2 * kind + i:2 * kind + i + 1, :] for i in range(2))
                        v.tensor_tensor(o, q, cos_w.to_broadcast([P, m, D]), ALU.mult)
                        v.tensor_tensor(s[:, :, 0:half], q[:, :, half:D], sin_w[:, :, 0:half].to_broadcast([P, m, half]), ALU.mult)
                        last = v.tensor_tensor(s[:, :, half:D], q[:, :, 0:half], sin_w[:, :, half:D].to_broadcast([P, m, half]), ALU.mult)
                    then(last)
                    return v.tensor_tensor(ra[:, h0:h0 + m0, :], ra[:, h0:h0 + m0, :], rb[:, 0:m0, :], ALU.add)

                def low_probs(g, w):
                    dve.wait_ge(s_phi, u * 6 + 3 * g + w + 1)
                    v.tensor_tensor(prT[:, 1, 2 * w:2 * w + 2, :], wide[w][:, :].rearrange("p (j c) -> p j c", j=2),
                                    prT[:, 0, 2 * w:2 * w + 2, :], ALU.subtract).then_inc(t_free[w], 1)

                def low_new(g):
                    dve.wait_ge(s_phi, u * 6 + 3 * g + 3)
                    src, done = (bank[0], c_free[0]) if g else (tail[1], j_free)
                    v.tensor_tensor(prT[:, 1, JT - 1, :], src[:, :], prT[:, 0, JT - 1, :], ALU.subtract).then_inc(done, 1)

                def halves(t):
                    return t.rearrange("p (c k) -> p c k", c=2)

                def low(nth, i, dst, src, high_part):
                    dve.wait_ge(s_high, n * 5 + nth)
                    v.tensor_tensor(dst, src, high_part, ALU.subtract).then_inc(c_free[i], 1)

                def mask_max(h, between):
                    dve.wait_ge(s_sfull, n * HP + h + 1 + HP)
                    v.memset(tick[:, 0:1], 0.0)
                    scores = wide[h % 2][:, :].rearrange("p (c k) -> p c k", c=2)[:, :, 0:NK // 2]
                    v.tensor_tensor_reduce(halves(pr[:, h, :]), scores, halves(bias[:, :]), 1.0, -3.0e38, ALU.add, ALU.max,
                                           mx[:, h:h + 1]).then_inc(s_sfree, 1)
                    between()
                    dve.wait_ge(s_sfree, n * HP + h + 1 + FIRST)
                    v.tensor_scalar(nm[:, h:h + 1], mx[:, h:h + 1], q_scale[:, 1, head(h)], None, ALU.mult).then_inc(s_nm, 1)

                def mask_keys():
                    dve.wait_ge(s_keyno, n + 3)
                    then(v.tensor_scalar(bias[:, 0:L], bias[:, 0:L], seq_f[:, bass.ds(b, 1)], NEG, ALU.is_ge, ALU.mult))

                def reciprocal(h):
                    dve.wait_ge(s_exp, n * HP + h + 1)
                    last = v.reciprocal(rden[:, h:h + 1], den[:, h:h + 1])
                    if h < SOON:
                        at.inc(last)
                    else:
                        last.then_inc(s_rden, 1)

                def normalise(h):
                    dve.wait_ge(s_step, n * NSTEP + (NSTEP - SOON + h + 1))
                    v.tensor_scalar(pr[:, h, :], pr[:, h, :], rden[:, h:h + 1], None, ALU.mult).then_inc(s_p[0], 1)

                def low_values(g):
                    dve.wait_ge(s_ohi, u * G + g + 1)
                    v.tensor_tensor(oT[:, 1, g, :], tail[g][:, :], oT[:, 0, g, :], ALU.subtract).then_inc(s_o, 1)

                if front:
                    arrive()
                    v.tensor_copy(qk[:, 0:REP, :], bank[1][:, :].rearrange("p (h d) -> p h d", d=D)).then_inc(s_q0, 1)
                if back:
                    low_probs(0, 0)
                    low_probs(0, 1)
                    low_new(0)
                if front:
                    dve.wait_ge(s_ropel, n * 16 + 16)
                    dve.wait_ge(s_kc, n + 1)
                    dve.wait_ge(s_q0, n + 1)
                    then(rotate(0, REP + G, ((0, REP, 0), (REP, G, 1))))
                if back:
                    low_probs(1, 0)
                if front:
                    root_begin()
                if back:
                    low_probs(1, 1)
                    low_new(1)
                    low_values(0)
                if front:
                    root_end()
                    keys = ra[:, REP:REP + G, :]
                    v.tensor_tensor(keys, keys, rs[:, REP:REP + G].rearrange("p (h o) -> p h o", o=1).to_broadcast([P, G, D]), ALU.mult).then_inc(s_rope, 1)
                if back:
                    low_values(1)
                if front:
                    low(1, 1, kT_low[:, 0, 0:L], bank[1][:, :], kT[:, 0, 0:L])
                    low(2, 0, kT_low[:, 1, 0:L], bank[0][:, :], kT[:, 1, 0:L])
                    rotate(REP + G, REP, ((REP + G, REP, 0),)).then_inc(s_rope, 1)
                    low(3, 1, qT_low[:, 0, :], bank[1][:, :], qT[:, 0, :])
                    low(4, 0, kT_low[:, :, L:NK], bank[0][:, 0:G * S].rearrange("p (g c) -> p g c", g=G), kT[:, :, L:NK])
                    mask_keys()
                    low(5, 1, qT_low[:, 1, :], bank[1][:, :], qT[:, 1, :])
                if extra == "next":
                    dve.wait_ge(s_v, (pair + 1) * (B * 16 * LT))
                    v.tensor_scalar(row_kv[:, :], row_kv[:, :], 1.0, None, ALU.add).then_inc(s_rowskv, 1)
                if front:
                    dve.wait_ge(s_p[1], n * LATE + FIRST)
                    for h in range(HP):
                        mask_max(h, lambda: reciprocal(h - 2) if h >= 2 else None)
                        if 2 <= h < REP + 2 and extra != "next":
                            normalise(h - 2)
                        for i, (_, dst) in chunks(extra, h):
                            if extra == "next":
                                low_weights(s_whi, pair * NWJ + (NWJ + i + 1), i % 2, dst)
                            else:
                                low_weights(s_wohi, pair * HP + (i + 1), i % 2, dst)
                    if extra != "next":
                        for h in range(REP, SOON):
                            normalise(h)
                    reciprocal(HP - 2)
                    reciprocal(HP - 1)
                    assert at.n == NSTEP, at.n
            for i, (_, dst) in enumerate(weight_jobs()):
                low_weights(s_whi, i + 1, i % len(w_place), dst)
            turns(dve, turn)


_NAMES = ["x", "itok_B_2_6", "itok_B_1_7", "itok_B_0_23", "itok_Bx16_0_63", "itok_B_207_1644",
          "L0_cond_W_gate", "L0_cond_W_up", "L0_cond_W_down", "L0_cond_A_gate", "L0_cond_B_gate", "L0_cond_A_up",
          "L0_cond_B_up", "L0_cond_A_down", "L0_cond_B_down", "L1_cond_weight", "L1_cond_bias", "L1_cond_lora_a_weights",
          "L1_cond_lora_b_weights", "L1_cond_scaling_factors", "L2_cond_W", "L2_cond_b", "L2_cond_lora_As",
          "L2_cond_lora_Bs", "L3_cond_Wq", "L3_cond_Wk", "L3_cond_Wv", "L3_cond_Wo", "L3_cond_q_norm_w",
          "L3_cond_k_norm_w", "L3_cond_k_cache", "L3_cond_v_cache"]


def kernel(**inputs):
    import concourse.bacc as bacc
    from concourse.bass_utils import run_bass_kernel_spmd

    nc = bacc.Bacc("TRN2", target_bir_lowering=False, num_devices=1)
    arrays = {n: np.ascontiguousarray(inputs[n]) for n in _NAMES}
    arrays["inv_freq"] = (np.float32(1.0) / np.power(np.float32(THETA), np.arange(0, D, 2, dtype=np.float32) / np.float32(D))).astype(np.float32)
    args = {n: nc.dram_tensor(n, v.shape, mybir.dt.from_np(v.dtype), kind="ExternalInput").ap() for n, v in arrays.items()}
    args["out"] = nc.dram_tensor("out", [B, S, H], F32, kind="ExternalOutput").ap()
    build_program(nc, args)
    r = run_bass_kernel_spmd(nc, [arrays], core_ids=[0])
    return r.results[0]["out"]
```
